# Optimizing a Trainium2 kernel written in Bass

```python
import numpy as np
import jax
import jax.numpy as jnp

def _softmax(x, axis=-1):
    return jax.nn.softmax(x, axis=axis)

def _gelu(x):
    return jax.nn.gelu(x, approximate=True)

def _silu(x):
    return jax.nn.silu(x)

def _sigmoid(x):
    return jax.nn.sigmoid(x)

def _layernorm(x, axis=-1, eps=1e-05):
    m = jnp.mean(x, axis=axis, keepdims=True)
    v = jnp.var(x, axis=axis, keepdims=True)
    return (x - m) / jnp.sqrt(v + eps)

def _scatter_add(tgt, idx, src, axis=0):
    return tgt.at[idx].add(src)

def _segment_sum(src, seg, n):
    return jax.ops.segment_sum(src, seg, n)
kernel_name = 'mk_flamingo_gated_d4_seqx_r8_df105b'

def setup_inputs(seed: int=0):
    np.random.seed(seed)
    _w = jnp.asarray

    def _rec_inputs():
        import jax
        import jax.numpy as jnp
        _rk = jax.random.key(seed)
        x = 7.22e-05 + 1 * jax.random.normal(jax.random.fold_in(_rk, 1), (2, 512, 128), jnp.float32)
        _lenS = 512 - jax.random.randint(jax.random.fold_in(_rk, 7), (2,), 0, max(1, 512 // 4) + 1, jnp.int32)
        _lenS2 = 77 - jax.random.randint(jax.random.fold_in(_rk, 8), (2,), 0, max(1, 77 // 4) + 1, jnp.int32)
        _ctx_1024P = jax.random.normal(jax.random.fold_in(_rk, 11), (2, 16, 128), jnp.float32)
        _ctx_1024c = jax.random.dirichlet(jax.random.fold_in(_rk, 511), 0.3 * jnp.ones((16,), jnp.float32), (2, 77))
        _ctx_1024t = jnp.einsum('bsk,bkd->bsd', _ctx_1024c, _ctx_1024P)
        _ctx_1024t = _ctx_1024t * jax.lax.rsqrt(jnp.mean(jnp.square(_ctx_1024t)) + 1e-12) * 0.953939
        ctx_1024 = -0.000514642 + 1.00011 * (_ctx_1024t + 0.3 * jax.random.normal(jax.random.fold_in(_rk, 611), (2, 77, 128), jnp.float32))
        _validS = jnp.arange(512)[None, :] < _lenS[:, None]
        _validS2 = jnp.arange(77)[None, :] < _lenS2[:, None]
        _causal = jnp.tril(jnp.ones((512, 512), dtype=bool))
        mask_Bx1xSxS2_ik1 = jnp.where(jnp.broadcast_to(_validS2[:, None, None, :], (2, 1, 512, 77)), 1, 0).astype(jnp.int32)
        _g = jax.random.normal(jax.random.fold_in(_rk, 9001), (2, 4), jnp.float32)
        _g = jnp.sign(_g) * jnp.maximum(jnp.abs(_g), 1.0) + (_g == 0) * 1.0
        g_xattn = _g[0]
        g_ffn = _g[1]
        return (x, ctx_1024, mask_Bx1xSxS2_ik1, g_xattn, g_ffn)
    x, ctx_1024, mask_Bx1xSxS2_ik1, g_xattn, g_ffn = _rec_inputs()

    def _L0_xattn_setup():
        import jax, jax.numpy as jnp
        import numpy as np
        B, L_ENC, L_DEC, D = (16, 64, 128, 128)
        key = jax.random.key(seed)
        k1, k2, k3, k4, k5, k6 = jax.random.split(key, 6)
        encoder_hc = jax.random.normal(k1, (B, L_ENC, D), dtype=jnp.float32)
        decoder_hq = jax.random.normal(k2, (B, L_DEC, D), dtype=jnp.float32)
        w_sim = jax.random.normal(k3, (3 * D,), dtype=jnp.float32) * 0.02
        b_sim = jax.random.normal(k4, (1,), dtype=jnp.float32) * 0.02
        W_qv = jax.random.normal(k5, (4 * D, D), dtype=jnp.float32) * 0.02
        b_qv = jax.random.normal(k6, (D,), dtype=jnp.float32) * 0.02
        return {'encoder_hc': encoder_hc, 'decoder_hq': decoder_hq, 'w_sim': w_sim, 'b_sim': b_sim, 'W_qv': W_qv, 'b_qv': b_qv}
    _L0_xattn_all = _L0_xattn_setup()
    _L0_xattn_in = {k: v for k, v in _L0_xattn_all.items() if k in ('w_sim', 'b_sim', 'W_qv', 'b_qv')}
    del _L0_xattn_all

    def _L0_ffn_setup():
        import jax, jax.numpy as jnp
        import numpy as np
        DIM = 128

        def _reference_tuple_inner(x, W_r, W_k, W_v, mu_r, mu_k):
            B, T, C = x.shape
            x_prev = jnp.concatenate([jnp.zeros((B, 1, C), x.dtype), x[:, :-1, :]], axis=1)
            xr = mu_r * x + (1.0 - mu_r) * x_prev
            xk = mu_k * x + (1.0 - mu_k) * x_prev
            r = jax.nn.sigmoid(jnp.einsum('btc,dc->btd', xr, W_r))
            k = jnp.einsum('btc,dc->btd', xk, W_k)
            k_act = jnp.square(jax.nn.relu(k))
            out = r * jnp.einsum('btc,dc->btd', k_act, W_v)
            new_state = x[:, -1, :]
            return (out, new_state)
        key = jax.random.key(seed)
        ks = jax.random.split(key, 6)
        B, T, C = (8, 256, DIM)
        x = jax.random.normal(ks[0], (B, T, C), dtype=jnp.float32)
        s = 1.0 / np.sqrt(C)
        W_r = jax.random.uniform(ks[1], (C, C), jnp.float32, -s, s)
        W_k = jax.random.uniform(ks[2], (C, C), jnp.float32, -s, s)
        W_v = jax.random.uniform(ks[3], (C, C), jnp.float32, -s, s)
        mu_r = jax.random.uniform(ks[4], (C,), jnp.float32)
        mu_k = jax.random.uniform(ks[5], (C,), jnp.float32)
        return {'x': x, 'W_r': W_r, 'W_k': W_k, 'W_v': W_v, 'mu_r': mu_r, 'mu_k': mu_k}
    _L0_ffn_all = _L0_ffn_setup()
    _L0_ffn_in = {k: v for k, v in _L0_ffn_all.items() if k in ('W_r', 'W_k', 'W_v', 'mu_r', 'mu_k')}
    del _L0_ffn_all

    def _L1_xattn_setup():
        import jax, jax.numpy as jnp
        import numpy as np
        H = 128
        B = 8
        L_CHAR = 256
        L_SUB = 128

        def _linear(x, W, b):
            return jnp.einsum('blh,oh->blo', x, W) + b

        def _interp_linear(x, out_len):
            L_in = x.shape[1]
            pos = (jnp.arange(out_len, dtype=x.dtype) + 0.5) * (L_in / out_len) - 0.5
            pos = jnp.clip(pos, 0.0, L_in - 1)
            lo = jnp.floor(pos).astype(jnp.int32)
            hi = jnp.minimum(lo + 1, L_in - 1)
            w = (pos - lo.astype(x.dtype))[None, :, None]
            return x[:, lo] * (1 - w) + x[:, hi] * w
        key = jax.random.key(seed)
        ks = jax.random.split(key, 18)
        s = 0.02
        inp = {'char_emb': jax.random.normal(ks[0], (B, L_CHAR, H), jnp.float32), 'subword_emb': jax.random.normal(ks[1], (B, L_SUB, H), jnp.float32)}
        names = ['Wq_c', 'Wk_s', 'Wv_s', 'Wq_s', 'Wk_c', 'Wv_c']
        for i, n in enumerate(names):
            inp[n] = jax.random.normal(ks[2 + 2 * i], (H, H), jnp.float32) * s
            inp['b' + n[1:]] = jax.random.normal(ks[3 + 2 * i], (H,), jnp.float32) * s
        inp['Wg'] = jax.random.normal(ks[14], (H, 2 * H), jnp.float32) * s
        inp['bg'] = jax.random.normal(ks[15], (H,), jnp.float32) * s
        return inp
    _L1_xattn_all = _L1_xattn_setup()
    _L1_xattn_in = {k: v for k, v in _L1_xattn_all.items() if k in ('Wq_c', 'bq_c', 'Wk_s', 'bk_s', 'Wv_s', 'bv_s', 'Wq_s', 'bq_s', 'Wk_c', 'bk_c', 'Wv_c', 'bv_c', 'Wg', 'bg')}
    del _L1_xattn_all

    def _L1_ffn_setup():
        import jax, jax.numpy as jnp
        import numpy as np
        TOP_K = 2
        key = jax.random.key(seed)
        ks = jax.random.split(key, 6)
        B, T, H, E, F = (2, 256, 128, 8, 512)
        s = 0.02
        return {'hidden_states': jax.random.normal(ks[0], (B, T, H), dtype=jnp.float32), 'router_w': jax.random.normal(ks[1], (E, H), dtype=jnp.float32) * s, 'w1': jax.random.normal(ks[2], (E, F, H), dtype=jnp.float32) * s, 'b1': jax.random.normal(ks[3], (E, F), dtype=jnp.float32) * s, 'w2': jax.random.normal(ks[4], (E, H, F), dtype=jnp.float32) * s, 'b2': jax.random.normal(ks[5], (E, H), dtype=jnp.float32) * s}
    _L1_ffn_all = _L1_ffn_setup()
    _L1_ffn_in = {k: v for k, v in _L1_ffn_all.items() if k in ('router_w', 'w1', 'b1', 'w2', 'b2')}
    del _L1_ffn_all

    def _L2_xattn_setup():
        import jax, jax.numpy as jnp
        import numpy as np
        D_MODEL = 128
        H = 16
        D_K = D_MODEL // H

        def _split_heads(x):
            B, S, _ = x.shape
            return x.reshape(B, S, H, D_K).transpose(0, 2, 1, 3)
        key = jax.random.key(seed)
        ks = jax.random.split(key, 8)
        B, S = (2, 256)
        q = jax.random.normal(ks[0], (B, S, D_MODEL), dtype=jnp.float32)
        k = jax.random.normal(ks[1], (B, S, D_MODEL), dtype=jnp.float32)
        v = jax.random.normal(ks[2], (B, S, D_MODEL), dtype=jnp.float32)
        mask = jax.random.randint(ks[3], (B, 1, S, S), 0, 2, dtype=jnp.int32)
        scale = 1.0 / np.sqrt(D_MODEL)
        w_q = jax.random.normal(ks[4], (D_MODEL, D_MODEL), dtype=jnp.float32) * scale
        w_k = jax.random.normal(ks[5], (D_MODEL, D_MODEL), dtype=jnp.float32) * scale
        w_v = jax.random.normal(ks[6], (D_MODEL, D_MODEL), dtype=jnp.float32) * scale
        w_o = jax.random.normal(ks[7], (D_MODEL, D_MODEL), dtype=jnp.float32) * scale
        return {'q': q, 'k': k, 'v': v, 'mask': mask, 'w_q': w_q, 'w_k': w_k, 'w_v': w_v, 'w_o': w_o}
    _L2_xattn_all = _L2_xattn_setup()
    _L2_xattn_in = {k: v for k, v in _L2_xattn_all.items() if k in ('w_q', 'w_k', 'w_v', 'w_o')}
    del _L2_xattn_all

    def _L2_ffn_setup():
        import jax, jax.numpy as jnp
        import numpy as np
        N_EXPERTS = 8
        N_GROUP = 4
        TOPK_GROUP = 2
        TOP_K = 2
        HIDDEN = 128
        INTER = 256
        B, S = (1, 128)

        def _grouped_topk(scores):
            T, E = scores.shape
            per_group = E // N_GROUP
            group_scores = scores.reshape(T, N_GROUP, per_group).max(-1)
            _, gidx = jax.lax.top_k(group_scores, TOPK_GROUP)
            gmask = jnp.zeros((T, N_GROUP), scores.dtype).at[jnp.arange(T)[:, None], gidx].set(1.0)
            smask = jnp.repeat(gmask, per_group, axis=1)
            masked = jnp.where(smask > 0, scores, 0.0)
            topk_w, topk_ids = jax.lax.top_k(masked, TOP_K)
            topk_w = topk_w / topk_w.sum(-1, keepdims=True)
            return (topk_ids, topk_w)
        key = jax.random.key(seed)
        k1, k2, k3, k4 = jax.random.split(key, 4)
        return {'hidden_states': jax.random.normal(k1, (B, S, HIDDEN), jnp.float32), 'gate_w': jax.random.normal(k2, (N_EXPERTS, HIDDEN), jnp.float32) * 0.02, 'w13_weight': jax.random.normal(k3, (N_EXPERTS, 2 * INTER, HIDDEN), jnp.float32) * 0.02, 'w2_weight': jax.random.normal(k4, (N_EXPERTS, HIDDEN, INTER), jnp.float32) * 0.02}
    _L2_ffn_all = _L2_ffn_setup()
    _L2_ffn_in = {k: v for k, v in _L2_ffn_all.items() if k in ('gate_w', 'w13_weight', 'w2_weight')}
    del _L2_ffn_all

    def _L3_xattn_setup():
        import jax, jax.numpy as jnp
        import numpy as np
        Q_DIM = 128
        K_DIM = 128
        NUM_HEADS = 16
        HEAD_DIM = K_DIM // NUM_HEADS
        SCALE = HEAD_DIM ** (-0.5)
        key = jax.random.key(seed)
        ks = jax.random.split(key, 7)
        B, N_q, N_k = (4, 128, 256)
        q = jax.random.normal(ks[0], (B, N_q, Q_DIM), dtype=jnp.float32)
        k = jax.random.normal(ks[1], (B, N_k, K_DIM), dtype=jnp.float32)
        s = 0.02
        Wq = jax.random.normal(ks[2], (K_DIM, Q_DIM), dtype=jnp.float32) * s
        bq = jnp.zeros((K_DIM,), dtype=jnp.float32)
        Wkv = jax.random.normal(ks[3], (2 * K_DIM, K_DIM), dtype=jnp.float32) * s
        Wo = jax.random.normal(ks[4], (K_DIM, K_DIM), dtype=jnp.float32) * s
        bo = jnp.zeros((K_DIM,), dtype=jnp.float32)
        return {'q': q, 'k': k, 'Wq': Wq, 'bq': bq, 'Wkv': Wkv, 'Wo': Wo, 'bo': bo}
    _L3_xattn_all = _L3_xattn_setup()
    _L3_xattn_in = {k: v for k, v in _L3_xattn_all.items() if k in ('Wq', 'bq', 'Wkv', 'Wo', 'bo')}
    del _L3_xattn_all

    def _L3_ffn_setup():
        import jax, jax.numpy as jnp
        import numpy as np
        D_MODEL = 128
        M = 64
        INNER = 16
        key = jax.random.key(seed)
        ks = jax.random.split(key, 9)

        def init(k, shape, fan_in):
            bound = 1.0 / np.sqrt(fan_in)
            return jax.random.uniform(k, shape, jnp.float32, -bound, bound)
        x = jax.random.normal(ks[0], (16, 512, D_MODEL), dtype=jnp.float32)
        Win = init(ks[1], (D_MODEL, M), D_MODEL)
        bin_ = init(ks[2], (M,), D_MODEL)
        W1 = init(ks[3], (M, INNER), 1)
        b1 = init(ks[4], (M, INNER), 1)
        W2 = init(ks[5], (M, INNER), INNER)
        b2 = init(ks[6], (M,), INNER)
        Wout = init(ks[7], (M, D_MODEL), M)
        bout = init(ks[8], (D_MODEL,), M)
        return {'x': x, 'Win': Win, 'bin_': bin_, 'W1': W1, 'b1': b1, 'W2': W2, 'b2': b2, 'Wout': Wout, 'bout': bout}
    _L3_ffn_all = _L3_ffn_setup()
    _L3_ffn_in = {k: v for k, v in _L3_ffn_all.items() if k in ('Win', 'bin_', 'W1', 'b1', 'W2', 'b2', 'Wout', 'bout')}
    del _L3_ffn_all
    return {'x': x, 'ctx_1024': ctx_1024, 'mask_Bx1xSxS2_ik1': mask_Bx1xSxS2_ik1, 'g_xattn': g_xattn, 'g_ffn': g_ffn, 'L0_xattn_w_sim': _L0_xattn_in['w_sim'], 'L0_xattn_b_sim': _L0_xattn_in['b_sim'], 'L0_xattn_W_qv': _L0_xattn_in['W_qv'], 'L0_xattn_b_qv': _L0_xattn_in['b_qv'], 'L0_ffn_W_r': _L0_ffn_in['W_r'], 'L0_ffn_W_k': _L0_ffn_in['W_k'], 'L0_ffn_W_v': _L0_ffn_in['W_v'], 'L0_ffn_mu_r': _L0_ffn_in['mu_r'], 'L0_ffn_mu_k': _L0_ffn_in['mu_k'], 'L1_xattn_Wq_c': _L1_xattn_in['Wq_c'], 'L1_xattn_bq_c': _L1_xattn_in['bq_c'], 'L1_xattn_Wk_s': _L1_xattn_in['Wk_s'], 'L1_xattn_bk_s': _L1_xattn_in['bk_s'], 'L1_xattn_Wv_s': _L1_xattn_in['Wv_s'], 'L1_xattn_bv_s': _L1_xattn_in['bv_s'], 'L1_xattn_Wq_s': _L1_xattn_in['Wq_s'], 'L1_xattn_bq_s': _L1_xattn_in['bq_s'], 'L1_xattn_Wk_c': _L1_xattn_in['Wk_c'], 'L1_xattn_bk_c': _L1_xattn_in['bk_c'], 'L1_xattn_Wv_c': _L1_xattn_in['Wv_c'], 'L1_xattn_bv_c': _L1_xattn_in['bv_c'], 'L1_xattn_Wg': _L1_xattn_in['Wg'], 'L1_xattn_bg': _L1_xattn_in['bg'], 'L1_ffn_router_w': _L1_ffn_in['router_w'], 'L1_ffn_w1': _L1_ffn_in['w1'], 'L1_ffn_b1': _L1_ffn_in['b1'], 'L1_ffn_w2': _L1_ffn_in['w2'], 'L1_ffn_b2': _L1_ffn_in['b2'], 'L2_xattn_w_q': _L2_xattn_in['w_q'], 'L2_xattn_w_k': _L2_xattn_in['w_k'], 'L2_xattn_w_v': _L2_xattn_in['w_v'], 'L2_xattn_w_o': _L2_xattn_in['w_o'], 'L2_ffn_gate_w': _L2_ffn_in['gate_w'], 'L2_ffn_w13_weight': _L2_ffn_in['w13_weight'], 'L2_ffn_w2_weight': _L2_ffn_in['w2_weight'], 'L3_xattn_Wq': _L3_xattn_in['Wq'], 'L3_xattn_bq': _L3_xattn_in['bq'], 'L3_xattn_Wkv': _L3_xattn_in['Wkv'], 'L3_xattn_Wo': _L3_xattn_in['Wo'], 'L3_xattn_bo': _L3_xattn_in['bo'], 'L3_ffn_Win': _L3_ffn_in['Win'], 'L3_ffn_bin_': _L3_ffn_in['bin_'], 'L3_ffn_W1': _L3_ffn_in['W1'], 'L3_ffn_b1': _L3_ffn_in['b1'], 'L3_ffn_W2': _L3_ffn_in['W2'], 'L3_ffn_b2': _L3_ffn_in['b2'], 'L3_ffn_Wout': _L3_ffn_in['Wout'], 'L3_ffn_bout': _L3_ffn_in['bout']}

def reference(x, ctx_1024, mask_Bx1xSxS2_ik1, g_xattn, g_ffn, L0_xattn_w_sim, L0_xattn_b_sim, L0_xattn_W_qv, L0_xattn_b_qv, L0_ffn_W_r, L0_ffn_W_k, L0_ffn_W_v, L0_ffn_mu_r, L0_ffn_mu_k, L1_xattn_Wq_c, L1_xattn_bq_c, L1_xattn_Wk_s, L1_xattn_bk_s, L1_xattn_Wv_s, L1_xattn_bv_s, L1_xattn_Wq_s, L1_xattn_bq_s, L1_xattn_Wk_c, L1_xattn_bk_c, L1_xattn_Wv_c, L1_xattn_bv_c, L1_xattn_Wg, L1_xattn_bg, L1_ffn_router_w, L1_ffn_w1, L1_ffn_b1, L1_ffn_w2, L1_ffn_b2, L2_xattn_w_q, L2_xattn_w_k, L2_xattn_w_v, L2_xattn_w_o, L2_ffn_gate_w, L2_ffn_w13_weight, L2_ffn_w2_weight, L3_xattn_Wq, L3_xattn_bq, L3_xattn_Wkv, L3_xattn_Wo, L3_xattn_bo, L3_ffn_Win, L3_ffn_bin_, L3_ffn_W1, L3_ffn_b1, L3_ffn_W2, L3_ffn_b2, L3_ffn_Wout, L3_ffn_bout):
    import jax
    import jax.numpy as jnp

    def _L0_xattn_ref(encoder_hc, decoder_hq, w_sim, b_sim, W_qv, b_qv):
        import jax, jax.numpy as jnp
        import numpy as np
        B, L_ENC, L_DEC, D = (16, 64, 128, 128)
        d = encoder_hc.shape[-1]
        w1, w2, w3 = (w_sim[:d], w_sim[d:2 * d], w_sim[2 * d:])
        Sim = (encoder_hc @ w1)[:, :, None] + (decoder_hq @ w2)[:, None, :] + jnp.einsum('bid,bjd->bij', encoder_hc * w3, decoder_hq) + b_sim[0]
        A = jax.nn.softmax(Sim, axis=2)
        hq_hat = jnp.einsum('bij,bjd->bid', A, decoder_hq)
        Batt = jax.nn.softmax(jnp.max(Sim, axis=2), axis=1)
        hc_bar = jnp.einsum('bi,bid->bd', Batt, encoder_hc)[:, None, :]
        hc_hat = jnp.broadcast_to(hc_bar, encoder_hc.shape)
        feats = jnp.concatenate([encoder_hc, hq_hat, encoder_hc * hq_hat, encoder_hc * hc_hat], axis=-1)
        hcq = feats @ W_qv + b_qv
        return hcq

    def _L0_ffn_ref(x, W_r, W_k, W_v, mu_r, mu_k):
        import jax, jax.numpy as jnp
        import numpy as np
        DIM = 128

        def _reference_tuple_inner(x, W_r, W_k, W_v, mu_r, mu_k):
            B, T, C = x.shape
            x_prev = jnp.concatenate([jnp.zeros((B, 1, C), x.dtype), x[:, :-1, :]], axis=1)
            xr = mu_r * x + (1.0 - mu_r) * x_prev
            xk = mu_k * x + (1.0 - mu_k) * x_prev
            r = jax.nn.sigmoid(jnp.einsum('btc,dc->btd', xr, W_r))
            k = jnp.einsum('btc,dc->btd', xk, W_k)
            k_act = jnp.square(jax.nn.relu(k))
            out = r * jnp.einsum('btc,dc->btd', k_act, W_v)
            new_state = x[:, -1, :]
            return (out, new_state)
        return _reference_tuple_inner(x, W_r, W_k, W_v, mu_r, mu_k)[0]

    def _L1_xattn_ref(char_emb, subword_emb, Wq_c, bq_c, Wk_s, bk_s, Wv_s, bv_s, Wq_s, bq_s, Wk_c, bk_c, Wv_c, bv_c, Wg, bg):
        import jax, jax.numpy as jnp
        import numpy as np
        H = 128
        B = 8
        L_CHAR = 256
        L_SUB = 128

        def _linear(x, W, b):
            return jnp.einsum('blh,oh->blo', x, W) + b

        def _interp_linear(x, out_len):
            L_in = x.shape[1]
            pos = (jnp.arange(out_len, dtype=x.dtype) + 0.5) * (L_in / out_len) - 0.5
            pos = jnp.clip(pos, 0.0, L_in - 1)
            lo = jnp.floor(pos).astype(jnp.int32)
            hi = jnp.minimum(lo + 1, L_in - 1)
            w = (pos - lo.astype(x.dtype))[None, :, None]
            return x[:, lo] * (1 - w) + x[:, hi] * w
        h = char_emb.shape[-1]
        scale = 1.0 / jnp.sqrt(jnp.asarray(h, char_emb.dtype))
        Q_char = _linear(char_emb, Wq_c, bq_c)
        K_sub = _linear(subword_emb, Wk_s, bk_s)
        V_sub = _linear(subword_emb, Wv_s, bv_s)
        scores = jnp.einsum('bqh,bkh->bqk', Q_char, K_sub) * scale
        char2sub = jnp.einsum('bqk,bkh->bqh', jax.nn.softmax(scores, axis=-1), V_sub)
        Q_sub = _linear(subword_emb, Wq_s, bq_s)
        K_char = _linear(char_emb, Wk_c, bk_c)
        V_char = _linear(char_emb, Wv_c, bv_c)
        scores2 = jnp.einsum('bqh,bkh->bqk', Q_sub, K_char) * scale
        sub2char = jnp.einsum('bqk,bkh->bqh', jax.nn.softmax(scores2, axis=-1), V_char)
        L_char = char_emb.shape[1]
        if sub2char.shape[1] != L_char:
            sub2char = _interp_linear(sub2char, L_char)
        gate_in = jnp.concatenate([char2sub, sub2char], axis=-1)
        gate = jax.nn.sigmoid(jnp.einsum('blh,oh->blo', gate_in, Wg) + bg)
        return gate * char2sub + (1 - gate) * sub2char

    def _L1_ffn_ref(hidden_states, router_w, w1, b1, w2, b2):
        import jax, jax.numpy as jnp
        import numpy as np
        TOP_K = 2
        x = hidden_states
        router_logits = jnp.einsum('bth,eh->bte', x, router_w)
        topk_values, topk_indices = jax.lax.top_k(router_logits, TOP_K)
        topk_weights = jax.nn.softmax(topk_values.astype(jnp.float32), axis=-1).astype(x.dtype)
        h1 = jnp.einsum('bth,efh->btef', x, w1) + b1
        h1 = jax.nn.gelu(h1, approximate=False)
        expert_outputs = jnp.einsum('btef,ehf->bteh', h1, w2) + b2
        gather_idx = topk_indices[..., None]
        topk_expert_outputs = jnp.take_along_axis(expert_outputs, gather_idx, axis=2)
        mixed_output = jnp.sum(topk_expert_outputs * topk_weights[..., None], axis=2)
        return mixed_output

    def _L2_xattn_ref(q, k, v, mask, w_q, w_k, w_v, w_o):
        import jax, jax.numpy as jnp
        import numpy as np
        D_MODEL = 128
        H = 16
        D_K = D_MODEL // H

        def _split_heads(x):
            B, S, _ = x.shape
            return x.reshape(B, S, H, D_K).transpose(0, 2, 1, 3)
        query = _split_heads(q @ w_q)
        key_ = _split_heads(k @ w_k)
        value = _split_heads(v @ w_v)
        scores = jnp.einsum('bhqd,bhkd->bhqk', query, key_) / jnp.sqrt(jnp.asarray(D_K, dtype=jnp.float32))
        scores = jnp.where(mask == 0, jnp.float32(-1000000000.0), scores)
        attn = jax.nn.softmax(scores, axis=-1)
        x = jnp.einsum('bhqk,bhkd->bhqd', attn, value)
        B, _, S, _ = x.shape
        x = x.transpose(0, 2, 1, 3).reshape(B, S, D_MODEL)
        return x @ w_o

    def _L2_ffn_ref(hidden_states, gate_w, w13_weight, w2_weight):
        import jax, jax.numpy as jnp
        import numpy as np
        N_EXPERTS = 8
        N_GROUP = 4
        TOPK_GROUP = 2
        TOP_K = 2
        HIDDEN = 128
        INTER = 256
        B, S = (1, 128)

        def _grouped_topk(scores):
            T, E = scores.shape
            per_group = E // N_GROUP
            group_scores = scores.reshape(T, N_GROUP, per_group).max(-1)
            _, gidx = jax.lax.top_k(group_scores, TOPK_GROUP)
            gmask = jnp.zeros((T, N_GROUP), scores.dtype).at[jnp.arange(T)[:, None], gidx].set(1.0)
            smask = jnp.repeat(gmask, per_group, axis=1)
            masked = jnp.where(smask > 0, scores, 0.0)
            topk_w, topk_ids = jax.lax.top_k(masked, TOP_K)
            topk_w = topk_w / topk_w.sum(-1, keepdims=True)
            return (topk_ids, topk_w)
        Bm, Sm, H = hidden_states.shape
        x = hidden_states.reshape(-1, H)
        T = x.shape[0]
        scores = jax.nn.softmax(x @ gate_w.T, axis=-1)
        topk_ids, topk_w = _grouped_topk(scores)
        combine = jnp.zeros((T, N_EXPERTS), x.dtype).at[jnp.arange(T)[:, None], topk_ids].add(topk_w)
        gu = jnp.einsum('th,eih->tei', x, w13_weight)
        gate, up = (gu[..., :INTER], gu[..., INTER:])
        act = jax.nn.silu(gate) * up
        act = act * combine[:, :, None]
        out = jnp.einsum('tei,ehi->th', act, w2_weight)
        return out.reshape(Bm, Sm, H)

    def _L3_xattn_ref(q, k, Wq, bq, Wkv, Wo, bo):
        import jax, jax.numpy as jnp
        import numpy as np
        Q_DIM = 128
        K_DIM = 128
        NUM_HEADS = 16
        HEAD_DIM = K_DIM // NUM_HEADS
        SCALE = HEAD_DIM ** (-0.5)
        B, N_k, K = k.shape
        _, N_q, _ = q.shape
        H, Dh = (NUM_HEADS, HEAD_DIM)
        kv = (k @ Wkv.T).reshape(B, N_k, 2, H, Dh)
        kh = kv[:, :, 0].transpose(0, 2, 1, 3)
        vh = kv[:, :, 1].transpose(0, 2, 1, 3)
        qh = (q @ Wq.T + bq).reshape(B, N_q, H, Dh).transpose(0, 2, 1, 3)
        attn = jnp.einsum('bhqd,bhkd->bhqk', qh, kh) * SCALE
        attn = jax.nn.softmax(attn, axis=-1)
        out = jnp.einsum('bhqk,bhkd->bhqd', attn, vh)
        out = out.transpose(0, 2, 1, 3).reshape(B, N_q, K)
        out = out @ Wo.T + bo
        return out

    def _L3_ffn_ref(x, Win, bin_, W1, b1, W2, b2, Wout, bout):
        import jax, jax.numpy as jnp
        import numpy as np
        D_MODEL = 128
        M = 64
        INNER = 16
        s = jnp.einsum('btd,dm->btm', x, Win) + bin_
        h = jax.nn.relu(s[..., None] * W1 + b1)
        g = jnp.einsum('btmh,mh->btm', h, W2) + b2
        out = jnp.einsum('btm,md->btd', g, Wout) + bout
        return out
    x = x + jnp.tanh(g_xattn[0]) * _L0_xattn_ref(_layernorm(x, axis=-1), ctx_1024, L0_xattn_w_sim, L0_xattn_b_sim, L0_xattn_W_qv, L0_xattn_b_qv)
    x = x + jnp.tanh(g_ffn[0]) * _L0_ffn_ref(_layernorm(x, axis=-1), L0_ffn_W_r, L0_ffn_W_k, L0_ffn_W_v, L0_ffn_mu_r, L0_ffn_mu_k)
    x = x + jnp.tanh(g_xattn[1]) * _L1_xattn_ref(_layernorm(x, axis=-1), ctx_1024, L1_xattn_Wq_c, L1_xattn_bq_c, L1_xattn_Wk_s, L1_xattn_bk_s, L1_xattn_Wv_s, L1_xattn_bv_s, L1_xattn_Wq_s, L1_xattn_bq_s, L1_xattn_Wk_c, L1_xattn_bk_c, L1_xattn_Wv_c, L1_xattn_bv_c, L1_xattn_Wg, L1_xattn_bg)
    x = x + jnp.tanh(g_ffn[1]) * _L1_ffn_ref(_layernorm(x, axis=-1), L1_ffn_router_w, L1_ffn_w1, L1_ffn_b1, L1_ffn_w2, L1_ffn_b2)
    x = x + jnp.tanh(g_xattn[2]) * _L2_xattn_ref(_layernorm(x, axis=-1), ctx_1024, ctx_1024, mask_Bx1xSxS2_ik1, L2_xattn_w_q, L2_xattn_w_k, L2_xattn_w_v, L2_xattn_w_o)
    x = x + jnp.tanh(g_ffn[2]) * _L2_ffn_ref(_layernorm(x, axis=-1), L2_ffn_gate_w, L2_ffn_w13_weight, L2_ffn_w2_weight)
    x = x + jnp.tanh(g_xattn[3]) * _L3_xattn_ref(_layernorm(x, axis=-1), ctx_1024, L3_xattn_Wq, L3_xattn_bq, L3_xattn_Wkv, L3_xattn_Wo, L3_xattn_bo)
    x = x + jnp.tanh(g_ffn[3]) * _L3_ffn_ref(_layernorm(x, axis=-1), L3_ffn_Win, L3_ffn_bin_, L3_ffn_W1, L3_ffn_b1, L3_ffn_W2, L3_ffn_b2, L3_ffn_Wout, L3_ffn_bout)
    return x

_drawn_inputs = setup_inputs


def setup_inputs(seed=0):
    import zlib

    import numpy as np

    out = dict(_drawn_inputs(seed))
    spreads = {'L3_xattn_bq': (0.0, 2.0), 'L3_xattn_bo': (0.0, 0.468)}
    factors = {'g_ffn': 8.0,
     'L0_xattn_w_sim': 3.115,
     'L0_xattn_b_qv': 3.462,
     'L0_ffn_W_r': 4.385,
     'L0_ffn_mu_r': 8.0,
     'L1_xattn_Wq_c': 8.0,
     'L1_xattn_bq_c': 8.0,
     'L1_xattn_Wk_s': 8.0,
     'L1_xattn_bk_s': 200.0,
     'L1_xattn_bv_s': 6.031,
     'L1_xattn_Wq_s': 8.0,
     'L1_xattn_bq_s': 8.0,
     'L1_xattn_Wk_c': 8.0,
     'L1_xattn_bk_c': 200.0,
     'L1_xattn_Wv_c': 5.722,
     'L1_xattn_bv_c': 6.28,
     'L1_xattn_Wg': 8.0,
     'L1_xattn_bg': 8.0,
     'L1_ffn_b1': 8.0,
     'L1_ffn_b2': 4.756,
     'L2_ffn_gate_w': 8.0,
     'L2_ffn_w13_weight': 8.0,
     'L2_ffn_w2_weight': 8.0,
     'L3_xattn_Wq': 8.0,
     'L3_xattn_Wkv': 3.406,
     'L3_xattn_Wo': 3.344,
     'L3_ffn_bin_': 45.733,
     'L3_ffn_Win': 3.692,
     'L3_ffn_W1': 3.364,
     'L3_ffn_bout': 3.392,
     'L3_ffn_b2': 2.691}
    for name, (base, spread) in spreads.items():
        noise = np.random.default_rng([zlib.crc32(name.encode()), seed]).standard_normal(out[name].shape)
        drawn = base * np.exp(spread * noise) if base else spread * noise
        out[name] = jnp.asarray(drawn.astype(out[name].dtype))
    for name, factor in factors.items():
        out[name] = (out[name] * factor).astype(out[name].dtype)
    return out
```

```python
from contextlib import ExitStack

import numpy as np

import concourse.bass as bass
from concourse import mybir

F32 = mybir.dt.float32
F32R = mybir.dt.float32r
BF16 = mybir.dt.bfloat16
I32 = mybir.dt.int32
ALU = mybir.AluOpType
ACT = mybir.ActivationFunctionType
AX = mybir.AxisListType.X

B, S, D, K = 2, 512, 128, 77
P = 128
NT = S // P
EPS = 1e-5
E = 8
F1 = 512
C1 = F1 // P
F2 = 256
C2 = F2 // P
H = 16
DH = D // H
GROUPS = 4
SPAN = H * K
CH = -(-SPAN // P)
HB = [(0, 6), (6, 12), (12, 16)]
VW = D + H
MASKED = -1e30
M_IN = 64
NH = 8

COL = {n: i for i, n in enumerate(
    ["w1", "w2", "w3", "mu_r", "mu_k", "bk_s", "bq_s", "bq_c", "bk_c", "bv_s", "bq3", "bin"])}
NC0 = len(COL)
C_W1, C_B1, C_W2, C_B2 = NC0, NC0 + NH, NC0 + 2 * NH, NC0 + 3 * NH
NCOL = NC0 + 3 * NH
ROW = {n: i for i, n in enumerate(["b_qv", "bo3", "bout", "bv_s", "bv_c", "bg"])}
R_G = len(ROW) * D
R_BSIM = R_G + 8
NROW = R_BSIM + 1
MAT0 = ["Wqv1", "Wqv2", "Wqv3", "Wqv4"]
MAT1 = ["WrT", "WkT", "WvT"]
MAT2 = ["WksT", "WqsT", "WvsT", "WvcT", "Wqc", "Wkc", "Wg1T", "Wg2T"]
MAT3 = ["wq2", "wk2", "wv2", "wo2", "WqT3", "WkT3", "WvT3", "WoT3", "WinD", "WoutD"]
MATS = MAT0 + MAT1 + MAT2 + MAT3
K_ID = 0
K_HEAD = K_ID + P
K_LT8 = K_HEAD + H
K_LT4 = K_LT8 + 64
K_REP = K_LT4 + 16
K_PAIR = K_REP + CH * P
K_INT = K_PAIR + CH * H
K_SEL = K_INT + S
NK = K_SEL + 4


def flamingo_program(nc, a, out):
    ctx = ExitStack()
    with ctx:
        def sb(name, shape, dt=F32):
            return ctx.enter_context(nc.sbuf_tensor(name, shape, dt))

        def sem(name):
            return ctx.enter_context(nc.semaphore(name))

        const = sb("const", [P, NK])
        mats = sb("mats", [P, len(MATS), P])
        cols = sb("cols", [P, NCOL])
        b2col = sb("b2col", [P, 1])
        rows = sb("rows", [P, NROW])
        ctxT = sb("ctxT", [P, B * K])
        ctxN = sb("ctxN", [K, B, D])
        mask = sb("mask", [P, B, NT, K], I32)
        rwT = sb("rwT", [P, 2 * E])
        b2E = sb("b2E", [2 * E, D])
        up_raw = [sb(f"up_raw{i}", [P, F1 + C1]) for i in range(2)]
        b1s = [sb(f"b1s{i}", [P, C1]) for i in range(2)]
        down_raw = [sb(f"down_raw{i}", [P, C1, D]) for i in range(2)]

        def mat(n):
            return mats[:, MATS.index(n), :]

        def col(n, p=P):
            return cols[0:p, COL[n]:COL[n] + 1]

        def row(n, p=P):
            return rows[0:p, ROW[n] * D:(ROW[n] + 1) * D]

        ident = const[:, K_ID:K_ID + P]
        head = const[:, K_HEAD:K_HEAD + H]

        def rep(c):
            return const[0:K, K_REP + c * P:K_REP + (c + 1) * P]

        pair = const[:, K_PAIR:K_PAIR + CH * H].rearrange("p (c h) -> p c h", h=H)
        interpT = const[0:K, K_INT:K_INT + S]

        x = [sb(f"x{b}", [P, NT, D]) for b in range(B)]
        h = [sb(f"h{b}", [P, NT, D]) for b in range(B)]
        hTz = [sb(f"hTz{b}", [P, S + 1]) for b in range(B)]
        hT = [t[:, 1:S + 1] for t in hTz]
        hhi = [sb(f"hhi{b}", [P, S], F32R) for b in range(B)]
        hlo = [sb(f"hlo{b}", [P, S], F32R) for b in range(B)]
        stats = [sb(f"stats{b}", [P, NT, 6]) for b in range(B)]
        mv = [sb(f"mv{b}", [P, NT, 2]) for b in range(B)]
        var = [sb(f"var{b}", [P, NT]) for b in range(B)]
        negmean = [sb(f"negmean{b}", [P, NT]) for b in range(B)]
        rstd = [sb(f"rstd{b}", [P, NT]) for b in range(B)]
        shift = [sb(f"shift{b}", [P, NT]) for b in range(B)]
        neghalf = sb("neghalf", [P, NT])
        ones = sb("ones", [P, P])
        ident_b = sb("ident_b", [P, P], BF16)
        tg = sb("tg", [P, 8])
        htg = sb("htg", [P, 8])
        tgb = sb("tgb", [P, 3, D])

        W1_ = [sb(f"wa{b}", [P, S]) for b in range(B)]
        W2_ = [sb(f"wb{b}", [P, S]) for b in range(B)]
        W3_ = [sb(f"wc{b}", [P, S]) for b in range(B)]
        W4_ = [sb(f"wd{b}", [P, S]) for b in range(B)]
        small = [sb(f"small{b}", [P, 64]) for b in range(B)]

        simR = sb("simR", [P, B * K])
        simrow = sb("simrow", [1, B * K])
        ctxW2 = sb("ctxW2", [K, B, D])
        w14 = [sb(f"w14_{b}", [P, D]) for b in range(B)]
        KsT = sb("KsT", [P, B * K])
        QsT = sb("QsT", [P, B * K])
        VsT = sb("VsT", [P, B * K])
        Mq = sb("Mq", [P, B * K])
        Mk = sb("Mk", [P, B * K])
        qrow = sb("qrow", [1, B * K])
        kshift = sb("kshift", [K, B])
        Vs = sb("Vs", [K, B, D])
        VsG = sb("VsG", [K, B, D])
        intV = [sb(f"intV{b}", [K, 2, D]) for b in range(B)]
        AhT = [sb(f"AhT{b}", [P, K]) for b in range(B)]
        s2cT = [sb(f"s2cT{b}", [P, K]) for b in range(B)]

        lg = [sb(f"lg{b}", [P, NT, E]) for b in range(B)]
        ex = [sb(f"ex{b}", [P, NT, E]) for b in range(B)]
        gt = [sb(f"gt{b}", [P, NT, E, E]) for b in range(B)]
        eq = [sb(f"eq{b}", [P, NT, E, E]) for b in range(B)]
        c2 = [sb(f"c2_{b}", [P, NT, 2 * E], F32R) for b in range(B)]
        cT = sb("cT", [2 * E, B * S], F32R)
        cflat = sb("cflat", [4 * B, E // 2, S], F32R)
        sel = sb("sel", [4 * B, 4, P], F32R)
        shared = sb("shared", [P, 2 * CH * P])
        PT = [shared[:, i * CH * P:(i + 1) * CH * P] for i in range(2)]
        ring = [shared[:, i * S:(i + 1) * S] for i in range(4)]
        zero_r = sb("zero_r", [4 * B, P], F32R)
        rhi = [sb(f"rhi{i}", [P, S], F32R) for i in range(4)]
        rlo = [sb(f"rlo{i}", [P, S], F32R) for i in range(4)]
        wuh = [sb(f"wuh{i}", [P, F1], F32R) for i in range(2)]
        wul = [sb(f"wul{i}", [P, F1], F32R) for i in range(2)]
        wdh = [sb(f"wdh{i}", [P, C1, D], F32R) for i in range(2)]
        wdl = [sb(f"wdl{i}", [P, C1, D], F32R) for i in range(2)]

        nb = sb("nb", [P, B, NT, K], BF16)
        kT = sb("kT", [P, B * K])
        kTh = sb("kTh", [P, B * K], F32R)
        kTl = sb("kTl", [P, B * K])
        kbh = [sb(f"kbh{b}", [P, H, K], F32R) for b in range(B)]
        kbl = [sb(f"kbl{b}", [P, H, K], F32R) for b in range(B)]
        vN = sb("vN", [K, B, D])
        vbd = [sb(f"vbd{b}", [P, CH, VW]) for b in range(B)]
        Sx = [sb(f"Sx{i}", [P, CH * P]) for i in range(2)]
        qh, ql = hhi, hlo

        bank = [ctx.enter_context(nc.psum_tensor(f"bank{i}", [P, 512], F32)) for i in range(8)]

        ld = {n: sem(f"ld_{n}") for n in
              ["x0", "x1", "first", "ctx", "l0", "l1", "l2", "l3", "mask", "const", "moe1", "pair", "b2m"]}
        raw_in = [sem(f"raw_in{i}") for i in range(2)]
        out_done = sem("out_done")
        dve_step, act_step, pool_step = sem("dve_step"), sem("act_step"), sem("pool_step")
        ready_const = sem("ready_const")
        ln_var, ln_h, ln_T, hT_ready = sem("ln_var"), sem("ln_h"), sem("ln_T"), sem("hT_ready")
        x_biased, resid = sem("x_biased"), sem("resid")
        gates = sem("gates")
        tgb_ready = sem("tgb_ready")
        p0_dve, p0_pe, p0_act = sem("p0_dve"), sem("p0_pe"), sem("p0_act")
        p2_pe, p2_act, p2_dve = sem("p2_pe"), sem("p2_act"), sem("p2_dve")
        l0 = {n: sem(f"l0_{n}") for n in
              ["S", "m", "sub", "exp", "P", "PT", "PTs", "hq", "u", "m1", "nM", "e", "hc", "W", "out"]}
        l1 = {n: sem(f"l1_{n}") for n in ["x", "k", "r", "kr", "rt", "ka", "v"]}
        l2 = {n: sem(f"l2_{n}") for n in
              ["S", "s2", "sub", "exp", "shift2", "exp2", "P", "PT", "PTs", "P2T", "P2Ts", "ah", "ahs", "s2c",
               "s2cs", "s2cT", "s2cTs", "s2g", "s2gs", "c2s", "s2ci", "z", "t", "sc"]}
        m = {n: sem(f"m_{n}") for n in
             ["split", "lg", "sub", "exp", "c", "cT", "cTs", "flat", "outTs", "outN"]}
        q = {n: sem(f"q_{n}") for n in
             ["h", "gelu", "scale", "hi", "loD", "loP", "free", "wh", "wl"]}
        r = {n: sem(f"r_{n}") for n in
             ["g", "silu", "mul", "scale", "hi", "loD", "loP", "free", "wh", "wl"]}
        kv = {n: sem(f"kv_{n}") for n in ["pe", "act", "pool", "rep", "bd", "hi"]}
        at = {n: sem(f"at_{n}") for n in
              ["q", "qhi", "qlo", "S", "sub", "exp", "T", "PT", "O", "norm", "OT", "OTs", "out"]}
        l3 = {n: sem(f"l3_{n}") for n in ["s", "ss", "u", "acc", "out"]}
        nb_ready = sem("nb_ready")

        block = ctx.enter_context(nc.Block())

        def tile(ap, t):
            return ap[:, t * P:(t + 1) * P]

        def over_tiles(ap):
            return ap.unsqueeze(1).broadcast_to([P, NT, D])

        def wait_positive(eng, semaphore, value):
            if not isinstance(value, int) or value > 0:
                eng.wait_ge(semaphore, value)

        def lo_on_pool(n):
            return n % 8 not in (3, 7)

        def pool_los(n):
            return sum(lo_on_pool(j) for j in range(n))

        def dve_los(n):
            return n - pool_los(n)

        def unit_on_pool(n):
            return n % 4 != 3

        def pool_units(n):
            return sum(unit_on_pool(j) for j in range(n))

        CH1 = [(p, b, c) for p in range(2) for b in range(B) for c in range(C1)]
        CH2 = [(p, b, c) for p in range(2) for b in range(B) for c in range(C2)]
        N1, N2 = len(CH1), len(CH2)
        LAG1, LAG2 = 3, 2
        PASSES = E // 2
        POOL1, POOL2 = pool_los(N1), pool_units(N2)
        BANKS1 = [1, 2, 3, 7]
        BANKG, BANKU = [1, 2], [3, 7]
        BANKC = [5, 6]

        @block.sync
        def _(sp):
            for b in range(B):
                sp.dma_start(x[b][:, :, :], a["x"][b].rearrange("(t p) d -> p t d", p=P)).then_inc(ld[f"x{b}"], 16)
            sp.dma_start(rows[:, :], a["rows"].partition_broadcast(P)).then_inc(ld["first"], 16)
            sp.dma_start(mats[:, 0:4, :], a["mats"][:, 0:4, :]).then_inc(ld["l0"], 16)
            sp.dma_start(mats[:, 7:15, :], a["mats"][:, 7:15, :]).then_inc(ld["l2"], 16)
            sp.dma_start(mats[:, 4:7, :], a["mats"][:, 4:7, :]).then_inc(ld["l1"], 16)
            sp.dma_start(rwT[:, :], a["rwT"]).then_inc(ld["moe1"], 16)
            for p in range(2):
                for j in range(2):
                    r0 = (2 * p + j) * (E // 2)
                    sp.dma_start(b2E[r0:r0 + E // 2, :],
                                 a["b2"].rearrange("(i p) d -> p i d", p=2)[p]).then_inc(ld["moe1"], 16)
            def load_expert(up, down, nd, e, p):
                sp.dma_start(up_raw[p][:, 0:a[up].shape[2]], a[up][:, e, :]).then_inc(raw_in[p], 16)
                sp.dma_start(down_raw[p][:, 0:nd, :], a[down][:, e, :, :]).then_inc(raw_in[p], 16)

            for p in range(2):
                load_expert("w1", "w2", C1, p, p)
            sp.dma_start(mats[:, 15:, :], a["mats"][:, 15:, :]).then_inc(ld["l3"], 16)
            sp.wait_ge(ready_const, 1)
            sp.dma_start(b2col[0:M_IN, :], a["b2m"]).then_inc(ld["b2m"], 16)

            def flatten(n):
                for b in range(B):
                    sp.wait_ge(m["cTs"], B * n + b + 1)
                    sp.dma_start(cflat[4 * b:4 * b + 4, :, :].bitcast(F32), cT[:, b * S:(b + 1) * S].bitcast(F32)).then_inc(m["flat"], 16)

            flatten(0)
            with sp.Fori(0, PASSES - 1) as i:
                for p in range(2):
                    sp.wait_ge(q["wl"], 2 * i + p + 1)
                    load_expert("w1", "w2", C1, 2 * i + 2 + p, p)
            for p in range(2):
                sp.wait_ge(q["wl"], E - 1 + p)
                load_expert("v13", "v2", C2, p, p)
            flatten(1)
            with sp.Fori(0, PASSES - 1) as i:
                for p in range(2):
                    sp.wait_ge(r["wl"], 2 * i + p + 1)
                    load_expert("v13", "v2", C2, 2 * i + 2 + p, p)
            for b in range(B):
                sp.wait_ge(resid, 2 * 7 + b + 1)
                sp.dma_start(out[b].rearrange("(t p) d -> p t d", p=P), x[b][:, :, :]).then_inc(out_done, 16)
            sp.wait_ge(out_done, 16 * B)

        @block.gpsimd
        def _(pool):
            pool.dma_start(const[:, :], a["const"]).then_inc(ld["const"], 16)
            pool.dma_start(mask[:, :, :, :], a["mask"].rearrange("b (t p) k -> p b t k", p=P)).then_inc(ld["mask"], 16)
            nc.gpsimd.memset(neghalf[:, :], -0.5)
            nc.gpsimd.memset(ones[:, :], 1.0)
            for b in range(B):
                nc.gpsimd.memset(hTz[b][:, 0:1], 0.0)
            for i in range(2):
                nc.gpsimd.memset(Sx[i][:, SPAN:], 0.0)
            nc.gpsimd.memset(b2col[:, :], 0.0).then_inc(ready_const, 1)
            pool.wait_ge(ready_const, 1)
            steps = [0]

            def link(ins):
                steps[0] += 1
                ins.then_inc(pool_step, 1)
                pool.wait_ge(pool_step, steps[0])

            def norm(k):
                b = k % B
                pool.wait_ge(ln_var, k + 1)
                link(nc.gpsimd.tensor_tensor(rstd[b][:, :], var[b][:, :], neghalf[:, :], ALU.pow))
                link(nc.gpsimd.tensor_tensor(shift[b][:, :], negmean[b][:, :], rstd[b][:, :], ALU.mult))
                for t in range(NT):
                    last = nc.gpsimd.tensor_scalar(h[b][:, t, :], x[b][:, t, :], rstd[b][:, t:t + 1],
                                                   shift[b][:, t:t + 1], ALU.mult, ALU.add)
                last.then_inc(ln_h, 1)

            def add_bias(n, b):
                pool.wait_ge(ln_h, 2 * [0, 6, 7][n] + b + 1)
                pool.wait_ge(tgb_ready, 1)
                nc.gpsimd.tensor_tensor(x[b][:, :, :], x[b][:, :, :], over_tiles(tgb[:, n, :]),
                                        ALU.add).then_inc(x_biased, 1)

            def keys(n):
                pool.wait_ge(kv["hi"], n + 1)
                pool.wait_ge(ld["const"], 16)
                if n == 1:
                    pool.wait_ge(at["S"], 3 * NT * B)
                for b in range(B):
                    for dst, src in ((kbh, kTh[:, b * K:(b + 1) * K].bitcast(F32)), (kbl, kTl[:, b * K:(b + 1) * K])):
                        last = nc.gpsimd.tensor_tensor(dst[b][:, :, :],
                                                       src.unsqueeze(1).broadcast_to([P, H, K]),
                                                       head.unsqueeze(2).broadcast_to([P, H, K]), ALU.mult)
                last.then_inc(kv["pool"], 1)

            for k in range(2):
                norm(k)
            for k in range(2):
                b = k
                add_bias(0, b)
                pool.wait_ge(l0["m1"], b + 1)
                link(nc.gpsimd.partition_all_reduce(small[b][:, 5:6], small[b][:, 4:5], P, bass.bass_isa.ReduceOp.max))
                nc.gpsimd.tensor_scalar(small[b][:, 6:7], small[b][:, 5:6], -1.0, 0.0, ALU.mult,
                                        ALU.add).then_inc(l0["nM"], 1)
            for k in range(2, 8):
                norm(k)
            keys(0)

            def split1(i, p):
                e = 2 * i + p
                pool.wait_ge(q["wh"], e + 1)
                nc.gpsimd.tensor_tensor(wul[p][:, :], up_raw[p][:, 0:F1], wuh[p][:, :].bitcast(F32), ALU.subtract)
                nc.gpsimd.tensor_tensor(wdl[p][:, :, :], down_raw[p][:, :, :], wdh[p][:, :, :].bitcast(F32),
                                        ALU.subtract).then_inc(q["wl"], 1)

            def body1(i, last):
                for n, (p, b, c) in enumerate(CH1):
                    g = N1 * i + n
                    if n == 1:
                        split1(i, 1)
                    if n == N1 // 2 + 1 and not last:
                        split1(i + 1, 0)
                    if lo_on_pool(n):
                        pool.wait_ge(q["hi"], g + 1)
                        nc.gpsimd.tensor_tensor(rlo[n % 4][:, :], ring[n % 4][:, :], rhi[n % 4][:, :].bitcast(F32),
                                                ALU.subtract).then_inc(q["loP"], 1)

            split1(0, 0)
            body1(0, False)
            with pool.Fori(1, PASSES - 1) as i:
                body1(i, False)
            body1(PASSES - 1, True)

            for k in range(8, 10):
                norm(k)
            for k in range(10, 12):
                norm(k)

            def split2(i, p):
                e = 2 * i + p
                pool.wait_ge(r["wh"], e + 1)
                nc.gpsimd.tensor_tensor(wul[p][:, :], up_raw[p][:, 0:F1], wuh[p][:, :].bitcast(F32), ALU.subtract)
                nc.gpsimd.tensor_tensor(wdl[p][:, 0:C2, :], down_raw[p][:, 0:C2, :],
                                        wdh[p][:, 0:C2, :].bitcast(F32), ALU.subtract).then_inc(r["wl"], 1)

            def body2(i, last):
                for n, (p, b, c) in enumerate(CH2):
                    g = N2 * i + n
                    if n == 1:
                        split2(i, 1)
                    if n == N2 // 2 + 1 and not last:
                        split2(i + 1, 0)
                    if unit_on_pool(n):
                        pool.wait_ge(r["hi"], g + 1)
                        nc.gpsimd.tensor_tensor(rlo[n % 4][:, :], ring[n % 4][:, :], rhi[n % 4][:, :].bitcast(F32),
                                                ALU.subtract).then_inc(r["loP"], 1)

            split2(0, 0)
            keys(1)
            body2(0, False)
            with pool.Fori(1, PASSES - 1) as i:
                body2(i, False)
            body2(PASSES - 1, True)
            for k in range(12, 14):
                norm(k)
                add_bias(1, k % B)
            for k in range(14, 16):
                norm(k)
                add_bias(2, k % B)

        @block.scalar
        def _(act):
            act.dma_start(cols[:, :], a["cols"]).then_inc(ld["ctx"], 16)
            act.dma_start(ctxT[:, :], a["ctxT"]).then_inc(ld["ctx"], 16)
            act.dma_start(ctxN[:, :, :], a["ctx"].rearrange("b k d -> k b d")).then_inc(ld["ctx"], 16)
            for b in range(B):
                act.dma_start(vbd[b][:, :, D:VW], a["pair"]).then_inc(ld["pair"], 16)
            steps = [0]

            def link(ins):
                steps[0] += 1
                ins.then_inc(act_step, 1)
                act.wait_ge(act_step, steps[0])

            def transposed(k):
                b = k % B
                act.wait_ge(ln_T, k + 1)
                nc.scalar.activation(hT[b], bank[4 * b][:, :], ACT.Copy).then_inc(hT_ready, 1)

            act.wait_ge(ld["first"], 16)
            nc.scalar.activation(tg[:, :], rows[:, R_G:R_G + 8], ACT.Tanh).then_inc(gates, 1)
            act.wait_ge(p0_pe, 1)
            nc.scalar.activation(simrow[:, :], bank[1][0:1, 0:B * K], ACT.Identity,
                                 bias=rows[0:1, R_BSIM:R_BSIM + 1])
            nc.scalar.activation(ctxW2[:, :, :], bank[2][0:K, 0:B * D], ACT.Copy).then_inc(p0_act, 1)
            act.wait_ge(p2_pe, 1)
            nc.scalar.activation(KsT[:, :], bank[3][:, 0:B * K], ACT.Identity, bias=col("bk_s"))
            nc.scalar.activation(QsT[:, :], bank[3][:, B * K:2 * B * K], ACT.Identity, bias=col("bq_s"))
            nc.scalar.activation(VsT[:, :], bank[6][:, 0:B * K], ACT.Identity, bias=col("bv_s")).then_inc(p2_act, 1)
            act.wait_ge(p2_pe, 2)
            sc = float(D) ** -0.5
            nc.scalar.activation(Mq[:, :], bank[7][:, 0:B * K], ACT.Copy, scale=sc)
            nc.scalar.activation(Mk[:, :], bank[7][:, B * K:2 * B * K], ACT.Copy, scale=sc)
            nc.scalar.activation(qrow[:, :], bank[1][0:1, B * K:2 * B * K], ACT.Copy, scale=sc)
            nc.scalar.activation(kshift[:, :], bank[2][0:K, 256:256 + B], ACT.Copy, scale=sc).then_inc(p2_act, 1)

            def layer0(b):
                transposed(b)
                act.wait_ge(l0["sub"], b + 1)
                nc.scalar.activation(W1_[b][:, 0:NT * K], W1_[b][:, 0:NT * K], ACT.Exp).then_inc(l0["exp"], 1)
                act.wait_ge(l0["nM"], b + 1)
                nc.scalar.activation(small[b][:, 8:12], small[b][:, 0:4], ACT.Exp, bias=small[b][:, 6:7],
                                     accum_out=small[b][:, 12:13]).then_inc(l0["e"], 1)
                act.wait_ge(l0["PT"], b + 1)
                nc.scalar.activation(W2_[b][0:K, :], bank[4 * b + 2][0:K, :], ACT.Copy).then_inc(l0["PTs"], 1)

            def layer1(b):
                transposed(2 + b)
                act.wait_ge(l1["k"], b + 1)
                nc.scalar.activation(W3_[b][:, :], bank[4 * b + 1][:, :], ACT.Relu).then_inc(l1["kr"], 1)
                act.wait_ge(l1["r"], b + 1)
                nc.scalar.activation(W4_[b][:, :], bank[4 * b + 2][:, :], ACT.Tanh, scale=0.5).then_inc(l1["rt"], 1)

            def layer2(b):
                transposed(4 + b)
                act.wait_ge(l2["sub"], b + 1)
                nc.scalar.activation(W1_[b][:, 0:NT * K], W1_[b][:, 0:NT * K], ACT.Exp).then_inc(l2["exp"], 1)
                act.wait_ge(l2["shift2"], b + 1)
                nc.scalar.activation(W2_[b][0:K, :], bank[4 * b + 2][0:K, :], ACT.Exp, bias=small[b][0:K, 22:23],
                                     accum_out=small[b][0:K, 23:24]).then_inc(l2["exp2"], 1)
                act.wait_ge(l2["PT"], b + 1)
                nc.scalar.activation(W3_[b][0:K, :], bank[4 * b + 3][0:K, :], ACT.Copy).then_inc(l2["PTs"], 1)
                act.wait_ge(l2["P2T"], b + 1)
                nc.scalar.activation(W4_[b][:, 0:NT * K], bank[4 * b][:, 0:NT * K], ACT.Copy).then_inc(l2["P2Ts"], 1)
                act.wait_ge(l2["ah"], b + 1)
                nc.scalar.activation(AhT[b][:, :], bank[4 * b + 2][:, 0:K], ACT.Copy).then_inc(l2["ahs"], 1)
                act.wait_ge(l2["s2cT"], b + 1)
                nc.scalar.activation(s2cT[b][:, :], bank[4 * b + 2][:, 256:256 + K], ACT.Copy).then_inc(l2["s2cTs"], 1)
                act.wait_ge(l2["s2g"], b + 1)
                nc.scalar.activation(intV[b][:, 1, :], bank[4 * b + 2][0:K, 384:512], ACT.Copy).then_inc(l2["s2gs"], 1)
                act.wait_ge(l2["s2ci"], b + 1)
                nc.scalar.activation(W2_[b][:, :], bank[4 * b + 3][:, :], ACT.Copy).then_inc(l2["sc"], 1)
                act.wait_ge(l2["z"], b + 1)
                nc.scalar.activation(W1_[b][:, :], bank[4 * b][:, :], ACT.Tanh, scale=0.5).then_inc(l2["t"], 1)

            for b in range(B):
                layer0(b)
            for b in range(B):
                layer1(b)
            for b in range(B):
                layer2(b)

            def route(n):
                for b in range(B):
                    act.wait_ge(m["sub"], 2 * n + b + 1)
                    nc.scalar.activation(ex[b][:, :, :], lg[b][:, :, :], ACT.Exp).then_inc(m["exp"], 1)
                for b in range(B):
                    act.wait_ge(m["cT"], 2 * n + b + 1)
                    nc.scalar.activation(cT[:, b * S:(b + 1) * S], bank[BANKC[b]][0:2 * E, :],
                                         ACT.Copy).then_inc(m["cTs"], 1)

            def values(n):
                act.wait_ge(kv["pe"], n + 1)
                nc.scalar.activation(kT[:, :], bank[1][:, 0:B * K], ACT.Copy, scale=float(DH) ** -0.5)
                nc.scalar.activation(vN[:, :, :], bank[2][0:K, 0:B * D], ACT.Copy).then_inc(kv["act"], 1)

            for b in range(B):
                transposed(6 + b)
            route(0)
            values(0)

            def slot_hi(i, p, first, nd, ready, free_at, slot_free):
                act.wait_ge(raw_in[p], 32 * (first + i + 1))
                wait_positive(act, slot_free, free_at)
                nc.scalar.activation(wuh[p][:, :], up_raw[p][:, 0:F1], ACT.Copy)
                if first == 0:
                    nc.scalar.activation(b1s[p][:, :], up_raw[p][:, F1:F1 + C1], ACT.Copy)
                nc.scalar.activation(wdh[p][:, 0:nd, :], down_raw[p][:, 0:nd, :], ACT.Copy).then_inc(ready, 1)

            def split1(i, p):
                slot_hi(i, p, 0, C1, q["wh"], N1 * i + N1 // 2 * p - N1 // 2, q["free"])

            def body1(i, last):
                for n, (p, b, c) in enumerate(CH1):
                    g = N1 * i + n
                    if n == 1:
                        split1(i, 1)
                    if n == N1 // 2 + 1 and not last:
                        split1(i + 1, 0)
                    act.wait_ge(q["h"], g + 1)
                    nc.scalar.activation(ring[n % 4][:, :], bank[BANKS1[n % 4]][:, :], ACT.Gelu,
                                         bias=b1s[p][:, c:c + 1]).then_inc(q["gelu"], 1)

            act.wait_ge(ld["moe1"], 80)
            split1(0, 0)
            body1(0, False)
            with act.Fori(1, PASSES - 1) as i:
                body1(i, False)
            body1(PASSES - 1, True)

            def combine(n, b):
                chunks, free = ((C1, q["free"]), (C2, r["free"]))[n]
                act.wait_ge(free, chunks * (E * B - B + 1 + b))
                nc.scalar.activation(W1_[b][:, :], bank[4 * b][:, :], ACT.Copy).then_inc(m["outTs"], 1)

            for b in range(B):
                combine(0, b)

            def attend(n):
                base = [8, 12][n]
                for b in range(B):
                    transposed(base + b)
                    act.wait_ge(at["q"], 2 * n + b + 1)
                    if n == 0:
                        nc.scalar.activation(qh[b][:, :], bank[4 * b][:, :], ACT.Copy).then_inc(at["qhi"], 1)
                    else:
                        nc.scalar.activation(qh[b][:, :], bank[4 * b][:, :], ACT.Identity,
                                             bias=col("bq3")).then_inc(at["qhi"], 1)
                for b in range(B):
                    for t in range(NT):
                        T = NT * (B * n + b) + t
                        act.wait_ge(at["sub"], 3 * (T + 1))
                        nc.scalar.activation(Sx[T % 2][:, 0:SPAN], Sx[T % 2][:, 0:SPAN], ACT.Exp).then_inc(at["exp"], 1)
                        if T >= 2:
                            act.wait_ge(at["O"], T - 1)
                        for j, w in enumerate((512, 512, 256)):
                            act.wait_ge(at["T"], 3 * T + j + 1)
                            nc.scalar.activation(PT[T % 2][:, 512 * j:512 * j + w], bank[5 + j][:, 0:w],
                                                 ACT.Copy).then_inc(at["PT"], 1)
                    act.wait_ge(at["OT"], 2 * n + b + 1)
                    nc.scalar.activation(W2_[b][:, :], bank[5][:, :], ACT.Copy).then_inc(at["OTs"], 1)

            attend(0)
            for b in range(B):
                transposed(10 + b)
            route(1)
            values(1)

            def split2(i, p):
                slot_hi(i, p, PASSES, C2, r["wh"], N2 * i + N2 // 2 * p - N2 // 2, r["free"])

            def body2(i, last):
                for n, (p, b, c) in enumerate(CH2):
                    g = N2 * i + n
                    if n == 1:
                        split2(i, 1)
                    if n == N2 // 2 + 1 and not last:
                        split2(i + 1, 0)
                    act.wait_ge(r["g"], g + 1)
                    nc.scalar.activation(ring[n % 4][:, :], bank[BANKG[n % 2]][:, :], ACT.Silu).then_inc(r["silu"], 1)

            split2(0, 0)
            body2(0, False)
            with act.Fori(1, PASSES - 1) as i:
                body2(i, False)
            body2(PASSES - 1, True)
            for b in range(B):
                combine(1, b)
            attend(1)

            for b in range(B):
                transposed(14 + b)
                act.wait_ge(l3["s"], b + 1)
                nc.scalar.activation(W1_[b][:, :], bank[4 * b + 1][:, :], ACT.Identity,
                                     bias=col("bin")).then_inc(l3["ss"], 1)
                act.wait_ge(l3["ss"], b + 1)
                for i in range(NH):
                    n = NH * b + i
                    if n >= 4:
                        act.wait_ge(l3["acc"], n - 3)
                    nc.scalar.activation(ring[n % 4][:, :], W1_[b][:, :], ACT.Relu,
                                         scale=cols[:, C_W1 + i:C_W1 + i + 1],
                                         bias=cols[:, C_B1 + i:C_B1 + i + 1]).then_inc(l3["u"], 1)

        @block.vector
        def _(dve):
            steps = [0]
            V = nc.vector

            def link(ins):
                steps[0] += 1
                ins.then_inc(dve_step, 1)
                dve.wait_ge(dve_step, steps[0])

            def statistics(k):
                b = k % B
                for t in range(NT):
                    last = V.bn_stats(stats[b][:, t, :], x[b][:, t, :])
                link(last)
                for t in range(NT):
                    last = V.bn_aggr(mv[b][:, t, :], stats[b][:, t, :])
                link(last)
                V.tensor_scalar(negmean[b][:, :], mv[b][:, :, 0], -1.0, None, ALU.mult)
                V.tensor_scalar(var[b][:, :], mv[b][:, :, 1], EPS, None, ALU.add).then_inc(ln_var, 1)

            def update(k, psum, gate):
                b = k % B
                V.scalar_tensor_tensor(x[b][:, :, :], psum, gate, x[b][:, :, :], ALU.mult, ALU.add).then_inc(resid, 1)
                dve.wait_ge(resid, k + 1)
                if k + 2 < 16:
                    statistics(k + 2)

            def tiles3(ap, w=K):
                return ap.rearrange("p (t k) -> p t k", k=w)

            for b in range(B):
                dve.wait_ge(ld[f"x{b}"], 16)
                statistics(b)
            dve.wait_ge(ld["ctx"], 48)
            V.tensor_scalar(simR[:, :], ctxT[:, :], col("w3"), col("w1"), ALU.mult, ALU.add).then_inc(p0_dve, 1)
            dve.wait_ge(gates, 1)
            V.tensor_scalar(htg[:, :], tg[:, :], 0.5, None, ALU.mult)
            for n, (name, g) in enumerate((("b_qv", 0), ("bo3", 3), ("bout", 7))):
                last = V.tensor_scalar(tgb[:, n, :], row(name), tg[:, g:g + 1], None, ALU.mult)
            last.then_inc(tgb_ready, 1)
            dve.wait_ge(ld["const"], 16)
            V.tensor_copy(ident_b[:, :], ident)
            dve.wait_ge(ready_const, 1)
            V.tensor_copy(sel[:, :, :], const[0:4 * B, K_SEL:K_SEL + 4].unsqueeze(2).broadcast_to([4 * B, 4, P]))
            V.tensor_scalar(zero_r[:, :], ones[0:4 * B, :], 0.0, None, ALU.mult)
            dve.wait_ge(ld["mask"], 16)
            V.tensor_scalar(nb[:, :, :, :], mask[:, :, :, :], 0.0, MASKED, ALU.is_equal, ALU.mult).then_inc(nb_ready, 1)
            dve.wait_ge(p2_pe, 1)
            V.tensor_tensor(Vs[:, :, :], bank[5][0:K, 0:B * D].rearrange("k (b d) -> k b d", b=B),
                            row("bv_s", K).unsqueeze(1).broadcast_to([K, B, D]), ALU.add).then_inc(p2_dve, 1)
            dve.wait_ge(p2_pe, 2)
            V.tensor_tensor(VsG[:, :, :], bank[5][0:K, B * D:2 * B * D].rearrange("k (b d) -> k b d", b=B),
                            row("bg", K).unsqueeze(1).broadcast_to([K, B, D]), ALU.add).then_inc(p2_dve, 1)

            def softmax_in(b, S_sem, sub_sem, maxcol):
                dve.wait_ge(S_sem, b + 1)
                sc = tiles3(bank[4 * b + 1][:, 0:NT * K])
                link(V.reduce_max(small[b][:, maxcol:maxcol + NT], sc, AX))
                V.tensor_tensor(tiles3(W1_[b][:, 0:NT * K]), sc,
                                small[b][:, maxcol:maxcol + NT].unsqueeze(2).broadcast_to([P, NT, K]),
                                ALU.subtract).then_inc(sub_sem, 1)

            def softmax_out(b, exp_sem, P_sem, sumcol):
                dve.wait_ge(exp_sem, b + 1)
                pr = tiles3(W1_[b][:, 0:NT * K])
                link(V.reduce_sum(small[b][:, sumcol:sumcol + NT], pr, AX))
                link(V.reciprocal(small[b][:, sumcol + NT:sumcol + 2 * NT], small[b][:, sumcol:sumcol + NT]))
                V.tensor_tensor(pr, pr, small[b][:, sumcol + NT:sumcol + 2 * NT].unsqueeze(2).broadcast_to([P, NT, K]),
                                ALU.mult).then_inc(P_sem, 1)

            def layer0(b):
                softmax_in(b, l0["S"], l0["sub"], 0)
                V.reduce_max(small[b][:, 4:5], small[b][:, 0:NT], AX).then_inc(l0["m1"], 1)
                softmax_out(b, l0["exp"], l0["P"], 24)
                dve.wait_ge(l0["hq"], b + 1)
                dve.wait_ge(hT_ready, b + 1)
                V.tensor_tensor(W3_[b][:, :], hT[b], bank[4 * b + 3][:, :], ALU.mult).then_inc(l0["u"], 1)
                dve.wait_ge(l0["hc"], b + 1)
                link(V.reciprocal(small[b][:, 14:15], bank[4 * b][:, 1:2]))
                link(V.tensor_tensor(small[b][:, 15:16], bank[4 * b][:, 0:1], small[b][:, 14:15], ALU.mult))
                V.scalar_tensor_tensor(w14[b][:, :], mat("Wqv4"), small[b][:, 15:16], mat("Wqv1"),
                                       ALU.mult, ALU.add).then_inc(l0["W"], 1)
                dve.wait_ge(l0["out"], b + 1)
                dve.wait_ge(x_biased, b + 1)
                update(b, bank[4 * b + 1][:, :].rearrange("p (t d) -> p t d", d=D), tg[:, 0:1])

            def layer1(b):
                k = 2 + b
                dve.wait_ge(hT_ready, k + 1)
                link(V.tensor_tensor(W1_[b][:, :], hTz[b][:, 1:S + 1], hTz[b][:, 0:S], ALU.subtract))
                V.scalar_tensor_tensor(W2_[b][:, :], W1_[b][:, :], col("mu_k"), hTz[b][:, 0:S], ALU.mult,
                                       ALU.add).then_inc(l1["x"], 1)
                V.scalar_tensor_tensor(W4_[b][:, :], W1_[b][:, :], col("mu_r"), hTz[b][:, 0:S], ALU.mult,
                                       ALU.add).then_inc(l1["x"], 1)
                dve.wait_ge(l1["kr"], b + 1)
                V.scalar_tensor_tensor(W3_[b][:, :], bank[4 * b + 1][:, :], 0.0, W3_[b][:, :], ALU.max,
                                       ALU.mult).then_inc(l1["ka"], 1)
                dve.wait_ge(l1["v"], b + 1)
                dve.wait_ge(l1["rt"], b + 1)
                link(V.scalar_tensor_tensor(W1_[b][:, :], W4_[b][:, :], 1.0, bank[4 * b + 3][:, :], ALU.add, ALU.mult))
                update(k, W1_[b][:, :].rearrange("p (t d) -> p t d", d=D), htg[:, 4:5])

            def layer2(b):
                k = 4 + b
                softmax_in(b, l2["S"], l2["sub"], 16)
                dve.wait_ge(l2["s2"], b + 1)
                link(V.reduce_max(small[b][0:K, 20:21], bank[4 * b + 2][0:K, :], AX))
                link(V.tensor_tensor(small[b][0:K, 21:22], small[b][0:K, 20:21], kshift[:, b:b + 1], ALU.add))
                V.tensor_tensor(small[b][0:K, 22:23], kshift[:, b:b + 1], small[b][0:K, 21:22],
                                ALU.subtract).then_inc(l2["shift2"], 1)
                softmax_out(b, l2["exp"], l2["P"], 32)
                dve.wait_ge(l2["exp2"], b + 1)
                link(V.reciprocal(small[b][0:K, 40:41], small[b][0:K, 23:24]))
                dve.wait_ge(l2["s2c"], b + 1)
                V.scalar_tensor_tensor(intV[b][:, 0, :], bank[4 * b + 2][0:K, 128:256], small[b][0:K, 40:41],
                                       row("bv_c", K), ALU.mult, ALU.add).then_inc(l2["s2cs"], 1)
                dve.wait_ge(l2["sc"], b + 1)
                dve.wait_ge(l2["c2s"], b + 1)
                link(V.tensor_tensor(W4_[b][:, :], bank[4 * b + 1][:, :], W2_[b][:, :], ALU.subtract))
                dve.wait_ge(l2["t"], b + 1)
                link(V.scalar_tensor_tensor(W4_[b][:, :], W1_[b][:, :], 1.0, W4_[b][:, :], ALU.add, ALU.mult))
                link(V.scalar_tensor_tensor(W4_[b][:, :], W4_[b][:, :], 0.5, W2_[b][:, :], ALU.mult, ALU.add))
                update(k, W4_[b][:, :].rearrange("p (t d) -> p t d", d=D), tg[:, 1:2])

            for b in range(B):
                layer0(b)
            for b in range(B):
                layer1(b)
            for b in range(B):
                layer2(b)

            def ranks(src, b, n, lt):
                big, same = gt[b][:, :, 0:n, 0:n], eq[b][:, :, 0:n, 0:n]
                this = src.unsqueeze(3).broadcast_to([P, NT, n, n])
                other = src.unsqueeze(2).broadcast_to([P, NT, n, n])
                V.tensor_tensor(big, other, this, ALU.is_gt)
                link(V.tensor_tensor(same, other, this, ALU.is_equal))
                link(V.tensor_tensor(same, same, lt.unsqueeze(1).broadcast_to([P, NT, n, n]), ALU.mult))
                link(V.tensor_tensor(big, big, same, ALU.add))
                return big

            def parts(k, b):
                dve.wait_ge(hT_ready, k + 1)
                link(V.tensor_copy(hhi[b][:, :], hT[b]))
                V.tensor_tensor(hlo[b][:, :], hT[b], hhi[b][:, :].bitcast(F32), ALU.subtract).then_inc(m["split"], 1)

            lt8 = const[:, K_LT8:K_LT8 + 64].rearrange("p (e j) -> p e j", j=8)
            lt4 = const[:, K_LT4:K_LT4 + 16].rearrange("p (e j) -> p e j", j=4)
            rank = [small[b][:, 0:32].rearrange("p (t e) -> p t e", e=E) for b in range(B)]

            def bcast_e(ap, n=E):
                return ap.unsqueeze(2).broadcast_to([P, NT, n])

            def logits(n, b):
                dve.wait_ge(m["lg"], 2 * n + b + 1)
                lp = bank[3 + 4 * b][:, 0:NT * E].rearrange("p (t e) -> p t e", e=E)
                link(V.reduce_max(small[b][:, 56:60], lp, AX))
                V.tensor_tensor(lg[b][:, :, :], lp, bcast_e(small[b][:, 56:60]), ALU.subtract).then_inc(m["sub"], 1)
                dve.wait_ge(m["sub"], 2 * n + b + 1)

            def weights(n, b, top):
                link(V.tensor_tensor(top, top, ex[b][:, :, :], ALU.mult))
                link(V.reduce_sum(small[b][:, 56:60], top, AX))
                link(V.reciprocal(small[b][:, 60:64], small[b][:, 56:60]))
                link(V.tensor_tensor(top, top, bcast_e(small[b][:, 60:64]), ALU.mult))
                by_parity = top.rearrange("p t (i q) -> p t q i", q=2)
                cp = c2[b][:, :, :].rearrange("p t (q j i) -> p t q j i", q=2, j=2)
                link(V.tensor_copy(cp[:, :, :, 0, :], by_parity))
                V.tensor_tensor(cp[:, :, :, 1, :], by_parity, cp[:, :, :, 0, :].bitcast(F32),
                                ALU.subtract).then_inc(m["c"], 1)

            def route1(b):
                logits(0, b)
                big = ranks(lg[b][:, :, :], b, E, lt8)
                link(V.tensor_reduce(rank[b], big, AX, ALU.add))
                link(V.tensor_scalar(rank[b], rank[b], 1.5, None, ALU.is_lt))
                dve.wait_ge(m["exp"], b + 1)
                weights(0, b, rank[b])

            def route2(b):
                logits(1, b)
                dve.wait_ge(m["exp"], 2 + b + 1)
                link(V.reduce_sum(small[b][:, 56:60], ex[b][:, :, :], AX))
                link(V.reciprocal(small[b][:, 60:64], small[b][:, 56:60]))
                link(V.tensor_tensor(ex[b][:, :, :], ex[b][:, :, :], bcast_e(small[b][:, 60:64]), ALU.mult))
                best = small[b][:, 40:56].rearrange("p (t g) -> p t g", g=GROUPS)
                link(V.reduce_max(best, ex[b][:, :, :].rearrange("p t (g e) -> p t g e", e=2), AX))
                big = ranks(best, b, GROUPS, lt4)
                grank = small[b][:, 0:16].rearrange("p (t g) -> p t g", g=GROUPS)
                link(V.tensor_reduce(grank, big, AX, ALU.add))
                link(V.tensor_scalar(grank, grank, 1.5, None, ALU.is_lt))
                link(V.tensor_tensor(ex[b][:, :, :].rearrange("p t (g e) -> p t g e", e=2),
                                     ex[b][:, :, :].rearrange("p t (g e) -> p t g e", e=2),
                                     grank.unsqueeze(3).broadcast_to([P, NT, GROUPS, 2]), ALU.mult))
                big = ranks(ex[b][:, :, :], b, E, lt8)
                link(V.tensor_reduce(rank[b], big, AX, ALU.add))
                link(V.tensor_scalar(rank[b], rank[b], 1.5, None, ALU.is_lt))
                weights(1, b, rank[b])

            def keys(n):
                dve.wait_ge(kv["act"], n + 1)
                if n == 1:
                    dve.wait_ge(kv["pool"], 1)
                link(V.tensor_copy(kTh[:, :], kT[:, :]))
                V.tensor_tensor(kTl[:, :], kT[:, :], kTh[:, :].bitcast(F32), ALU.subtract).then_inc(kv["hi"], 1)
                for b in range(B):
                    for j in range(3):
                        c0, c1 = 4 * j, min(4 * j + 4, CH)
                        dve.wait_ge(kv["rep"], 3 * (2 * n + b) + j + 1)
                        V.tensor_tensor(
                            vbd[b][:, c0:c1, 0:D].rearrange("p c (h e) -> p c h e", e=DH),
                            bank[1 + j][:, 0:(c1 - c0) * P].rearrange("p (c h e) -> p c h e", h=H, e=DH),
                            pair[:, c0:c1, :].unsqueeze(3).broadcast_to([P, c1 - c0, H, DH]),
                            ALU.mult).then_inc(kv["bd"], 1)

            for b in range(B):
                parts(6 + b, b)
                route1(b)
            keys(0)

            def body1(i, last):
                for n, (p, b, c) in enumerate(CH1):
                    g = N1 * i + n
                    dve.wait_ge(q["gelu"], g + 1)
                    V.tensor_tensor(ring[n % 4][:, :], ring[n % 4][:, :], bank[BANKC[b]][:, :],
                                    ALU.mult).then_inc(q["scale"], 1)
                    dve.wait_ge(q["scale"], g + 1)
                    ins = V.tensor_copy(rhi[n % 4][:, :], ring[n % 4][:, :])
                    ins.then_inc(q["hi"], 1)
                    if not lo_on_pool(n):
                        dve.wait_ge(q["hi"], g + 1)
                        V.tensor_tensor(rlo[n % 4][:, :], ring[n % 4][:, :], rhi[n % 4][:, :].bitcast(F32),
                                        ALU.subtract).then_inc(q["loD"], 1)

            body1(0, False)
            with dve.Fori(1, PASSES - 1) as i:
                body1(i, False)
            body1(PASSES - 1, True)

            for b in range(B):
                dve.wait_ge(m["outN"], b + 1)
                update(6 + b, bank[1 + b][:, :].rearrange("p (t d) -> p t d", d=D), tg[:, 5:6])

            def attend(n):
                base, gate = [8, 12][n], [2, 3][n]
                for b in range(B):
                    dve.wait_ge(at["qhi"], 2 * n + b + 1)
                    if n == 0:
                        V.tensor_tensor(ql[b][:, :], bank[4 * b][:, :], qh[b][:, :].bitcast(F32),
                                        ALU.subtract).then_inc(at["qlo"], 1)
                    else:
                        V.scalar_tensor_tensor(ql[b][:, :], bank[4 * b][:, :], col("bq3"), qh[b][:, :].bitcast(F32),
                                               ALU.add, ALU.subtract).then_inc(at["qlo"], 1)
                for b in range(B):
                    def normalise(t):
                        T = NT * (B * n + b) + t
                        dve.wait_ge(at["O"], T + 1)
                        o = bank[4 * ((b + t) % 2)][:, 0:VW]
                        link(V.reciprocal(small[b][:, 16 * (t % 2):16 * (t % 2) + 16], o[:, D:VW]))
                        V.tensor_tensor(W1_[b][:, t * D:(t + 1) * D].rearrange("p (h e) -> p h e", e=DH),
                                        o[:, 0:D].rearrange("p (h e) -> p h e", e=DH),
                                        small[b][:, 16 * (t % 2):16 * (t % 2) + 16].unsqueeze(2).broadcast_to([P, H, DH]),
                                        ALU.mult).then_inc(at["norm"], 1)

                    for t in range(NT):
                        T = NT * (B * n + b) + t
                        if T >= 2:
                            dve.wait_ge(at["T"], 3 * (T - 1))
                        for j, (h0, h1) in enumerate(HB):
                            dve.wait_ge(at["S"], 3 * T + j + 1)
                            sc = bank[1 + j][:, 0:(h1 - h0) * K].rearrange("p (h k) -> p h k", k=K)
                            mx = small[b][:, 32 + h0:32 + h1]
                            link(V.reduce_max(mx, sc, AX))
                            V.tensor_tensor(Sx[T % 2][:, h0 * K:h1 * K].rearrange("p (h k) -> p h k", k=K), sc,
                                            mx.unsqueeze(2).broadcast_to([P, h1 - h0, K]),
                                            ALU.subtract).then_inc(at["sub"], 1)
                        if t >= 1:
                            normalise(t - 1)
                    normalise(NT - 1)
                    dve.wait_ge(at["out"], 2 * n + b + 1)
                    if n == 1:
                        dve.wait_ge(x_biased, B + b + 1)
                    update(base + b, bank[4 * b][:, :].rearrange("p (t d) -> p t d", d=D), tg[:, gate:gate + 1])

            attend(0)
            for b in range(B):
                parts(10 + b, b)
                route2(b)
            keys(1)

            def body2(i, last):
                for n, (p, b, c) in enumerate(CH2):
                    g = N2 * i + n
                    dve.wait_ge(r["silu"], g + 1)
                    V.tensor_tensor(ring[n % 4][:, :], ring[n % 4][:, :], bank[BANKU[n % 2]][:, :],
                                    ALU.mult).then_inc(r["mul"], 1)
                    dve.wait_ge(r["mul"], g + 1)
                    V.tensor_tensor(ring[n % 4][:, :], ring[n % 4][:, :], bank[BANKC[b]][:, :],
                                    ALU.mult).then_inc(r["scale"], 1)
                    dve.wait_ge(r["scale"], g + 1)
                    V.tensor_copy(rhi[n % 4][:, :], ring[n % 4][:, :]).then_inc(r["hi"], 1)
                    if not unit_on_pool(n):
                        dve.wait_ge(r["hi"], g + 1)
                        V.tensor_tensor(rlo[n % 4][:, :], ring[n % 4][:, :], rhi[n % 4][:, :].bitcast(F32),
                                        ALU.subtract).then_inc(r["loD"], 1)

            body2(0, False)
            with dve.Fori(1, PASSES - 1) as i:
                body2(i, False)
            body2(PASSES - 1, True)
            for b in range(B):
                dve.wait_ge(m["outN"], B + b + 1)
                update(10 + b, bank[1 + b][:, :].rearrange("p (t d) -> p t d", d=D), tg[:, 6:7])
            attend(1)

            dve.wait_ge(ld["b2m"], 16)
            for b in range(B):
                for i in range(NH):
                    n = NH * b + i
                    dve.wait_ge(l3["u"], n + 1)
                    w = cols[:, C_W2 + i:C_W2 + i + 1]
                    if i == 0:
                        V.tensor_scalar(W2_[b][:, :], ring[n % 4][:, :], w, b2col[:, 0:1], ALU.mult,
                                        ALU.add).then_inc(l3["acc"], 1)
                    else:
                        V.scalar_tensor_tensor(W2_[b][:, :], ring[n % 4][:, :], w, W2_[b][:, :], ALU.mult,
                                               ALU.add).then_inc(l3["acc"], 1)
                    if i + 1 < NH:
                        dve.wait_ge(l3["acc"], n + 1)
                dve.wait_ge(l3["out"], b + 1)
                dve.wait_ge(x_biased, 2 * B + b + 1)
                update(14 + b, bank[4 * b + 2][:, :].rearrange("p (t d) -> p t d", d=D), tg[:, 7:8])

        @block.tensor
        def _(pe):
            mm = nc.tensor.matmul

            def mm3(o, lh, ll, rh, rl, start, stop):
                mm(o, lh, rh, start=start, stop=False)
                mm(o, lh, rl, start=False, stop=False)
                return mm(o, ll, rh, start=False, stop=stop)

            def transposes(k):
                b = k % B
                pe.wait_ge(ln_h, k + 1)
                for t in range(NT):
                    last = nc.tensor.transpose(tile(bank[4 * b], t), h[b][:, t, :], ident)
                last.then_inc(ln_T, 1)

            pe.wait_ge(ld["ctx"], 48)
            pe.wait_ge(ld["l0"], 16)
            mm(bank[1][0:1, 0:B * K], col("w2"), ctxT[:, :], start=True, stop=True)
            for b in range(B):
                last = mm(bank[2][0:K, b * D:(b + 1) * D], ctxT[:, b * K:(b + 1) * K], mat("Wqv2"), start=True, stop=True)
            last.then_inc(p0_pe, 1)
            pe.wait_ge(ld["l2"], 16)
            mm(bank[3][:, 0:B * K], mat("WksT"), ctxT[:, :], start=True, stop=True)
            mm(bank[3][:, B * K:2 * B * K], mat("WqsT"), ctxT[:, :], start=True, stop=True)
            mm(bank[6][:, 0:B * K], mat("WvsT"), ctxT[:, :], start=True, stop=True)
            for b in range(B):
                last = mm(bank[5][0:K, b * D:(b + 1) * D], ctxT[:, b * K:(b + 1) * K], mat("WvsT"), start=True, stop=True)
            last.then_inc(p2_pe, 1)
            pe.wait_ge(p2_act, 1)
            pe.wait_ge(p0_act, 1)
            pe.wait_ge(p2_dve, 1)
            mm(bank[7][:, 0:B * K], mat("Wqc"), KsT[:, :], start=True, stop=True)
            mm(bank[7][:, B * K:2 * B * K], mat("Wkc"), QsT[:, :], start=True, stop=True)
            mm(bank[1][0:1, B * K:2 * B * K], col("bq_c"), KsT[:, :], start=True, stop=True)
            for b in range(B):
                mm(bank[2][0:K, 256 + b:257 + b], QsT[:, b * K:(b + 1) * K], col("bk_c"), start=True, stop=True)
            for b in range(B):
                last = mm(bank[5][0:K, (2 + b) * D:(3 + b) * D], VsT[:, b * K:(b + 1) * K], mat("Wg1T"), start=True, stop=True)
            last.then_inc(p2_pe, 1)
            pe.wait_ge(ld["const"], 16)
            pe.wait_ge(ready_const, 1)
            pe.wait_ge(p2_act, 2)
            pe.wait_ge(p2_dve, 2)

            def scores(b, right, shift, done):
                for t in range(NT):
                    o = bank[4 * b + 1][:, t * K:(t + 1) * K]
                    mm(o, tile(hT[b], t), right[:, b * K:(b + 1) * K], start=True, stop=False)
                    last = mm(o, ones[0:1, :], shift[:, b * K:(b + 1) * K], start=False, stop=True)
                last.then_inc(done, 1)

            def layer0(b):
                transposes(b)
                pe.wait_ge(hT_ready, b + 1)
                pe.wait_ge(p0_dve, 1)
                scores(b, simR, simrow, l0["S"])
                pe.wait_ge(l0["P"], b + 1)
                for t in range(NT):
                    last = nc.tensor.transpose(bank[4 * b + 2][0:K, t * P:(t + 1) * P], W1_[b][:, t * K:(t + 1) * K], ident)
                last.then_inc(l0["PT"], 1)
                pe.wait_ge(l0["e"], b + 1)
                for t in range(NT):
                    mm(bank[4 * b][:, 0:1], h[b][:, t, :], small[b][:, 8 + t:9 + t], start=(t == 0), stop=(t == NT - 1))
                mm(bank[4 * b][:, 1:2], ones[:, :], small[b][:, 12:13], start=True, stop=True).then_inc(l0["hc"], 1)
                pe.wait_ge(l0["PTs"], b + 1)
                mm(bank[4 * b + 3][:, :], ctxN[:, b, :], W2_[b][0:K, :], start=True, stop=True).then_inc(l0["hq"], 1)
                pe.wait_ge(l0["W"], b + 1)
                pe.wait_ge(l0["u"], b + 1)
                for t in range(NT):
                    o = tile(bank[4 * b + 1], t)
                    mm(o, tile(hT[b], t), w14[b][:, :], start=True, stop=False)
                    mm(o, W2_[b][0:K, t * P:(t + 1) * P], ctxW2[:, b, :], start=False, stop=False)
                    last = mm(o, tile(W3_[b], t), mat("Wqv3"), start=False, stop=True)
                last.then_inc(l0["out"], 1)

            def layer1(b):
                transposes(2 + b)
                pe.wait_ge(l1["x"], 2 * b + 1)
                mm(bank[4 * b + 1][:, :], mat("WkT"), W2_[b][:, :], start=True, stop=True).then_inc(l1["k"], 1)
                pe.wait_ge(l1["x"], 2 * b + 2)
                for t in range(NT):
                    last = mm(tile(bank[4 * b + 2], t), tile(W4_[b], t), mat("WrT"), start=True, stop=True)
                last.then_inc(l1["r"], 1)
                pe.wait_ge(l1["ka"], b + 1)
                for t in range(NT):
                    last = mm(tile(bank[4 * b + 3], t), tile(W3_[b], t), mat("WvT"), start=True, stop=True)
                last.then_inc(l1["v"], 1)

            def layer2(b):
                transposes(4 + b)
                pe.wait_ge(hT_ready, 4 + b + 1)
                scores(b, Mq, qrow, l2["S"])
                mm(bank[4 * b + 2][0:K, :], Mk[:, b * K:(b + 1) * K], hT[b], start=True, stop=True).then_inc(l2["s2"], 1)
                pe.wait_ge(l2["P"], b + 1)
                for t in range(NT):
                    last = nc.tensor.transpose(bank[4 * b + 3][0:K, t * P:(t + 1) * P], W1_[b][:, t * K:(t + 1) * K], ident)
                last.then_inc(l2["PT"], 1)
                pe.wait_ge(l2["exp2"], b + 1)
                for t in range(NT):
                    last = nc.tensor.transpose(bank[4 * b][:, t * K:(t + 1) * K], W2_[b][0:K, t * P:(t + 1) * P],
                                               ident[0:K, 0:K])
                last.then_inc(l2["P2T"], 1)
                pe.wait_ge(l2["P2Ts"], b + 1)
                for t in range(NT):
                    last = mm(bank[4 * b + 2][:, 0:K], h[b][:, t, :], W4_[b][:, t * K:(t + 1) * K],
                              start=(t == 0), stop=(t == NT - 1))
                last.then_inc(l2["ah"], 1)
                pe.wait_ge(l2["ahs"], b + 1)
                mm(bank[4 * b + 2][0:K, 128:256], AhT[b][:, :], mat("WvcT"), start=True, stop=True).then_inc(l2["s2c"], 1)
                pe.wait_ge(l2["PTs"], b + 1)
                for t in range(NT):
                    last = mm(tile(bank[4 * b + 1], t), W3_[b][0:K, t * P:(t + 1) * P], Vs[:, b, :], start=True, stop=True)
                last.then_inc(l2["c2s"], 1)
                pe.wait_ge(l2["s2cs"], b + 1)
                nc.tensor.transpose(bank[4 * b + 2][:, 256:256 + K], intV[b][:, 0, :],
                                    ident[0:K, 0:K]).then_inc(l2["s2cT"], 1)
                for t in range(NT):
                    last = mm(tile(bank[4 * b + 3], t), interpT[:, t * P:(t + 1) * P], intV[b][:, 0, :], start=True, stop=True)
                last.then_inc(l2["s2ci"], 1)
                pe.wait_ge(l2["s2cTs"], b + 1)
                mm(bank[4 * b + 2][0:K, 384:512], s2cT[b][:, :], mat("Wg2T"), start=True, stop=True).then_inc(l2["s2g"], 1)
                pe.wait_ge(l2["s2gs"], b + 1)
                for t in range(NT):
                    o = tile(bank[4 * b], t)
                    mm(o, W3_[b][0:K, t * P:(t + 1) * P], VsG[:, b, :], start=True, stop=False)
                    last = mm(o, interpT[:, t * P:(t + 1) * P], intV[b][:, 1, :], start=False, stop=True)
                last.then_inc(l2["z"], 1)

            for b in range(B):
                layer0(b)
            pe.wait_ge(ld["l1"], 16)
            for b in range(B):
                layer1(b)
            for b in range(B):
                layer2(b)

            def router(n, b, k):
                pe.wait_ge(hT_ready, k + 1)
                for t in range(NT):
                    last = mm(bank[3 + 4 * b][:, E * t:E * (t + 1)], tile(hT[b], t),
                              rwT[:, n * E:(n + 1) * E], start=True, stop=True)
                last.then_inc(m["lg"], 1)

            def context(n):
                wk, wv = (("wk2", "wv2"), ("WkT3", "WvT3"))[n]
                mm(bank[1][:, 0:B * K], mat(wk), ctxT[:, :], start=True, stop=True)
                for b in range(B):
                    last = mm(bank[2][0:K, b * D:(b + 1) * D], ctxT[:, b * K:(b + 1) * K], mat(wv), start=True, stop=True)
                last.then_inc(kv["pe"], 1)
                pe.wait_ge(kv["act"], n + 1)
                for b in range(B):
                    for j in range(3):
                        if b == 1:
                            pe.wait_ge(kv["bd"], 3 * 2 * n + j + 1)
                        c0, c1 = 4 * j, min(4 * j + 4, CH)
                        for c in range(c0, c1):
                            last = mm(tile(bank[1 + j], c - c0), rep(c), vN[:, b, :], start=True, stop=True)
                        last.then_inc(kv["rep"], 1)

            def weights_T(n, b):
                pe.wait_ge(m["c"], 2 * n + b + 1)
                for t in range(NT):
                    last = nc.tensor.transpose(bank[BANKC[b]][0:2 * E, t * P:(t + 1) * P],
                                               c2[b][:, t, :].bitcast(F32), ident)
                last.then_inc(m["cT"], 1)

            def weights_row(i, p, b):
                mm(bank[BANKC[b]][:, :], sel[:, 2 * b + p, :], cflat[:, i, :], start=True, stop=True)

            pe.wait_ge(ld["moe1"], 80)
            for b in range(B):
                transposes(6 + b)
                router(0, b, 6 + b)
            pe.wait_ge(resid, 6)
            pe.wait_ge(ld["l3"], 16)
            for b in range(B):
                weights_T(0, b)
            context(0)
            for b in range(B):
                pe.wait_ge(m["cTs"], b + 1)
                mm(bank[4 * b][:, :], b2E[:, :], cT[:, b * S:(b + 1) * S].bitcast(F32), start=True, stop=False)
            pe.wait_ge(m["flat"], 16 * B)
            pe.wait_ge(kv["bd"], 6)
            pe.wait_ge(m["split"], B)

            def hidden1(i, n):
                p, b, c = CH1[n]
                g = N1 * i + n
                if c == 0:
                    if b == 0:
                        pe.wait_ge(q["wl"], 2 * i + p + 1)
                    wait_positive(pe, q["scale"], g - C1)
                wait_positive(pe, q["gelu"], g - 3)
                w = slice(c * P, (c + 1) * P)
                o = bank[BANKS1[n % 4]][:, :]
                mm(o, wuh[p][:, w], hhi[b][:, :], start=True, stop=False)
                if c == 0:
                    weights_row(i, p, b)
                mm(o, wuh[p][:, w], hlo[b][:, :], start=False, stop=False)
                mm(o, wul[p][:, w], hhi[b][:, :], start=False, stop=True).then_inc(q["h"], 1)

            def down1(i, n, last):
                p, b, c = CH1[n]
                g = N1 * i + n
                if lo_on_pool(n):
                    pe.wait_ge(q["loP"], POOL1 * i + pool_los(n + 1))
                else:
                    pe.wait_ge(q["loD"], (N1 - POOL1) * i + dve_los(n + 1))
                end = last and (p, c) == (1, C1 - 1)
                mm3(bank[4 * b][:, :], wdh[p][:, c, :], wdl[p][:, c, :], rhi[n % 4][:, :], rlo[n % 4][:, :],
                    False, end).then_inc(q["free"], 1)

            def body1(i, last):
                for n in range(N1):
                    if n + LAG1 < N1:
                        hidden1(i, n + LAG1)
                    elif not last:
                        hidden1(i + 1, n + LAG1 - N1)
                    down1(i, n, last)

            for n in range(LAG1):
                hidden1(0, n)
            body1(0, False)
            with pe.Fori(1, PASSES - 1) as i:
                body1(i, False)
            body1(PASSES - 1, True)

            def finish(n):
                for b in range(B):
                    pe.wait_ge(m["outTs"], 2 * n + b + 1)
                    for t in range(NT):
                        last = nc.tensor.transpose(tile(bank[1 + b], t), tile(W1_[b], t), ident)
                    last.then_inc(m["outN"], 1)

            finish(0)

            def attend(n):
                base = [8, 12][n]
                wq, wo = (("wq2", "wo2"), ("WqT3", "WoT3"))[n]
                pe.wait_ge(nb_ready, 1)
                pe.wait_ge(ld["pair"], 32)
                pe.wait_ge(kv["pool"], n + 1)
                for b in range(B):
                    transposes(base + b)
                    pe.wait_ge(hT_ready, base + b + 1)
                    mm(bank[4 * b][:, :], mat(wq), hT[b], start=True, stop=True).then_inc(at["q"], 1)

                def scores_of(u):
                    b, t = u // NT, u % NT
                    T = NT * B * n + u
                    pe.wait_ge(at["qlo"], 2 * n + b + 1)
                    for j, (h0, h1) in enumerate(HB):
                        if u >= 1:
                            pe.wait_ge(at["sub"], 3 * (T - 1) + j + 1)
                        o = bank[1 + j][:, 0:(h1 - h0) * K]
                        if n == 0:
                            mm(o, ident_b[:, :], nb[:, b, t, :].unsqueeze(1).broadcast_to([P, h1 - h0, K]),
                               start=True, stop=False)
                        mm3(o, tile(qh[b], t), tile(ql[b], t), kbh[b][:, h0:h1, :], kbl[b][:, h0:h1, :],
                            n == 1, True).then_inc(at["S"], 1)

                def values_of(u):
                    b, t = u // NT, u % NT
                    T = NT * B * n + u
                    pe.wait_ge(at["exp"], T + 1)
                    if T >= 1:
                        pe.wait_ge(at["PT"], 3 * T)
                    if u == NT:
                        pe.wait_ge(at["OTs"], 2 * n + 1)
                    for c in range(CH):
                        last = nc.tensor.transpose(tile(bank[5 + c // 4], c % 4), tile(Sx[T % 2], c), ident)
                        if c % 4 == 3 or c == CH - 1:
                            last.then_inc(at["T"], 1)
                    pe.wait_ge(at["PT"], 3 * (T + 1))
                    if u >= 2:
                        pe.wait_ge(at["norm"], T - 1)
                    if u == 1:
                        pe.wait_ge(at["qlo"], 2 * n + 2)
                    if u == NT + 1:
                        pe.wait_ge(resid, base + 1)
                    o = bank[4 * ((b + t) % 2)][:, 0:VW]
                    for c in range(CH):
                        last = mm(o, tile(PT[T % 2], c), vbd[b][:, c, :], start=(c == 0), stop=(c == CH - 1))
                    last.then_inc(at["O"], 1)

                scores_of(0)
                for u in range(NT * B):
                    if u + 1 < NT * B:
                        scores_of(u + 1)
                    values_of(u)
                    if u % NT == NT - 1:
                        b = u // NT
                        pe.wait_ge(at["norm"], NT * (B * n + b + 1))
                        pe.wait_ge(at["PT"], 3 * (NT * B * n + u + 1))
                        for t in range(NT):
                            last = nc.tensor.transpose(tile(bank[5], t), tile(W1_[b], t), ident)
                        last.then_inc(at["OT"], 1)
                        pe.wait_ge(at["OTs"], 2 * n + b + 1)
                        for t in range(NT):
                            last = mm(tile(bank[4 * b], t), tile(W2_[b], t), mat(wo), start=True, stop=True)
                        last.then_inc(at["out"], 1)

            attend(0)
            for b in range(B):
                transposes(10 + b)
                router(1, b, 10 + b)
            for b in range(B):
                weights_T(1, b)
            context(1)
            pe.wait_ge(m["flat"], 32 * B)
            pe.wait_ge(kv["bd"], 12)
            pe.wait_ge(m["split"], 2 * B)

            def hidden2(i, n):
                p, b, c = CH2[n]
                g = N2 * i + n
                if c == 0:
                    if b == 0:
                        pe.wait_ge(r["wl"], 2 * i + p + 1)
                    wait_positive(pe, r["scale"], g - C2)
                wait_positive(pe, r["mul"], g - 1)
                for bk, off in ((BANKG[n % 2], 0), (BANKU[n % 2], F2)):
                    w = slice(off + c * P, off + (c + 1) * P)
                    last = mm3(bank[bk][:, :], wuh[p][:, w], wul[p][:, w], hhi[b][:, :], hlo[b][:, :], True, True)
                    if c == 0 and off == 0:
                        weights_row(i, p, b)
                last.then_inc(r["g"], 1)

            def down2(i, n, last):
                p, b, c = CH2[n]
                if unit_on_pool(n):
                    pe.wait_ge(r["loP"], POOL2 * i + pool_units(n + 1))
                else:
                    pe.wait_ge(r["loD"], (N2 - POOL2) * i + n + 1 - pool_units(n + 1))
                end = last and (p, c) == (1, C2 - 1)
                mm3(bank[4 * b][:, :], wdh[p][:, c, :], wdl[p][:, c, :], rhi[n % 4][:, :], rlo[n % 4][:, :],
                    False, end).then_inc(r["free"], 1)

            def body2(i, last):
                for n in range(N2):
                    if n + LAG2 < N2:
                        hidden2(i, n + LAG2)
                    elif not last:
                        hidden2(i + 1, n + LAG2 - N2)
                    down2(i, n, last)

            for n in range(LAG2):
                hidden2(0, n)
            for b in range(B):
                mm(bank[4 * b][:, :], zero_r[:, :], cflat[:, 0, :], start=True, stop=False)
            body2(0, False)
            with pe.Fori(1, PASSES - 1) as i:
                body2(i, False)
            body2(PASSES - 1, True)
            finish(1)
            attend(1)

            for b in range(B):
                transposes(14 + b)
                pe.wait_ge(hT_ready, 14 + b + 1)
                mm(bank[4 * b + 1][:, :], mat("WinD"), hT[b], start=True, stop=True).then_inc(l3["s"], 1)
            for b in range(B):
                pe.wait_ge(l3["acc"], NH * (b + 1))
                for t in range(NT):
                    last = mm(tile(bank[4 * b + 2], t), tile(W2_[b], t), mat("WoutD"), start=True, stop=True)
                last.then_inc(l3["out"], 1)


def shape_constants():
    c = np.zeros((P, NK), np.float32)
    c[:, K_ID:K_ID + P] = np.eye(P)
    c[np.arange(D), K_HEAD + np.arange(D) // DH] = 1
    c[:, K_LT8:K_LT8 + 64] = np.tril(np.ones((8, 8)), -1).ravel()
    c[:, K_LT4:K_LT4 + 16] = np.tril(np.ones((4, 4)), -1).ravel()
    pairs = np.arange(SPAN)
    c[pairs % K, K_REP + pairs] = 1
    pair = np.zeros((P, CH, H), np.float32)
    pair[pairs % P, pairs // P, pairs // K] = 1
    c[:, K_PAIR:K_PAIR + CH * H] = pair.reshape(P, -1)
    pos = np.clip((np.arange(S, dtype=np.float32) + np.float32(0.5)) * np.float32(K / S) - np.float32(0.5), 0, K - 1)
    lo = np.floor(pos).astype(np.int64)
    hi = np.minimum(lo + 1, K - 1)
    w = (pos - lo).astype(np.float32)
    for i in range(S):
        c[lo[i], K_INT + i] += 1 - w[i]
        c[hi[i], K_INT + i] += w[i]
    c[np.arange(8), K_SEL + np.arange(8) // 2] = 1
    return c, pair


def kernel(**inputs):
    import concourse.bacc as bacc
    from concourse.bass_utils import run_bass_kernel_spmd

    z = {k: np.asarray(v) for k, v in inputs.items()}
    T = np.transpose
    qv = z["L0_xattn_W_qv"].reshape(4, D, D)
    wg = z["L1_xattn_Wg"]
    kv3 = z["L3_xattn_Wkv"]
    by_name = {
        "Wqv1": qv[0], "Wqv2": qv[1], "Wqv3": qv[2], "Wqv4": qv[3],
        "WrT": T(z["L0_ffn_W_r"]), "WkT": T(z["L0_ffn_W_k"]), "WvT": T(z["L0_ffn_W_v"]),
        "WksT": T(z["L1_xattn_Wk_s"]), "WqsT": T(z["L1_xattn_Wq_s"]), "WvsT": T(z["L1_xattn_Wv_s"]),
        "WvcT": T(z["L1_xattn_Wv_c"]), "Wqc": z["L1_xattn_Wq_c"], "Wkc": z["L1_xattn_Wk_c"],
        "Wg1T": T(wg[:, :D]), "Wg2T": T(wg[:, D:]),
        "wq2": z["L2_xattn_w_q"], "wk2": z["L2_xattn_w_k"], "wv2": z["L2_xattn_w_v"], "wo2": z["L2_xattn_w_o"],
        "WqT3": T(z["L3_xattn_Wq"]), "WkT3": T(kv3[:D]), "WvT3": T(kv3[D:]), "WoT3": T(z["L3_xattn_Wo"]),
        "WinD": np.concatenate([z["L3_ffn_Win"]] * 2, 1), "WoutD": np.concatenate([z["L3_ffn_Wout"]] * 2, 0),
    }
    ws = z["L0_xattn_w_sim"]

    def doubled(w):
        return np.concatenate([w[:, :NH], w[:, NH:]], 0)

    bin_ = z["L3_ffn_bin_"]
    vecs = [ws[:D], ws[D:2 * D], ws[2 * D:], z["L0_ffn_mu_r"], z["L0_ffn_mu_k"], z["L1_xattn_bk_s"],
            z["L1_xattn_bq_s"], z["L1_xattn_bq_c"], z["L1_xattn_bk_c"], z["L1_xattn_bv_s"], z["L3_xattn_bq"],
            np.concatenate([bin_, bin_])]
    cols = np.concatenate([np.stack(vecs, 1), doubled(z["L3_ffn_W1"]), doubled(z["L3_ffn_b1"]),
                           doubled(z["L3_ffn_W2"])], 1)
    rows = np.concatenate([z["L0_xattn_b_qv"], z["L3_xattn_bo"], z["L3_ffn_bout"], z["L1_xattn_bv_s"],
                           z["L1_xattn_bv_c"], z["L1_xattn_bg"], z["g_xattn"], z["g_ffn"], z["L0_xattn_b_sim"]])
    const, pair = shape_constants()
    arrays = {
        "x": z["x"], "ctx": z["ctx_1024"], "ctxT": T(z["ctx_1024"], (2, 0, 1)).reshape(D, B * K),
        "mask": z["mask_Bx1xSxS2_ik1"].reshape(B, S, K), "rows": rows, "cols": cols,
        "mats": np.stack([by_name[n] for n in MATS], 1), "const": const, "pair": pair,
        "b2m": z["L3_ffn_b2"].reshape(M_IN, 1),
        "rwT": np.concatenate([T(z["L1_ffn_router_w"]), T(z["L2_ffn_gate_w"])], 1),
        "b2": z["L1_ffn_b2"],
        "w1": np.concatenate([T(z["L1_ffn_w1"], (2, 0, 1)),
                                                    T(z["L1_ffn_b1"].reshape(E, C1, P), (2, 0, 1))], 2), "w2": T(z["L1_ffn_w2"].reshape(E, D, C1, P), (3, 0, 2, 1)),
        "v13": T(z["L2_ffn_w13_weight"], (2, 0, 1)),
        "v2": T(z["L2_ffn_w2_weight"].reshape(E, D, C2, P), (3, 0, 2, 1)),
    }
    arrays = {f"in_{k}": np.ascontiguousarray(v) for k, v in arrays.items()}
    nc = bacc.Bacc("TRN2", target_bir_lowering=False, num_devices=1)
    aps = {k[3:]: nc.dram_tensor(k, v.shape, mybir.dt.from_np(v.dtype), kind="ExternalInput").ap()
           for k, v in arrays.items()}
    out = nc.dram_tensor("out", (B, S, D), F32, kind="ExternalOutput").ap()
    flamingo_program(nc, aps, out)
    res = run_bass_kernel_spmd(nc, [arrays], core_ids=[0])
    return res.results[0]["out"]
```

```python
from contextlib import ExitStack

import numpy as np

import concourse.bass as bass
from concourse import mybir

F32 = mybir.dt.float32
F32R = mybir.dt.float32r
BF16 = mybir.dt.bfloat16
I32 = mybir.dt.int32
ALU = mybir.AluOpType
ACT = mybir.ActivationFunctionType
AX = mybir.AxisListType.X

B, S, D, K = 2, 512, 128, 77
P = 128
NT = S // P
EPS = 1e-5
E = 8
F1 = 512
C1 = F1 // P
F2 = 256
C2 = F2 // P
H = 16
DH = D // H
GROUPS = 4
SPAN = H * K
CH = -(-SPAN // P)
HB = [(0, 6), (6, 12), (12, 16)]
VW = D + H
MASKED = -1e30
M_IN = 64
NH = 8

COL = {n: i for i, n in enumerate(
    ["w1", "w2", "w3", "mu_r", "mu_k", "bk_s", "bq_s", "bq_c", "bk_c", "bv_s", "bv_c", "bq3", "bin"])}
NC0 = len(COL)
C_W1, C_B1, C_W2, C_B2 = NC0, NC0 + NH, NC0 + 2 * NH, NC0 + 3 * NH
NCOL = NC0 + 3 * NH
ROW = {n: i for i, n in enumerate(["b_qv", "bo3", "bout", "bv_s", "bv_c", "bg"])}
R_G = len(ROW) * D
R_BSIM = R_G + 8
NROW = R_BSIM + 1
MAT0 = ["Wqv1", "Wqv2", "Wqv3", "Wqv4"]
MAT1 = ["WrT", "WkT", "WvT"]
MAT2 = ["WksT", "WqsT", "WvsT", "WvcT", "Wvc", "Wqc", "Wkc", "Wg1T", "Wg2T"]
MAT3 = ["wq2", "wk2", "wv2", "wo2", "WqT3", "WkT3", "WvT3", "WoT3", "WinD", "WoutD"]
MATS = MAT0 + MAT1 + MAT2 + MAT3
K_ID = 0
K_HEAD = K_ID + P
K_LT8 = K_HEAD + H
K_LT4 = K_LT8 + 64
K_REP = K_LT4 + 16
K_PAIR = K_REP + CH * P
K_INT = K_PAIR + CH * H
K_SEL = K_INT + S
NK = K_SEL + 4


def flamingo_program(nc, a, out):
    ctx = ExitStack()
    with ctx:
        def sb(name, shape, dt=F32):
            return ctx.enter_context(nc.sbuf_tensor(name, shape, dt))

        def sem(name):
            return ctx.enter_context(nc.semaphore(name))

        const = sb("const", [P, NK])
        mats = sb("mats", [P, len(MATS), P])
        cols = sb("cols", [P, NCOL])
        b2col = sb("b2col", [P, 1])
        rows = sb("rows", [P, NROW])
        ctxT = sb("ctxT", [P, B * K])
        ctxN = sb("ctxN", [K, B, D])
        mask = sb("mask", [P, B, NT, K], I32)
        rwT = sb("rwT", [P, 2 * E])
        b2E = sb("b2E", [2 * E, D])
        up_raw = [sb(f"up_raw{i}", [P, F1 + C1]) for i in range(2)]
        b1s = [sb(f"b1s{i}", [P, C1]) for i in range(2)]
        down_raw = [sb(f"down_raw{i}", [P, C1, D]) for i in range(2)]

        def mat(n):
            return mats[:, MATS.index(n), :]

        def col(n, p=P):
            return cols[0:p, COL[n]:COL[n] + 1]

        def row(n, p=P):
            return rows[0:p, ROW[n] * D:(ROW[n] + 1) * D]

        ident = const[:, K_ID:K_ID + P]
        head = const[:, K_HEAD:K_HEAD + H]

        def rep(c):
            return const[0:K, K_REP + c * P:K_REP + (c + 1) * P]

        pair = const[:, K_PAIR:K_PAIR + CH * H].rearrange("p (c h) -> p c h", h=H)
        interpT = const[0:K, K_INT:K_INT + S]

        x = [sb(f"x{b}", [P, NT, D]) for b in range(B)]
        h = [sb(f"h{b}", [P, NT, D]) for b in range(B)]
        hTz = [sb(f"hTz{b}", [P, S + 1]) for b in range(B)]
        hT = [t[:, 1:S + 1] for t in hTz]
        hhi = [sb(f"hhi{b}", [P, S], F32R) for b in range(B)]
        hlo = [sb(f"hlo{b}", [P, S], F32R) for b in range(B)]
        stats = [sb(f"stats{b}", [P, NT, 6]) for b in range(B)]
        mv = [sb(f"mv{b}", [P, NT, 2]) for b in range(B)]
        var = [sb(f"var{b}", [P, NT]) for b in range(B)]
        rstd = [sb(f"rstd{b}", [P, NT]) for b in range(B)]
        neghalf = sb("neghalf", [P, NT])
        ones = sb("ones", [P, P])
        ident_b = sb("ident_b", [P, P], BF16)
        tg = sb("tg", [P, 8])
        htg = sb("htg", [P, 8])
        tgb = sb("tgb", [P, 3, D])

        W1_ = [sb(f"wa{b}", [P, S]) for b in range(B)]
        W2_ = [sb(f"wb{b}", [P, S]) for b in range(B)]
        W3_ = [sb(f"wc{b}", [P, S]) for b in range(B)]
        W4_ = [sb(f"wd{b}", [P, S]) for b in range(B)]
        small = [sb(f"small{b}", [P, 64]) for b in range(B)]

        simR = sb("simR", [P, B * K])
        simrow = sb("simrow", [1, B * K])
        ctxW2 = sb("ctxW2", [K, B, D])
        w14 = [sb(f"w14_{b}", [P, D]) for b in range(B)]
        KsT = sb("KsT", [P, B * K])
        QsT = sb("QsT", [P, B * K])
        VsT = sb("VsT", [P, B * K])
        Mq = sb("Mq", [P, B * K])
        Mk = sb("Mk", [P, B * K])
        qrow = sb("qrow", [1, B * K])
        kshift = sb("kshift", [K, B])
        Vs = sb("Vs", [K, B, D])
        VsG = sb("VsG", [K, B, D])
        intV = [sb(f"intV{b}", [K, 2, D]) for b in range(B)]
        AhT = [sb(f"AhT{b}", [P, K]) for b in range(B)]
        WvG = sb("WvG", [P, 2, D])
        bvB = sb("bvB", [P, K])
        vcrow = sb("vcrow", [K, 2, D])

        lg = [sb(f"lg{b}", [P, NT, E]) for b in range(B)]
        ex = [sb(f"ex{b}", [P, NT, E]) for b in range(B)]
        gt = [sb(f"gt{b}", [P, NT, E, E]) for b in range(B)]
        eq = [sb(f"eq{b}", [P, NT, E, E]) for b in range(B)]
        c2 = [sb(f"c2_{b}", [P, NT, 2 * E], F32R) for b in range(B)]
        cT = sb("cT", [2 * E, B * S], F32R)
        cflat = sb("cflat", [4 * B, E // 2, S], F32R)
        sel = sb("sel", [4 * B, 4, P], F32R)
        shared = sb("shared", [P, 2 * CH * P])
        PT = [shared[:, i * CH * P:(i + 1) * CH * P] for i in range(2)]
        ring = [shared[:, i * S:(i + 1) * S] for i in range(4)]
        ysb, acc = W1_, W2_
        rhi = [sb(f"rhi{i}", [P, S], F32R) for i in range(4)]
        rlo = [sb(f"rlo{i}", [P, S], F32R) for i in range(4)]
        wuh = [sb(f"wuh{i}", [P, F1], F32R) for i in range(2)]
        wul = [sb(f"wul{i}", [P, F1], F32R) for i in range(2)]
        wdh = [sb(f"wdh{i}", [P, C1, D], F32R) for i in range(2)]
        wdl = [sb(f"wdl{i}", [P, C1, D], F32R) for i in range(2)]

        nb = sb("nb", [P, B, NT, K], BF16)
        kT = sb("kT", [P, B * K])
        kTh = sb("kTh", [P, B * K], F32R)
        kTl = sb("kTl", [P, B * K])
        kbh = [sb(f"kbh{b}", [P, H, K], F32R) for b in range(B)]
        kbl = [sb(f"kbl{b}", [P, H, K], F32R) for b in range(B)]
        vN = sb("vN", [K, B, D])
        vbd = [sb(f"vbd{b}", [P, CH, VW]) for b in range(B)]
        Sx = [sb(f"Sx{i}", [P, CH * P]) for i in range(2)]
        qh, ql = hhi, hlo

        bank = [ctx.enter_context(nc.psum_tensor(f"bank{i}", [P, 512], F32)) for i in range(8)]

        ld = {n: sem(f"ld_{n}") for n in
              ["x0", "x1", "first", "ctx", "l0", "l1", "l2", "l3", "mask", "const", "moe1", "pair", "b2m"]}
        raw_in = [sem(f"raw_in{i}") for i in range(2)]
        out_done = sem("out_done")
        dve_step, pool_step = sem("dve_step"), sem("pool_step")
        ready_const = sem("ready_const")
        ln_var, ln_rstd, ln_h, ln_T, hT_ready = [sem(n) for n in ("ln_var", "ln_rstd", "ln_h", "ln_T", "hT_ready")]
        x_biased, resid = sem("x_biased"), sem("resid")
        gates = sem("gates")
        tgb_ready = sem("tgb_ready")
        p0_dve, p0_pe, p0_act = sem("p0_dve"), sem("p0_pe"), sem("p0_act")
        p2_pe, p2_act, p2_dve = sem("p2_pe"), sem("p2_act"), sem("p2_dve")
        l0 = {n: sem(f"l0_{n}") for n in
              ["S", "m", "sub", "exp", "P", "PT", "PTs", "hq", "u", "m1", "nM", "e", "hc", "W", "out"]}
        l1 = {n: sem(f"l1_{n}") for n in ["x", "k", "r", "kr", "rt", "ka", "v"]}
        l2 = {n: sem(f"l2_{n}") for n in
              ["S", "s2", "sub", "exp", "shift2", "exp2", "P", "PT", "PTs", "P2T", "P2Ts", "ah", "ahs", "s2c",
               "s2cs", "c2s", "s2ci", "z", "t", "sc"]}
        m = {n: sem(f"m_{n}") for n in
             ["split", "lg", "sub", "exp", "c", "cT", "cTs", "flat", "b2", "acc0", "zero", "outN"]}
        q = {n: sem(f"q_{n}") for n in
             ["h", "gelu", "hiA", "hiD", "loD", "loP", "free", "wh", "wl", "ys", "row", "mult", "add"]}
        r = {n: sem(f"r_{n}") for n in
             ["g", "silu", "mul", "hi", "loD", "loP", "free", "wh", "wl", "ys", "row", "mult", "add"]}
        kv = {n: sem(f"kv_{n}") for n in ["pe", "act", "pool", "rep", "reps", "bd", "hi"]}
        at = {n: sem(f"at_{n}") for n in
              ["q", "qhi", "qlo", "S", "sub", "exp", "T", "PT", "O", "norm", "OT", "OTs", "out"]}
        l3 = {n: sem(f"l3_{n}") for n in ["s", "ss", "u", "acc", "out"]}
        nb_ready = sem("nb_ready")

        block = ctx.enter_context(nc.Block())

        def tile(ap, t):
            return ap[:, t * P:(t + 1) * P]

        def over_tiles(ap):
            return ap.unsqueeze(1).broadcast_to([P, NT, D])

        def wait_positive(eng, semaphore, value):
            if not isinstance(value, int) or value > 0:
                eng.wait_ge(semaphore, value)

        def i_is(i, value):
            return isinstance(i, int) and i == value

        def before(members, n):
            return sum(j in members for j in range(n))

        CH1 = [(p, b, c) for p in range(2) for b in range(B) for c in range(C1)]
        CH2 = [(p, b, c) for p in range(2) for b in range(B) for c in range(C2)]
        N1, N2 = len(CH1), len(CH2)
        LAG1, LAG2 = 3, 2
        PASSES = E // 2
        G1, G2 = N1 // C1, N2 // C2
        LO_POOL1 = {n for n in range(N1) if n % 4 == 2}
        HI_ACT1 = {n for n in range(N1) if n % 4 == 1}
        LO_POOL2 = {1, 4, 6}
        ALL1, ALL2 = set(range(N1)), set(range(N2))
        HI_DVE1, LO_DVE1, LO_DVE2 = ALL1 - HI_ACT1, ALL1 - LO_POOL1, ALL2 - LO_POOL2
        BANKS1 = [1, 2, 3, 7]
        BANKG, BANKU = [1, 2], [3, 7]
        BANKC = [5, 6]
        BANKV = {(0, 0): (5, 2, 6), (0, 1): (2, 6, 3), (1, 0): (7, 5, 6), (1, 1): (3, 7, 5)}

        @block.sync
        def _(sp):
            M0, M1 = len(MAT0), len(MAT0 + MAT1)
            M2 = M1 + len(MAT2)
            for b in range(B):
                sp.dma_start(x[b][:, :, :], a["x"][b].rearrange("(t p) d -> p t d", p=P)).then_inc(ld[f"x{b}"], 16)
            sp.dma_start(rows[:, :], a["rows"].partition_broadcast(P)).then_inc(ld["first"], 16)
            sp.dma_start(mats[:, 0:M0, :], a["mats"][:, 0:M0, :]).then_inc(ld["l0"], 16)
            sp.dma_start(mats[:, M1:M2, :], a["mats"][:, M1:M2, :]).then_inc(ld["l2"], 16)
            sp.dma_start(mats[:, M0:M1, :], a["mats"][:, M0:M1, :]).then_inc(ld["l1"], 16)
            sp.dma_start(mats[:, M2:, :], a["mats"][:, M2:, :]).then_inc(ld["l3"], 16)
            sp.dma_start(rwT[:, :], a["rwT"]).then_inc(ld["moe1"], 16)
            for p in range(2):
                for j in range(2):
                    r0 = (2 * p + j) * (E // 2)
                    sp.dma_start(b2E[r0:r0 + E // 2, :],
                                 a["b2"].rearrange("(i p) d -> p i d", p=2)[p]).then_inc(ld["moe1"], 16)
            def load_expert(up, down, nd, e, p):
                sp.dma_start(up_raw[p][:, 0:a[up].shape[2]], a[up][:, e, :]).then_inc(raw_in[p], 16)
                sp.dma_start(down_raw[p][:, 0:nd, :], a[down][:, e, :, :]).then_inc(raw_in[p], 16)

            for p in range(2):
                load_expert("w1", "w2", C1, p, p)
            sp.wait_ge(ready_const, 1)
            sp.dma_start(b2col[0:M_IN, :], a["b2m"]).then_inc(ld["b2m"], 16)

            def flatten(n):
                for b in range(B):
                    sp.wait_ge(m["cTs"], B * n + b + 1)
                    sp.dma_start(cflat[4 * b:4 * b + 4, :, :].bitcast(F32), cT[:, b * S:(b + 1) * S].bitcast(F32)).then_inc(m["flat"], 16)

            flatten(0)
            with sp.Fori(0, PASSES - 1) as i:
                for p in range(2):
                    sp.wait_ge(q["wl"], 2 * i + p + 1)
                    load_expert("w1", "w2", C1, 2 * i + 2 + p, p)
            for p in range(2):
                sp.wait_ge(q["wl"], E - 1 + p)
                load_expert("v13", "v2", C2, p, p)
            flatten(1)
            with sp.Fori(0, PASSES - 1) as i:
                for p in range(2):
                    sp.wait_ge(r["wl"], 2 * i + p + 1)
                    load_expert("v13", "v2", C2, 2 * i + 2 + p, p)
            for b in range(B):
                sp.wait_ge(resid, 2 * 7 + b + 1)
                sp.dma_start(out[b].rearrange("(t p) d -> p t d", p=P), x[b][:, :, :]).then_inc(out_done, 16)
            sp.wait_ge(out_done, 16 * B)

        @block.gpsimd
        def _(pool):
            pool.dma_start(const[:, :], a["const"]).then_inc(ld["const"], 16)
            pool.dma_start(mask[:, :, :, :], a["mask"].rearrange("b (t p) k -> p b t k", p=P)).then_inc(ld["mask"], 16)
            nc.gpsimd.memset(neghalf[:, :], -0.5)
            nc.gpsimd.memset(ones[:, :], 1.0)
            for b in range(B):
                nc.gpsimd.memset(hTz[b][:, 0:1], 0.0)
            for i in range(2):
                nc.gpsimd.memset(Sx[i][:, SPAN:], 0.0)
            nc.gpsimd.memset(b2col[:, :], 0.0).then_inc(ready_const, 1)
            pool.wait_ge(ready_const, 1)
            steps = [0]

            def link(ins):
                steps[0] += 1
                ins.then_inc(pool_step, 1)
                pool.wait_ge(pool_step, steps[0])

            def norm(k):
                b = k % B
                pool.wait_ge(ln_var, k + 1)
                nc.gpsimd.tensor_tensor(rstd[b][:, :], var[b][:, :], neghalf[:, :], ALU.pow).then_inc(ln_rstd, 1)

            def add_bias(n, b):
                pool.wait_ge(ln_h, 2 * [0, 6, 7][n] + b + 1)
                pool.wait_ge(tgb_ready, 1)
                nc.gpsimd.tensor_tensor(x[b][:, :, :], x[b][:, :, :], over_tiles(tgb[:, n, :]),
                                        ALU.add).then_inc(x_biased, 1)

            def key(b, part):
                dst, src = ((kbh, kTh[:, b * K:(b + 1) * K].bitcast(F32)), (kbl, kTl[:, b * K:(b + 1) * K]))[part]
                nc.gpsimd.tensor_tensor(dst[b][:, :, :], src.unsqueeze(1).broadcast_to([P, H, K]),
                                        head.unsqueeze(2).broadcast_to([P, H, K]), ALU.mult).then_inc(kv["pool"], 1)

            def mask_values(n, b):
                pool.wait_ge(kv["reps"], 3 * (2 * n + b + 1))
                v = vbd[b][:, :, 0:D].rearrange("p c (h e) -> p c h e", e=DH)
                nc.gpsimd.tensor_tensor(v, v, pair.unsqueeze(3).broadcast_to([P, CH, H, DH]),
                                        ALU.mult).then_inc(kv["bd"], 1)

            for k in range(2):
                norm(k)
            for b in range(B):
                add_bias(0, b)
            for b in range(B):
                pool.wait_ge(l0["m1"], b + 1)
                link(nc.gpsimd.partition_all_reduce(small[b][:, 5:6], small[b][:, 4:5], P, bass.bass_isa.ReduceOp.max))
                nc.gpsimd.tensor_scalar(small[b][:, 6:7], small[b][:, 5:6], -1.0, 0.0, ALU.mult,
                                        ALU.add).then_inc(l0["nM"], 1)
            for k in range(2, 6):
                norm(k)
            pool.wait_ge(ld["const"], 16)
            pool.wait_ge(kv["hi"], 1)
            for b in range(B):
                for part in range(2):
                    key(b, part)
            mask_values(0, 0)
            for k in range(6, 8):
                norm(k)

            def split(i, p, nd, wh, wl):
                pool.wait_ge(wh, 2 * i + p + 1)
                nc.gpsimd.tensor_tensor(wul[p][:, :], up_raw[p][:, 0:F1], wuh[p][:, :].bitcast(F32), ALU.subtract)
                nc.gpsimd.tensor_tensor(wdl[p][:, 0:nd, :], down_raw[p][:, 0:nd, :],
                                        wdh[p][:, 0:nd, :].bitcast(F32), ALU.subtract).then_inc(wl, 1)

            def low(n, hi, count, lo):
                pool.wait_ge(hi, count)
                nc.gpsimd.tensor_tensor(rlo[n % 4][:, :], ring[n % 4][:, :], rhi[n % 4][:, :].bitcast(F32),
                                        ALU.subtract).then_inc(lo, 1)

            def add(i, j, groups, mult, done):
                G, b = groups * i + j, j % B
                if isinstance(G, int) and G < 0:
                    return
                pool.wait_ge(mult, G + 1)
                wait_positive(pool, done, G - 1)
                nc.gpsimd.tensor_tensor(acc[b][:, :], acc[b][:, :], ysb[b][:, :], ALU.add).then_inc(done, 1)

            def body1(i, last):
                for n in range(N1):
                    if n == 3:
                        split(i, 1, C1, q["wh"], q["wl"])
                    if n == 3 + N1 // 2 and not last:
                        split(i + 1, 0, C1, q["wh"], q["wl"])
                    if n in LO_POOL1:
                        low(n, q["hiD"], len(HI_DVE1) * i + before(HI_DVE1, n + 1), q["loP"])
                    if i_is(i, 0) and n == 11:
                        pool.wait_ge(m["acc0"], B)
                    if n % 4 == 3:
                        add(i, (n - 3) // 4 - 2, G1, q["mult"], q["add"])

            split(0, 0, C1, q["wh"], q["wl"])
            mask_values(0, 1)
            body1(0, False)
            with pool.Fori(1, PASSES - 1) as i:
                body1(i, False)
            body1(PASSES - 1, True)
            for j in range(G1 - B, G1):
                add(PASSES - 1, j, G1, q["mult"], q["add"])

            for k in range(8, 12):
                norm(k)
            for b in range(B):
                nc.gpsimd.memset(acc[b][:, :], 0.0).then_inc(m["zero"], 1)
            split(0, 0, C2, r["wh"], r["wl"])
            pool.wait_ge(kv["hi"], 2)
            pool.wait_ge(at["S"], 3 * NT * B)
            key(0, 0)
            mask_values(1, 0)
            pool.wait_ge(m["zero"], B)

            def body2(i, last):
                for n in range(N2):
                    if n == 2:
                        split(i, 1, C2, r["wh"], r["wl"])
                    if n == 2 + N2 // 2 and not last:
                        split(i + 1, 0, C2, r["wh"], r["wl"])
                    if n in LO_POOL2:
                        low(n, r["hi"], N2 * i + n + 1, r["loP"])
                    if n % 2 == 1:
                        add(i, (n - 1) // 2 - 2, G2, r["mult"], r["add"])
                    if i_is(i, 0) and n == 4:
                        key(0, 1)
                    if last and n == 3:
                        key(1, 0)
                    if last and n == 6:
                        key(1, 1)

            body2(0, False)
            with pool.Fori(1, PASSES - 1) as i:
                body2(i, False)
            body2(PASSES - 1, True)
            for j in range(G2 - B, G2):
                add(PASSES - 1, j, G2, r["mult"], r["add"])
            for k in range(12, 14):
                norm(k)
            mask_values(1, 1)
            for b in range(B):
                add_bias(1, b)
            for k in range(14, 16):
                norm(k)
            for b in range(B):
                add_bias(2, b)

        @block.scalar
        def _(act):
            act.dma_start(cols[:, :], a["cols"]).then_inc(ld["ctx"], 16)
            act.dma_start(ctxT[:, :], a["ctxT"]).then_inc(ld["ctx"], 16)
            act.dma_start(ctxN[:, :, :], a["ctx"].rearrange("b k d -> k b d")).then_inc(ld["ctx"], 16)
            for b in range(B):
                act.dma_start(vbd[b][:, :, D:VW], a["pair"]).then_inc(ld["pair"], 16)

            def transposed(k):
                b = k % B
                act.wait_ge(ln_T, k + 1)
                nc.scalar.activation(hT[b], bank[4 * b][:, :], ACT.Copy).then_inc(hT_ready, 1)

            def values(n):
                act.wait_ge(kv["pe"], n + 1)
                bk, bv = ((2, 3), (5, 6))[n]
                if n == 1:
                    act.wait_ge(kv["hi"], 1)
                    act.wait_ge(kv["rep"], 6)
                nc.scalar.activation(kT[:, :], bank[bk][:, 0:B * K], ACT.Copy, scale=float(DH) ** -0.5)
                nc.scalar.activation(vN[:, :, :], bank[bv][0:K, 0:B * D], ACT.Copy).then_inc(kv["act"], 1)

            def replicated(n, b):
                for j, bk in enumerate(BANKV[n, b]):
                    c0, c1 = 4 * j, min(4 * j + 4, CH)
                    act.wait_ge(kv["rep"], 3 * (2 * n + b) + j + 1)
                    nc.scalar.activation(vbd[b][:, c0:c1, 0:D],
                                         bank[bk][:, 0:(c1 - c0) * P].rearrange("p (c d) -> p c d", d=D),
                                         ACT.Copy).then_inc(kv["reps"], 1)

            act.wait_ge(ld["first"], 16)
            nc.scalar.activation(tg[:, :], rows[:, R_G:R_G + 8], ACT.Tanh).then_inc(gates, 1)
            act.wait_ge(p0_pe, 1)
            nc.scalar.activation(simrow[:, :], bank[1][0:1, 0:B * K], ACT.Identity,
                                 bias=rows[0:1, R_BSIM:R_BSIM + 1])
            nc.scalar.activation(ctxW2[:, :, :], bank[2][0:K, 0:B * D], ACT.Copy).then_inc(p0_act, 1)
            act.wait_ge(p2_pe, 1)
            nc.scalar.activation(KsT[:, :], bank[3][:, 0:B * K], ACT.Identity, bias=col("bk_s"))
            nc.scalar.activation(QsT[:, :], bank[3][:, B * K:2 * B * K], ACT.Identity, bias=col("bq_s"))
            nc.scalar.activation(VsT[:, :], bank[6][:, 0:B * K], ACT.Identity, bias=col("bv_s")).then_inc(p2_act, 1)
            act.wait_ge(p2_pe, 2)
            sc = float(D) ** -0.5
            nc.scalar.activation(Mq[:, :], bank[7][:, 0:B * K], ACT.Copy, scale=sc)
            nc.scalar.activation(Mk[:, :], bank[7][:, B * K:2 * B * K], ACT.Copy, scale=sc)
            nc.scalar.activation(WvG[:, 1, :], bank[6][:, 256:384], ACT.Copy)
            nc.scalar.activation(vcrow[:, 1, :], bank[6][0:K, 384:512], ACT.Copy)
            nc.scalar.activation(qrow[:, :], bank[1][0:1, B * K:2 * B * K], ACT.Copy, scale=sc)
            nc.scalar.activation(kshift[:, :], bank[2][0:K, 256:256 + B], ACT.Copy, scale=sc).then_inc(p2_act, 1)

            for b in range(B):
                transposed(b)
            for b in range(B):
                act.wait_ge(l0["sub"], b + 1)
                nc.scalar.activation(W1_[b][:, 0:NT * K], W1_[b][:, 0:NT * K], ACT.Exp).then_inc(l0["exp"], 1)
            for b in range(B):
                act.wait_ge(l0["nM"], b + 1)
                nc.scalar.activation(small[b][:, 8:12], small[b][:, 0:4], ACT.Exp, bias=small[b][:, 6:7],
                                     accum_out=small[b][:, 12:13]).then_inc(l0["e"], 1)
            for b in range(B):
                act.wait_ge(l0["PT"], b + 1)
                nc.scalar.activation(W2_[b][0:K, :], bank[4 * b + 2][0:K, :], ACT.Copy).then_inc(l0["PTs"], 1)
            values(0)

            for b in range(B):
                transposed(2 + b)
            for b in range(B):
                act.wait_ge(l1["k"], b + 1)
                nc.scalar.activation(W3_[b][:, :], bank[4 * b + 1][:, :], ACT.Relu).then_inc(l1["kr"], 1)
                act.wait_ge(l1["r"], b + 1)
                nc.scalar.activation(W4_[b][:, :], bank[4 * b + 2][:, :], ACT.Tanh, scale=0.5).then_inc(l1["rt"], 1)
            replicated(0, 0)

            for b in range(B):
                transposed(4 + b)
            for b in range(B):
                act.wait_ge(l2["shift2"], b + 1)
                nc.scalar.activation(W2_[b][0:K, :], bank[4 * b + 2][0:K, :], ACT.Exp, bias=small[b][0:K, 22:23],
                                     accum_out=small[b][0:K, 23:24]).then_inc(l2["exp2"], 1)
            for b in range(B):
                act.wait_ge(l2["sub"], b + 1)
                nc.scalar.activation(W1_[b][:, 0:NT * K], W1_[b][:, 0:NT * K], ACT.Exp).then_inc(l2["exp"], 1)
            for b in range(B):
                act.wait_ge(l2["P2T"], b + 1)
                nc.scalar.activation(W4_[b][:, 0:NT * K], bank[4 * b][:, 0:NT * K], ACT.Copy).then_inc(l2["P2Ts"], 1)
            for b in range(B):
                act.wait_ge(l2["PT"], b + 1)
                nc.scalar.activation(W3_[b][0:K, :], bank[4 * b + 3][0:K, :], ACT.Copy).then_inc(l2["PTs"], 1)
            for b in range(B):
                act.wait_ge(l2["ah"], b + 1)
                nc.scalar.activation(AhT[b][:, :], bank[4 * b + 2][:, 0:K], ACT.Copy).then_inc(l2["ahs"], 1)
            for b in range(B):
                act.wait_ge(l2["s2ci"], b + 1)
                nc.scalar.activation(W2_[b][:, :], bank[4 * b + 3][:, :], ACT.Copy).then_inc(l2["sc"], 1)
                act.wait_ge(l2["z"], b + 1)
                nc.scalar.activation(W1_[b][:, :], bank[4 * b][:, :], ACT.Tanh, scale=0.5).then_inc(l2["t"], 1)
            replicated(0, 1)

            def exponentials(n):
                for b in range(B):
                    act.wait_ge(m["sub"], 2 * n + b + 1)
                    nc.scalar.activation(ex[b][:, :, :], lg[b][:, :, :], ACT.Exp).then_inc(m["exp"], 1)

            def weights_T(n, b):
                act.wait_ge(m["cT"], 2 * n + b + 1)
                nc.scalar.activation(cT[:, b * S:(b + 1) * S], bank[BANKC[b]][0:2 * E, :],
                                     ACT.Copy).then_inc(m["cTs"], 1)

            for b in range(B):
                transposed(6 + b)
            exponentials(0)

            def slot_hi(i, p, first, nd, ready, free_at, slot_free):
                act.wait_ge(raw_in[p], 32 * (first + i + 1))
                wait_positive(act, slot_free, free_at)
                nc.scalar.activation(wuh[p][:, :], up_raw[p][:, 0:F1], ACT.Copy)
                if first == 0:
                    nc.scalar.activation(b1s[p][:, :], up_raw[p][:, F1:F1 + C1], ACT.Copy)
                nc.scalar.activation(wdh[p][:, 0:nd, :], down_raw[p][:, 0:nd, :], ACT.Copy).then_inc(ready, 1)

            def output(i, j, groups, chunks, free, added, done):
                G, b = groups * i + j, j % B
                if isinstance(G, int) and G < 0:
                    return
                act.wait_ge(free, chunks * (G + 1))
                wait_positive(act, added, G - 1)
                nc.scalar.activation(ysb[b][:, :], bank[4 * b][:, :], ACT.Copy).then_inc(done, 1)

            def split1(i, p):
                slot_hi(i, p, 0, C1, q["wh"], N1 * i + N1 // 2 * p - N1 // 2, q["free"])

            def body1(i, last):
                for n, (p, b, c) in enumerate(CH1):
                    g = N1 * i + n
                    if n == 3:
                        split1(i, 1)
                    if n == 3 + N1 // 2 and not last:
                        split1(i + 1, 0)
                    act.wait_ge(q["h"], g + 1)
                    nc.scalar.activation(ring[n % 4][:, :], bank[BANKS1[n % 4]][:, :], ACT.Gelu,
                                         bias=b1s[p][:, c:c + 1]).then_inc(q["gelu"], 1)
                    if n in HI_ACT1:
                        act.wait_ge(q["gelu"], g + 1)
                        nc.scalar.activation(rhi[n % 4][:, :], ring[n % 4][:, :], ACT.Copy).then_inc(q["hiA"], 1)
                    if i_is(i, 0) and n in (5, 7):
                        weights_T(0, (n - 5) // 2)
                    if i_is(i, 0) and n == 8:
                        for b0 in range(B):
                            act.wait_ge(m["b2"], b0 + 1)
                            nc.scalar.activation(acc[b0][:, :], bank[BANKC[b0]][:, :],
                                                 ACT.Copy).then_inc(m["acc0"], 1)
                    if n % 4 == 2:
                        output(i, (n - 2) // 4 - 1, G1, C1, q["free"], q["add"], q["ys"])

            act.wait_ge(ld["moe1"], 80)
            split1(0, 0)
            body1(0, False)
            with act.Fori(1, PASSES - 1) as i:
                body1(i, False)
            body1(PASSES - 1, True)
            output(PASSES - 1, G1 - 1, G1, C1, q["free"], q["add"], q["ys"])

            def attend(n):
                base = [8, 12][n]
                for b in range(B):
                    transposed(base + b)
                for b in range(B):
                    act.wait_ge(at["q"], 2 * n + b + 1)
                    if n == 0:
                        nc.scalar.activation(qh[b][:, :], bank[4 * b][:, :], ACT.Copy).then_inc(at["qhi"], 1)
                    else:
                        nc.scalar.activation(qh[b][:, :], bank[4 * b][:, :], ACT.Identity,
                                             bias=col("bq3")).then_inc(at["qhi"], 1)
                for u in range(NT * B):
                    T = NT * B * n + u
                    act.wait_ge(at["sub"], 3 * (T + 1))
                    nc.scalar.activation(Sx[T % 2][:, 0:SPAN], Sx[T % 2][:, 0:SPAN], ACT.Exp).then_inc(at["exp"], 1)
                    if T >= 2:
                        act.wait_ge(at["O"], T - 1)
                    for j, w in enumerate((512, 512, 256)):
                        act.wait_ge(at["T"], 3 * T + j + 1)
                        nc.scalar.activation(PT[T % 2][:, 512 * j:512 * j + w], bank[5 + j][:, 0:w],
                                             ACT.Copy).then_inc(at["PT"], 1)
                for b in range(B):
                    act.wait_ge(at["OT"], 2 * n + b + 1)
                    nc.scalar.activation(W2_[b][:, :], bank[(1, 3)[b]][:, :], ACT.Copy).then_inc(at["OTs"], 1)
                    if n == 0 and b == 0:
                        values(1)

            attend(0)
            for b in range(B):
                replicated(1, b)
            for b in range(B):
                transposed(10 + b)
            exponentials(1)

            def split2(i, p):
                slot_hi(i, p, PASSES, C2, r["wh"], N2 * i + N2 // 2 * p - N2 // 2, r["free"])

            def body2(i, last):
                for n, (p, b, c) in enumerate(CH2):
                    g = N2 * i + n
                    if n == 2:
                        split2(i, 1)
                    if n == 2 + N2 // 2 and not last:
                        split2(i + 1, 0)
                    act.wait_ge(r["g"], g + 1)
                    nc.scalar.activation(ring[n % 4][:, :], bank[BANKG[n % 2]][:, :], ACT.Silu).then_inc(r["silu"], 1)
                    if i_is(i, 0) and n in (3, 4):
                        weights_T(1, n - 3)
                    if n % 2 == 1:
                        output(i, (n - 1) // 2 - 1, G2, C2, r["free"], r["add"], r["ys"])

            split2(0, 0)
            body2(0, False)
            with act.Fori(1, PASSES - 1) as i:
                body2(i, False)
            body2(PASSES - 1, True)
            output(PASSES - 1, G2 - 1, G2, C2, r["free"], r["add"], r["ys"])
            attend(1)

            for b in range(B):
                transposed(14 + b)
                act.wait_ge(l3["s"], b + 1)
                nc.scalar.activation(W1_[b][:, :], bank[4 * b + 3][:, :], ACT.Identity,
                                     bias=col("bin")).then_inc(l3["ss"], 1)
                act.wait_ge(l3["ss"], b + 1)
                for i in range(NH):
                    n = NH * b + i
                    if n >= 4:
                        act.wait_ge(l3["acc"], n - 3)
                    nc.scalar.activation(ring[n % 4][:, :], W1_[b][:, :], ACT.Relu,
                                         scale=cols[:, C_W1 + i:C_W1 + i + 1],
                                         bias=cols[:, C_B1 + i:C_B1 + i + 1]).then_inc(l3["u"], 1)

        @block.vector
        def _(dve):
            steps = [0]
            V = nc.vector

            def link(ins):
                steps[0] += 1
                ins.then_inc(dve_step, 1)
                dve.wait_ge(dve_step, steps[0])

            def statistics(k):
                b = k % B
                for t in range(NT):
                    last = V.bn_stats(stats[b][:, t, :], x[b][:, t, :])
                link(last)
                for t in range(NT):
                    last = V.bn_aggr(mv[b][:, t, :], stats[b][:, t, :])
                link(last)
                V.tensor_scalar(var[b][:, :], mv[b][:, :, 1], EPS, None, ALU.add).then_inc(ln_var, 1)

            def normalised(k):
                b = k % B
                dve.wait_ge(ln_rstd, k + 1)
                for t in range(NT):
                    last = V.tensor_scalar(h[b][:, t, :], x[b][:, t, :], mv[b][:, t, 0:1], rstd[b][:, t:t + 1],
                                           ALU.subtract, ALU.mult)
                last.then_inc(ln_h, 1)

            def update(k, psum, gate):
                b = k % B
                V.scalar_tensor_tensor(x[b][:, :, :], psum, gate, x[b][:, :, :], ALU.mult, ALU.add).then_inc(resid, 1)
                dve.wait_ge(resid, k + 1)
                if k + 2 < 16:
                    statistics(k + 2)
                    normalised(k + 2)

            def tiles3(ap, w=K):
                return ap.rearrange("p (t k) -> p t k", k=w)

            def by_tile(ap):
                return ap.rearrange("p (t d) -> p t d", d=D)

            for b in range(B):
                dve.wait_ge(ld[f"x{b}"], 16)
                statistics(b)
            for b in range(B):
                normalised(b)
            dve.wait_ge(ld["ctx"], 48)
            V.tensor_scalar(simR[:, :], ctxT[:, :], col("w3"), col("w1"), ALU.mult, ALU.add).then_inc(p0_dve, 1)
            dve.wait_ge(ready_const, 1)
            V.tensor_scalar(bvB[:, :], ones[:, 0:K], col("bv_c"), None, ALU.mult).then_inc(p0_dve, 1)
            dve.wait_ge(gates, 1)
            V.tensor_scalar(htg[:, :], tg[:, :], 0.5, None, ALU.mult)
            for n, (name, g) in enumerate((("b_qv", 0), ("bo3", 3), ("bout", 7))):
                last = V.tensor_scalar(tgb[:, n, :], row(name), tg[:, g:g + 1], None, ALU.mult)
            last.then_inc(tgb_ready, 1)
            V.tensor_copy(vcrow[:, 0, :], row("bv_c", K))
            dve.wait_ge(ld["const"], 16)
            V.tensor_copy(ident_b[:, :], ident)
            V.tensor_copy(sel[:, :, :], const[0:4 * B, K_SEL:K_SEL + 4].unsqueeze(2).broadcast_to([4 * B, 4, P]))
            dve.wait_ge(ld["l2"], 16)
            V.tensor_copy(WvG[:, 0, :], mat("WvcT"))
            dve.wait_ge(p2_pe, 1)
            V.tensor_tensor(Vs[:, :, :], bank[5][0:K, 0:B * D].rearrange("k (b d) -> k b d", b=B),
                            row("bv_s", K).unsqueeze(1).broadcast_to([K, B, D]), ALU.add).then_inc(p2_dve, 1)
            dve.wait_ge(p2_pe, 2)
            V.tensor_tensor(VsG[:, :, :], bank[5][0:K, B * D:2 * B * D].rearrange("k (b d) -> k b d", b=B),
                            row("bg", K).unsqueeze(1).broadcast_to([K, B, D]), ALU.add).then_inc(p2_dve, 1)

            def softmax_in(b, S_sem, sub_sem, maxcol):
                dve.wait_ge(S_sem, b + 1)
                sc = tiles3(bank[4 * b + 1][:, 0:NT * K])
                link(V.reduce_max(small[b][:, maxcol:maxcol + NT], sc, AX))
                V.tensor_tensor(tiles3(W1_[b][:, 0:NT * K]), sc,
                                small[b][:, maxcol:maxcol + NT].unsqueeze(2).broadcast_to([P, NT, K]),
                                ALU.subtract).then_inc(sub_sem, 1)

            def softmax_out(b, exp_sem, P_sem, sumcol):
                dve.wait_ge(exp_sem, b + 1)
                pr = tiles3(W1_[b][:, 0:NT * K])
                link(V.reduce_sum(small[b][:, sumcol:sumcol + NT], pr, AX))
                link(V.reciprocal(small[b][:, sumcol + NT:sumcol + 2 * NT], small[b][:, sumcol:sumcol + NT]))
                V.tensor_tensor(pr, pr, small[b][:, sumcol + NT:sumcol + 2 * NT].unsqueeze(2).broadcast_to([P, NT, K]),
                                ALU.mult).then_inc(P_sem, 1)

            for b in range(B):
                softmax_in(b, l0["S"], l0["sub"], 0)
                V.reduce_max(small[b][:, 4:5], small[b][:, 0:NT], AX).then_inc(l0["m1"], 1)
            for b in range(B):
                softmax_out(b, l0["exp"], l0["P"], 24)
            for b in range(B):
                dve.wait_ge(l0["hc"], b + 1)
                link(V.reciprocal(small[b][:, 14:15], bank[4 * b][:, 1:2]))
                link(V.tensor_tensor(small[b][:, 15:16], bank[4 * b][:, 0:1], small[b][:, 14:15], ALU.mult))
                V.scalar_tensor_tensor(w14[b][:, :], mat("Wqv4"), small[b][:, 15:16], mat("Wqv1"),
                                       ALU.mult, ALU.add).then_inc(l0["W"], 1)
                dve.wait_ge(l0["hq"], b + 1)
                dve.wait_ge(hT_ready, b + 1)
                V.tensor_tensor(W3_[b][:, :], hT[b], bank[4 * b + 3][:, :], ALU.mult).then_inc(l0["u"], 1)
            dve.wait_ge(ld["mask"], 16)
            V.tensor_scalar(nb[:, :, :, :], mask[:, :, :, :], 0.0, MASKED, ALU.is_equal, ALU.mult).then_inc(nb_ready, 1)
            for b in range(B):
                dve.wait_ge(l0["out"], b + 1)
                dve.wait_ge(x_biased, b + 1)
                update(b, by_tile(bank[4 * b + 1][:, :]), tg[:, 0:1])

            def keys(n):
                dve.wait_ge(kv["act"], n + 1)
                if n == 1:
                    dve.wait_ge(kv["pool"], 4)
                link(V.tensor_copy(kTh[:, :], kT[:, :]))
                V.tensor_tensor(kTl[:, :], kT[:, :], kTh[:, :].bitcast(F32), ALU.subtract).then_inc(kv["hi"], 1)

            for b in range(B):
                dve.wait_ge(hT_ready, 2 + b + 1)
                link(V.tensor_tensor(W1_[b][:, :], hTz[b][:, 1:S + 1], hTz[b][:, 0:S], ALU.subtract))
                V.scalar_tensor_tensor(W2_[b][:, :], W1_[b][:, :], col("mu_k"), hTz[b][:, 0:S], ALU.mult,
                                       ALU.add).then_inc(l1["x"], 1)
                V.scalar_tensor_tensor(W4_[b][:, :], W1_[b][:, :], col("mu_r"), hTz[b][:, 0:S], ALU.mult,
                                       ALU.add).then_inc(l1["x"], 1)
            for b in range(B):
                dve.wait_ge(l1["kr"], b + 1)
                V.scalar_tensor_tensor(W3_[b][:, :], bank[4 * b + 1][:, :], 0.0, W3_[b][:, :], ALU.max,
                                       ALU.mult).then_inc(l1["ka"], 1)
            for b in range(B):
                dve.wait_ge(l1["v"], b + 1)
                dve.wait_ge(l1["rt"], b + 1)
                link(V.scalar_tensor_tensor(W1_[b][:, :], W4_[b][:, :], 1.0, bank[4 * b + 3][:, :], ALU.add, ALU.mult))
                update(2 + b, by_tile(W1_[b][:, :]), htg[:, 4:5])
            keys(0)

            for b in range(B):
                dve.wait_ge(l2["s2"], b + 1)
                link(V.reduce_max(small[b][0:K, 20:21], bank[4 * b + 2][0:K, :], AX))
                link(V.tensor_tensor(small[b][0:K, 21:22], small[b][0:K, 20:21], kshift[:, b:b + 1], ALU.add))
                V.tensor_tensor(small[b][0:K, 22:23], kshift[:, b:b + 1], small[b][0:K, 21:22],
                                ALU.subtract).then_inc(l2["shift2"], 1)
            for b in range(B):
                softmax_in(b, l2["S"], l2["sub"], 16)
            for b in range(B):
                softmax_out(b, l2["exp"], l2["P"], 32)
            for b in range(B):
                dve.wait_ge(l2["exp2"], b + 1)
                link(V.reciprocal(small[b][0:K, 40:41], small[b][0:K, 23:24]))
                dve.wait_ge(l2["s2c"], b + 1)
                V.scalar_tensor_tensor(intV[b][:, :, :], bank[4 * b + 2][0:K, 128:384].rearrange("k (j d) -> k j d", d=D),
                                       small[b][0:K, 40:41], vcrow[:, :, :], ALU.mult, ALU.add).then_inc(l2["s2cs"], 1)
            for b in range(B):
                dve.wait_ge(l2["sc"], b + 1)
                dve.wait_ge(l2["c2s"], b + 1)
                link(V.tensor_tensor(W4_[b][:, :], bank[4 * b + 1][:, :], W2_[b][:, :], ALU.subtract))
                dve.wait_ge(l2["t"], b + 1)
                link(V.scalar_tensor_tensor(W4_[b][:, :], W1_[b][:, :], 1.0, W4_[b][:, :], ALU.add, ALU.mult))
                link(V.scalar_tensor_tensor(W4_[b][:, :], W4_[b][:, :], 0.5, W2_[b][:, :], ALU.mult, ALU.add))
                update(4 + b, by_tile(W4_[b][:, :]), tg[:, 1:2])

            def ranks(src, b, n, lt):
                big, same = gt[b][:, :, 0:n, 0:n], eq[b][:, :, 0:n, 0:n]
                this = src.unsqueeze(3).broadcast_to([P, NT, n, n])
                other = src.unsqueeze(2).broadcast_to([P, NT, n, n])
                V.tensor_tensor(big, other, this, ALU.is_gt)
                link(V.tensor_tensor(same, other, this, ALU.is_equal))
                link(V.tensor_tensor(same, same, lt.unsqueeze(1).broadcast_to([P, NT, n, n]), ALU.mult))
                link(V.tensor_tensor(big, big, same, ALU.add))
                return big

            def parts(k, b):
                dve.wait_ge(hT_ready, k + 1)
                link(V.tensor_copy(hhi[b][:, :], hT[b]))
                V.tensor_tensor(hlo[b][:, :], hT[b], hhi[b][:, :].bitcast(F32), ALU.subtract).then_inc(m["split"], 1)

            lt8 = const[:, K_LT8:K_LT8 + 64].rearrange("p (e j) -> p e j", j=8)
            lt4 = const[:, K_LT4:K_LT4 + 16].rearrange("p (e j) -> p e j", j=4)
            rank = [small[b][:, 0:32].rearrange("p (t e) -> p t e", e=E) for b in range(B)]

            def bcast_e(ap, n=E):
                return ap.unsqueeze(2).broadcast_to([P, NT, n])

            def logits(n, b):
                dve.wait_ge(m["lg"], 2 * n + b + 1)
                lp = bank[BANKC[b]][:, 0:NT * E].rearrange("p (t e) -> p t e", e=E)
                link(V.reduce_max(small[b][:, 56:60], lp, AX))
                V.tensor_tensor(lg[b][:, :, :], lp, bcast_e(small[b][:, 56:60]), ALU.subtract).then_inc(m["sub"], 1)

            def weights(n, b, top):
                link(V.tensor_tensor(top, top, ex[b][:, :, :], ALU.mult))
                link(V.reduce_sum(small[b][:, 56:60], top, AX))
                link(V.reciprocal(small[b][:, 60:64], small[b][:, 56:60]))
                link(V.tensor_tensor(top, top, bcast_e(small[b][:, 60:64]), ALU.mult))
                by_parity = top.rearrange("p t (i q) -> p t q i", q=2)
                cp = c2[b][:, :, :].rearrange("p t (q j i) -> p t q j i", q=2, j=2)
                link(V.tensor_copy(cp[:, :, :, 0, :], by_parity))
                V.tensor_tensor(cp[:, :, :, 1, :], by_parity, cp[:, :, :, 0, :].bitcast(F32),
                                ALU.subtract).then_inc(m["c"], 1)

            def route1(b):
                dve.wait_ge(m["sub"], b + 1)
                big = ranks(lg[b][:, :, :], b, E, lt8)
                link(V.tensor_reduce(rank[b], big, AX, ALU.add))
                link(V.tensor_scalar(rank[b], rank[b], 1.5, None, ALU.is_lt))
                dve.wait_ge(m["exp"], b + 1)
                weights(0, b, rank[b])

            def route2(b):
                dve.wait_ge(m["exp"], 2 + b + 1)
                link(V.reduce_sum(small[b][:, 56:60], ex[b][:, :, :], AX))
                link(V.reciprocal(small[b][:, 60:64], small[b][:, 56:60]))
                link(V.tensor_tensor(ex[b][:, :, :], ex[b][:, :, :], bcast_e(small[b][:, 60:64]), ALU.mult))
                best = small[b][:, 40:56].rearrange("p (t g) -> p t g", g=GROUPS)
                link(V.reduce_max(best, ex[b][:, :, :].rearrange("p t (g e) -> p t g e", e=2), AX))
                big = ranks(best, b, GROUPS, lt4)
                grank = small[b][:, 0:16].rearrange("p (t g) -> p t g", g=GROUPS)
                link(V.tensor_reduce(grank, big, AX, ALU.add))
                link(V.tensor_scalar(grank, grank, 1.5, None, ALU.is_lt))
                link(V.tensor_tensor(ex[b][:, :, :].rearrange("p t (g e) -> p t g e", e=2),
                                     ex[b][:, :, :].rearrange("p t (g e) -> p t g e", e=2),
                                     grank.unsqueeze(3).broadcast_to([P, NT, GROUPS, 2]), ALU.mult))
                big = ranks(ex[b][:, :, :], b, E, lt8)
                link(V.tensor_reduce(rank[b], big, AX, ALU.add))
                link(V.tensor_scalar(rank[b], rank[b], 1.5, None, ALU.is_lt))
                weights(1, b, rank[b])

            def weigh(i, j, groups, ys, row_ready, done):
                G, b = groups * i + j, j % B
                if isinstance(G, int) and G < 0:
                    return
                dve.wait_ge(ys, G + 1)
                dve.wait_ge(row_ready, G + 1)
                V.tensor_tensor(ysb[b][:, :], ysb[b][:, :], bank[BANKC[b]][:, :], ALU.mult).then_inc(done, 1)

            for b in range(B):
                parts(6 + b, b)
                logits(0, b)

            def body1(i, last):
                for n in range(N1):
                    g = N1 * i + n
                    if n not in HI_ACT1:
                        dve.wait_ge(q["gelu"], g + 1)
                        V.tensor_copy(rhi[n % 4][:, :], ring[n % 4][:, :]).then_inc(q["hiD"], 1)
                    if n not in LO_POOL1:
                        if n in HI_ACT1:
                            dve.wait_ge(q["hiA"], len(HI_ACT1) * i + before(HI_ACT1, n + 1))
                        else:
                            dve.wait_ge(q["hiD"], len(HI_DVE1) * i + before(HI_DVE1, n + 1))
                        V.tensor_tensor(rlo[n % 4][:, :], ring[n % 4][:, :], rhi[n % 4][:, :].bitcast(F32),
                                        ALU.subtract).then_inc(q["loD"], 1)
                    if i_is(i, 0) and n in (1, 3):
                        route1(n // 2)
                    if n % 4 == 2:
                        weigh(i, (n - 2) // 4 - 2, G1, q["ys"], q["row"], q["mult"])

            body1(0, False)
            with dve.Fori(1, PASSES - 1) as i:
                body1(i, False)
            body1(PASSES - 1, True)
            for j in range(G1 - B, G1):
                weigh(PASSES - 1, j, G1, q["ys"], q["row"], q["mult"])

            for b in range(B):
                dve.wait_ge(m["outN"], b + 1)
                update(6 + b, by_tile(bank[1 + b][:, :]), tg[:, 5:6])

            def attend(n):
                base, gate = [8, 12][n], [2, 3][n]
                for b in range(B):
                    dve.wait_ge(at["qhi"], 2 * n + b + 1)
                    if n == 0:
                        V.tensor_tensor(ql[b][:, :], bank[4 * b][:, :], qh[b][:, :].bitcast(F32),
                                        ALU.subtract).then_inc(at["qlo"], 1)
                    else:
                        V.scalar_tensor_tensor(ql[b][:, :], bank[4 * b][:, :], col("bq3"), qh[b][:, :].bitcast(F32),
                                               ALU.add, ALU.subtract).then_inc(at["qlo"], 1)

                def normalise(u):
                    b, t = u // NT, u % NT
                    dve.wait_ge(at["O"], NT * B * n + u + 1)
                    o = bank[4 * (u % 2)][:, 0:VW]
                    inv = small[b][:, 16 * (t % 2):16 * (t % 2) + 16]
                    link(V.reciprocal(inv, o[:, D:VW]))
                    V.tensor_tensor(W1_[b][:, t * D:(t + 1) * D].rearrange("p (h e) -> p h e", e=DH),
                                    o[:, 0:D].rearrange("p (h e) -> p h e", e=DH),
                                    inv.unsqueeze(2).broadcast_to([P, H, DH]), ALU.mult).then_inc(at["norm"], 1)

                for u in range(NT * B):
                    b, T = u // NT, NT * B * n + u
                    if T >= 2:
                        dve.wait_ge(at["T"], 3 * (T - 1))
                    for j, (h0, h1) in enumerate(HB):
                        dve.wait_ge(at["S"], 3 * T + j + 1)
                        sc = bank[1 + j][:, 0:(h1 - h0) * K].rearrange("p (h k) -> p h k", k=K)
                        mx = small[b][:, 32 + h0:32 + h1]
                        link(V.reduce_max(mx, sc, AX))
                        V.tensor_tensor(Sx[T % 2][:, h0 * K:h1 * K].rearrange("p (h k) -> p h k", k=K), sc,
                                        mx.unsqueeze(2).broadcast_to([P, h1 - h0, K]),
                                        ALU.subtract).then_inc(at["sub"], 1)
                    if u >= 3:
                        normalise(u - 3)
                for u in range(NT * B - 3, NT * B):
                    normalise(u)
                for b in range(B):
                    dve.wait_ge(at["out"], 2 * n + b + 1)
                    if n == 1:
                        dve.wait_ge(x_biased, B + b + 1)
                    update(base + b, by_tile(bank[(2, 1)[b]][:, :]), tg[:, gate:gate + 1])

            attend(0)
            keys(1)

            for b in range(B):
                parts(10 + b, b)
                logits(1, b)

            def body2(i, last):
                for n in range(N2):
                    g = N2 * i + n
                    dve.wait_ge(r["silu"], g + 1)
                    V.tensor_tensor(ring[n % 4][:, :], ring[n % 4][:, :], bank[BANKU[n % 2]][:, :],
                                    ALU.mult).then_inc(r["mul"], 1)
                    dve.wait_ge(r["mul"], g + 1)
                    V.tensor_copy(rhi[n % 4][:, :], ring[n % 4][:, :]).then_inc(r["hi"], 1)
                    if n not in LO_POOL2:
                        dve.wait_ge(r["hi"], g + 1)
                        V.tensor_tensor(rlo[n % 4][:, :], ring[n % 4][:, :], rhi[n % 4][:, :].bitcast(F32),
                                        ALU.subtract).then_inc(r["loD"], 1)
                    if i_is(i, 0) and n < B:
                        route2(n)
                    if n % 2 == 1:
                        weigh(i, (n - 1) // 2 - 2, G2, r["ys"], r["row"], r["mult"])

            body2(0, False)
            with dve.Fori(1, PASSES - 1) as i:
                body2(i, False)
            body2(PASSES - 1, True)
            for j in range(G2 - B, G2):
                weigh(PASSES - 1, j, G2, r["ys"], r["row"], r["mult"])
            for b in range(B):
                dve.wait_ge(m["outN"], B + b + 1)
                update(10 + b, by_tile(bank[1 + b][:, :]), tg[:, 6:7])
            attend(1)

            dve.wait_ge(ld["b2m"], 16)
            for b in range(B):
                for i in range(NH):
                    n = NH * b + i
                    dve.wait_ge(l3["u"], n + 1)
                    w = cols[:, C_W2 + i:C_W2 + i + 1]
                    if i == 0:
                        V.tensor_scalar(W2_[b][:, :], ring[n % 4][:, :], w, b2col[:, 0:1], ALU.mult,
                                        ALU.add).then_inc(l3["acc"], 1)
                    else:
                        V.scalar_tensor_tensor(W2_[b][:, :], ring[n % 4][:, :], w, W2_[b][:, :], ALU.mult,
                                               ALU.add).then_inc(l3["acc"], 1)
                    if i + 1 < NH:
                        dve.wait_ge(l3["acc"], n + 1)
                dve.wait_ge(l3["out"], b + 1)
                dve.wait_ge(x_biased, 2 * B + b + 1)
                update(14 + b, by_tile(bank[4 * b + 2][:, :]), tg[:, 7:8])

        @block.tensor
        def _(pe):
            mm = nc.tensor.matmul

            def mm3(o, lh, ll, rh, rl, start, stop):
                mm(o, lh, rh, start=start, stop=False)
                mm(o, lh, rl, start=False, stop=False)
                return mm(o, ll, rh, start=False, stop=stop)

            def transposes(k):
                b = k % B
                pe.wait_ge(ln_h, k + 1)
                for t in range(NT):
                    last = nc.tensor.transpose(tile(bank[4 * b], t), h[b][:, t, :], ident)
                last.then_inc(ln_T, 1)

            pe.wait_ge(ld["ctx"], 48)
            pe.wait_ge(ld["l0"], 16)
            mm(bank[1][0:1, 0:B * K], col("w2"), ctxT[:, :], start=True, stop=True)
            for b in range(B):
                last = mm(bank[2][0:K, b * D:(b + 1) * D], ctxT[:, b * K:(b + 1) * K], mat("Wqv2"), start=True, stop=True)
            last.then_inc(p0_pe, 1)
            pe.wait_ge(ld["l2"], 16)
            mm(bank[3][:, 0:B * K], mat("WksT"), ctxT[:, :], start=True, stop=True)
            mm(bank[3][:, B * K:2 * B * K], mat("WqsT"), ctxT[:, :], start=True, stop=True)
            mm(bank[6][:, 0:B * K], mat("WvsT"), ctxT[:, :], start=True, stop=True)
            for b in range(B):
                last = mm(bank[5][0:K, b * D:(b + 1) * D], ctxT[:, b * K:(b + 1) * K], mat("WvsT"), start=True, stop=True)
            last.then_inc(p2_pe, 1)
            pe.wait_ge(p2_act, 1)
            pe.wait_ge(p0_act, 1)
            pe.wait_ge(p0_dve, 2)
            pe.wait_ge(p2_dve, 1)
            mm(bank[7][:, 0:B * K], mat("Wqc"), KsT[:, :], start=True, stop=True)
            mm(bank[7][:, B * K:2 * B * K], mat("Wkc"), QsT[:, :], start=True, stop=True)
            mm(bank[1][0:1, B * K:2 * B * K], col("bq_c"), KsT[:, :], start=True, stop=True)
            for b in range(B):
                mm(bank[2][0:K, 256 + b:257 + b], QsT[:, b * K:(b + 1) * K], col("bk_c"), start=True, stop=True)
            mm(bank[6][:, 256:384], mat("Wvc"), mat("Wg2T"), start=True, stop=True)
            mm(bank[6][0:K, 384:512], bvB[:, :], mat("Wg2T"), start=True, stop=True)
            for b in range(B):
                last = mm(bank[5][0:K, (2 + b) * D:(3 + b) * D], VsT[:, b * K:(b + 1) * K], mat("Wg1T"), start=True, stop=True)
            last.then_inc(p2_pe, 1)
            pe.wait_ge(ld["const"], 16)
            pe.wait_ge(ready_const, 1)
            pe.wait_ge(p2_act, 2)
            pe.wait_ge(p2_dve, 2)

            def scores(b, right, shift, done):
                for t in range(NT):
                    o = bank[4 * b + 1][:, t * K:(t + 1) * K]
                    mm(o, tile(hT[b], t), right[:, b * K:(b + 1) * K], start=True, stop=False)
                    last = mm(o, ones[0:1, :], shift[:, b * K:(b + 1) * K], start=False, stop=True)
                last.then_inc(done, 1)

            def context(n):
                wk, wv = (("wk2", "wv2"), ("WkT3", "WvT3"))[n]
                bk, bv = ((2, 3), (5, 6))[n]
                mm(bank[bk][:, 0:B * K], mat(wk), ctxT[:, :], start=True, stop=True)
                for b in range(B):
                    last = mm(bank[bv][0:K, b * D:(b + 1) * D], ctxT[:, b * K:(b + 1) * K], mat(wv), start=True, stop=True)
                last.then_inc(kv["pe"], 1)

            def replicate(n, b):
                pe.wait_ge(kv["act"], n + 1)
                for j, bk in enumerate(BANKV[n, b]):
                    if (n, b, j) == (1, 1, 1):
                        pe.wait_ge(kv["reps"], 10)
                    if (n, b, j) == (1, 1, 2):
                        pe.wait_ge(kv["reps"], 11)
                    c0, c1 = 4 * j, min(4 * j + 4, CH)
                    for c in range(c0, c1):
                        last = mm(tile(bank[bk], c - c0), rep(c), vN[:, b, :], start=True, stop=True)
                    last.then_inc(kv["rep"], 1)

            for b in range(B):
                transposes(b)
            pe.wait_ge(p0_dve, 1)
            for b in range(B):
                pe.wait_ge(hT_ready, b + 1)
                scores(b, simR, simrow, l0["S"])
            for b in range(B):
                pe.wait_ge(l0["P"], b + 1)
                for t in range(NT):
                    last = nc.tensor.transpose(bank[4 * b + 2][0:K, t * P:(t + 1) * P], W1_[b][:, t * K:(t + 1) * K], ident)
                last.then_inc(l0["PT"], 1)
            for b in range(B):
                pe.wait_ge(l0["e"], b + 1)
                for t in range(NT):
                    mm(bank[4 * b][:, 0:1], h[b][:, t, :], small[b][:, 8 + t:9 + t], start=(t == 0), stop=(t == NT - 1))
                mm(bank[4 * b][:, 1:2], ones[:, :], small[b][:, 12:13], start=True, stop=True).then_inc(l0["hc"], 1)
            for b in range(B):
                pe.wait_ge(l0["PTs"], b + 1)
                mm(bank[4 * b + 3][:, :], ctxN[:, b, :], W2_[b][0:K, :], start=True, stop=True).then_inc(l0["hq"], 1)
            for b in range(B):
                pe.wait_ge(l0["W"], b + 1)
                pe.wait_ge(l0["u"], b + 1)
                for t in range(NT):
                    o = tile(bank[4 * b + 1], t)
                    mm(o, tile(hT[b], t), w14[b][:, :], start=True, stop=False)
                    mm(o, W2_[b][0:K, t * P:(t + 1) * P], ctxW2[:, b, :], start=False, stop=False)
                    last = mm(o, tile(W3_[b], t), mat("Wqv3"), start=False, stop=True)
                last.then_inc(l0["out"], 1)
            pe.wait_ge(ld["l3"], 16)
            context(0)

            pe.wait_ge(ld["l1"], 16)
            for b in range(B):
                transposes(2 + b)
            pe.wait_ge(kv["act"], 1)
            for b in range(B):
                pe.wait_ge(l1["x"], 2 * b + 1)
                mm(bank[4 * b + 1][:, :], mat("WkT"), W2_[b][:, :], start=True, stop=True).then_inc(l1["k"], 1)
                pe.wait_ge(l1["x"], 2 * b + 2)
                for t in range(NT):
                    last = mm(tile(bank[4 * b + 2], t), tile(W4_[b], t), mat("WrT"), start=True, stop=True)
                last.then_inc(l1["r"], 1)
            for b in range(B):
                pe.wait_ge(l1["ka"], b + 1)
                for t in range(NT):
                    last = mm(tile(bank[4 * b + 3], t), tile(W3_[b], t), mat("WvT"), start=True, stop=True)
                last.then_inc(l1["v"], 1)
            pe.wait_ge(l1["rt"], B)
            replicate(0, 0)

            for b in range(B):
                transposes(4 + b)
            pe.wait_ge(kv["reps"], 3)
            for b in range(B):
                pe.wait_ge(hT_ready, 4 + b + 1)
                mm(bank[4 * b + 2][0:K, :], Mk[:, b * K:(b + 1) * K], hT[b], start=True, stop=True).then_inc(l2["s2"], 1)
            for b in range(B):
                scores(b, Mq, qrow, l2["S"])
            for b in range(B):
                pe.wait_ge(l2["exp2"], b + 1)
                for t in range(NT):
                    last = nc.tensor.transpose(bank[4 * b][:, t * K:(t + 1) * K], W2_[b][0:K, t * P:(t + 1) * P],
                                               ident[0:K, 0:K])
                last.then_inc(l2["P2T"], 1)
            for b in range(B):
                pe.wait_ge(l2["P2Ts"], b + 1)
                for t in range(NT):
                    last = mm(bank[4 * b + 2][:, 0:K], h[b][:, t, :], W4_[b][:, t * K:(t + 1) * K],
                              start=(t == 0), stop=(t == NT - 1))
                last.then_inc(l2["ah"], 1)
                pe.wait_ge(l2["P"], b + 1)
                for t in range(NT):
                    last = nc.tensor.transpose(bank[4 * b + 3][0:K, t * P:(t + 1) * P], W1_[b][:, t * K:(t + 1) * K], ident)
                last.then_inc(l2["PT"], 1)
            for b in range(B):
                pe.wait_ge(l2["ahs"], b + 1)
                mm(bank[4 * b + 2][0:K, 128:384], AhT[b][:, :], WvG[:, :, :], start=True, stop=True).then_inc(l2["s2c"], 1)
            for b in range(B):
                pe.wait_ge(l2["PTs"], b + 1)
                for t in range(NT):
                    last = mm(tile(bank[4 * b + 1], t), W3_[b][0:K, t * P:(t + 1) * P], Vs[:, b, :], start=True, stop=True)
                last.then_inc(l2["c2s"], 1)
            for b in range(B):
                pe.wait_ge(l2["s2cs"], b + 1)
                for t in range(NT):
                    last = mm(tile(bank[4 * b + 3], t), interpT[:, t * P:(t + 1) * P], intV[b][:, 0, :], start=True, stop=True)
                last.then_inc(l2["s2ci"], 1)
                for t in range(NT):
                    o = tile(bank[4 * b], t)
                    mm(o, W3_[b][0:K, t * P:(t + 1) * P], VsG[:, b, :], start=True, stop=False)
                    last = mm(o, interpT[:, t * P:(t + 1) * P], intV[b][:, 1, :], start=False, stop=True)
                last.then_inc(l2["z"], 1)
            pe.wait_ge(l2["sc"], 1)
            replicate(0, 1)

            def router(n, b, k):
                pe.wait_ge(hT_ready, k + 1)
                for t in range(NT):
                    last = mm(bank[BANKC[b]][:, E * t:E * (t + 1)], tile(hT[b], t),
                              rwT[:, n * E:(n + 1) * E], start=True, stop=True)
                last.then_inc(m["lg"], 1)

            def weights_T(n, b):
                pe.wait_ge(m["c"], 2 * n + b + 1)
                for t in range(NT):
                    last = nc.tensor.transpose(bank[BANKC[b]][0:2 * E, t * P:(t + 1) * P],
                                               c2[b][:, t, :].bitcast(F32), ident)
                last.then_inc(m["cT"], 1)

            def weights_row(i, j, groups, done):
                if isinstance(i, int) and groups * i + j < 0:
                    return
                p, b = j // B % 2, j % B
                mm(bank[BANKC[b]][:, :], sel[:, 2 * b + p, :], cflat[:, i + j // (2 * B), :],
                   start=True, stop=True).then_inc(done, 1)

            def down(i, n, chunks, groups, sems, lo, lo_count):
                j, c = n // chunks, n % chunks
                G, b = groups * i + j, j % B
                if c == 0:
                    wait_positive(pe, sems["ys"], G - 1)
                end = c == chunks - 1
                if end:
                    wait_positive(pe, sems["mult"], G - 2)
                    if i_is(i, 0) and j == 1:
                        pe.wait_ge(m["flat"], 16 * B * ((sems is r) + 1))
                        if sems is q:
                            pe.wait_ge(m["acc0"], B)
                pe.wait_ge(lo, lo_count)
                o = bank[4 * b][:, :]
                mm(o, wdh[j // B][:, c, :], rhi[n % 4][:, :], start=(c == 0), stop=False)
                if end:
                    weights_row(i, j - 1, groups, sems["row"])
                mm(o, wdh[j // B][:, c, :], rlo[n % 4][:, :], start=False, stop=False)
                mm(o, wdl[j // B][:, c, :], rhi[n % 4][:, :], start=False, stop=end).then_inc(sems["free"], 1)

            pe.wait_ge(kv["reps"], 6)
            pe.wait_ge(ld["moe1"], 80)
            pe.wait_ge(resid, 6)
            for b in range(B):
                transposes(6 + b)
                router(0, b, 6 + b)

            def hidden1(i, n):
                p, b, c = CH1[n]
                g = N1 * i + n
                if c == 0 and b == 0:
                    pe.wait_ge(q["wl"], 2 * i + p + 1)
                wait_positive(pe, q["gelu"], g - 3)
                w = slice(c * P, (c + 1) * P)
                mm3(bank[BANKS1[n % 4]][:, :], wuh[p][:, w], wul[p][:, w], hhi[b][:, :], hlo[b][:, :],
                    True, True).then_inc(q["h"], 1)

            def body1(i, last):
                for n in range(N1):
                    if n + LAG1 < N1:
                        hidden1(i, n + LAG1)
                    elif not last:
                        hidden1(i + 1, n + LAG1 - N1)
                    if i_is(i, 0) and n in (2, 4):
                        weights_T(0, n // 2 - 1)
                    if i_is(i, 0) and n == 5:
                        for b in range(B):
                            pe.wait_ge(m["cTs"], b + 1)
                            mm(bank[BANKC[b]][:, :], b2E[:, :], cT[:, b * S:(b + 1) * S].bitcast(F32),
                               start=True, stop=True).then_inc(m["b2"], 1)
                    if n in LO_POOL1:
                        down(i, n, C1, G1, q, q["loP"], len(LO_POOL1) * i + before(LO_POOL1, n + 1))
                    else:
                        down(i, n, C1, G1, q, q["loD"], len(LO_DVE1) * i + before(LO_DVE1, n + 1))

            def finish(n, sems, groups):
                pe.wait_ge(sems["mult"], PASSES * groups - 2)
                weights_row(PASSES - 1, groups - 1, groups, sems["row"])
                for b in range(B):
                    pe.wait_ge(sems["add"], PASSES * groups - 1 + b)
                    for t in range(NT):
                        last = nc.tensor.transpose(tile(bank[1 + b], t), tile(acc[b], t), ident)
                    last.then_inc(m["outN"], 1)

            pe.wait_ge(m["split"], B)
            for n in range(LAG1):
                hidden1(0, n)
            body1(0, False)
            with pe.Fori(1, PASSES - 1) as i:
                body1(i, False)
            body1(PASSES - 1, True)
            pe.wait_ge(q["gelu"], N1 * PASSES)
            finish(0, q, G1)

            def attend(n):
                base = [8, 12][n]
                wq, wo = (("wq2", "wo2"), ("WqT3", "WoT3"))[n]
                pe.wait_ge(nb_ready, 1)
                pe.wait_ge(ld["pair"], 32)
                for b in range(B):
                    transposes(base + b)
                for b in range(B):
                    pe.wait_ge(hT_ready, base + b + 1)
                    mm(bank[4 * b][:, :], mat(wq), hT[b], start=True, stop=True).then_inc(at["q"], 1)
                pe.wait_ge(kv["pool"], 4 * (n + 1))

                def scores_of(u):
                    b, t = u // NT, u % NT
                    T = NT * B * n + u
                    pe.wait_ge(at["qlo"], 2 * n + b + 1)
                    for j, (h0, h1) in enumerate(HB):
                        if u >= 1:
                            pe.wait_ge(at["sub"], 3 * (T - 1) + j + 1)
                        o = bank[1 + j][:, 0:(h1 - h0) * K]
                        if n == 0:
                            mm(o, ident_b[:, :], nb[:, b, t, :].unsqueeze(1).broadcast_to([P, h1 - h0, K]),
                               start=True, stop=False)
                        mm3(o, tile(qh[b], t), tile(ql[b], t), kbh[b][:, h0:h1, :], kbl[b][:, h0:h1, :],
                            n == 1, True).then_inc(at["S"], 1)

                def transpose_of(u):
                    T = NT * B * n + u
                    pe.wait_ge(at["exp"], T + 1)
                    if T >= 1:
                        pe.wait_ge(at["PT"], 3 * T)
                    for c in range(CH):
                        last = nc.tensor.transpose(tile(bank[5 + c // 4], c % 4), tile(Sx[T % 2], c), ident)
                        if c % 4 == 3 or c == CH - 1:
                            last.then_inc(at["T"], 1)

                def values_of(u):
                    b = u // NT
                    T = NT * B * n + u
                    pe.wait_ge(at["PT"], 3 * (T + 1))
                    if u < B:
                        pe.wait_ge(at["qlo"], 2 * n + u + 1)
                    else:
                        pe.wait_ge(at["norm"], T - 1)
                    if u % NT == 0:
                        pe.wait_ge(kv["bd"], 2 * n + b + 1)
                    o = bank[4 * (u % 2)][:, 0:VW]
                    for c in range(CH):
                        last = mm(o, tile(PT[T % 2], c), vbd[b][:, c, :], start=(c == 0), stop=(c == CH - 1))
                    last.then_inc(at["O"], 1)

                def output_T(b):
                    pe.wait_ge(at["norm"], NT * (B * n + b + 1))
                    for t in range(NT):
                        last = nc.tensor.transpose(tile(bank[(1, 3)[b]], t), tile(W1_[b], t), ident)
                    last.then_inc(at["OT"], 1)

                def output_of(b):
                    pe.wait_ge(at["OTs"], 2 * n + b + 1)
                    for t in range(NT):
                        last = mm(tile(bank[(2, 1)[b]], t), tile(W2_[b], t), mat(wo), start=True, stop=True)
                    last.then_inc(at["out"], 1)

                scores_of(0)
                for u in range(NT * B):
                    if u + 1 < NT * B:
                        scores_of(u + 1)
                    transpose_of(u)
                    if u >= 1:
                        values_of(u - 1)
                pe.wait_ge(at["sub"], 3 * NT * B * (n + 1))
                output_T(0)
                values_of(NT * B - 1)
                if n == 0:
                    context(1)
                output_of(0)
                output_T(1)
                output_of(1)

            attend(0)
            for b in range(B):
                replicate(1, b)
            for b in range(B):
                transposes(10 + b)
            pe.wait_ge(kv["reps"], 12)
            for b in range(B):
                router(1, b, 10 + b)

            def hidden2(i, n):
                p, b, c = CH2[n]
                g = N2 * i + n
                if c == 0 and b == 0:
                    pe.wait_ge(r["wl"], 2 * i + p + 1)
                wait_positive(pe, r["mul"], g - 1)
                for bk, off in ((BANKG[n % 2], 0), (BANKU[n % 2], F2)):
                    w = slice(off + c * P, off + (c + 1) * P)
                    last = mm3(bank[bk][:, :], wuh[p][:, w], wul[p][:, w], hhi[b][:, :], hlo[b][:, :], True, True)
                last.then_inc(r["g"], 1)

            def body2(i, last):
                for n in range(N2):
                    if n + LAG2 < N2:
                        hidden2(i, n + LAG2)
                    elif not last:
                        hidden2(i + 1, n + LAG2 - N2)
                    if i_is(i, 0) and n in (1, 2):
                        weights_T(1, n - 1)
                    if n in LO_POOL2:
                        down(i, n, C2, G2, r, r["loP"], len(LO_POOL2) * i + before(LO_POOL2, n + 1))
                    else:
                        down(i, n, C2, G2, r, r["loD"], len(LO_DVE2) * i + before(LO_DVE2, n + 1))

            pe.wait_ge(resid, 10)
            pe.wait_ge(m["split"], 2 * B)
            for n in range(LAG2):
                hidden2(0, n)
            body2(0, False)
            with pe.Fori(1, PASSES - 1) as i:
                body2(i, False)
            body2(PASSES - 1, True)
            finish(1, r, G2)
            attend(1)

            for b in range(B):
                transposes(14 + b)
                pe.wait_ge(hT_ready, 14 + b + 1)
                mm(bank[4 * b + 3][:, :], mat("WinD"), hT[b], start=True, stop=True).then_inc(l3["s"], 1)
            for b in range(B):
                pe.wait_ge(l3["acc"], NH * (b + 1))
                for t in range(NT):
                    last = mm(tile(bank[4 * b + 2], t), tile(W2_[b], t), mat("WoutD"), start=True, stop=True)
                last.then_inc(l3["out"], 1)


def shape_constants():
    c = np.zeros((P, NK), np.float32)
    c[:, K_ID:K_ID + P] = np.eye(P)
    c[np.arange(D), K_HEAD + np.arange(D) // DH] = 1
    c[:, K_LT8:K_LT8 + 64] = np.tril(np.ones((8, 8)), -1).ravel()
    c[:, K_LT4:K_LT4 + 16] = np.tril(np.ones((4, 4)), -1).ravel()
    pairs = np.arange(SPAN)
    c[pairs % K, K_REP + pairs] = 1
    pair = np.zeros((P, CH, H), np.float32)
    pair[pairs % P, pairs // P, pairs // K] = 1
    c[:, K_PAIR:K_PAIR + CH * H] = pair.reshape(P, -1)
    pos = np.clip((np.arange(S, dtype=np.float32) + np.float32(0.5)) * np.float32(K / S) - np.float32(0.5), 0, K - 1)
    lo = np.floor(pos).astype(np.int64)
    hi = np.minimum(lo + 1, K - 1)
    w = (pos - lo).astype(np.float32)
    for i in range(S):
        c[lo[i], K_INT + i] += 1 - w[i]
        c[hi[i], K_INT + i] += w[i]
    c[np.arange(8), K_SEL + np.arange(8) // 2] = 1
    return c, pair


def kernel(**inputs):
    import concourse.bacc as bacc
    from concourse.bass_utils import run_bass_kernel_spmd

    z = {k: np.asarray(v) for k, v in inputs.items()}
    T = np.transpose
    qv = z["L0_xattn_W_qv"].reshape(4, D, D)
    wg = z["L1_xattn_Wg"]
    kv3 = z["L3_xattn_Wkv"]
    by_name = {
        "Wqv1": qv[0], "Wqv2": qv[1], "Wqv3": qv[2], "Wqv4": qv[3],
        "WrT": T(z["L0_ffn_W_r"]), "WkT": T(z["L0_ffn_W_k"]), "WvT": T(z["L0_ffn_W_v"]),
        "WksT": T(z["L1_xattn_Wk_s"]), "WqsT": T(z["L1_xattn_Wq_s"]), "WvsT": T(z["L1_xattn_Wv_s"]),
        "WvcT": T(z["L1_xattn_Wv_c"]), "Wvc": z["L1_xattn_Wv_c"], "Wqc": z["L1_xattn_Wq_c"], "Wkc": z["L1_xattn_Wk_c"],
        "Wg1T": T(wg[:, :D]), "Wg2T": T(wg[:, D:]),
        "wq2": z["L2_xattn_w_q"], "wk2": z["L2_xattn_w_k"], "wv2": z["L2_xattn_w_v"], "wo2": z["L2_xattn_w_o"],
        "WqT3": T(z["L3_xattn_Wq"]), "WkT3": T(kv3[:D]), "WvT3": T(kv3[D:]), "WoT3": T(z["L3_xattn_Wo"]),
        "WinD": np.concatenate([z["L3_ffn_Win"]] * 2, 1), "WoutD": np.concatenate([z["L3_ffn_Wout"]] * 2, 0),
    }
    ws = z["L0_xattn_w_sim"]

    def doubled(w):
        return np.concatenate([w[:, :NH], w[:, NH:]], 0)

    bin_ = z["L3_ffn_bin_"]
    vecs = [ws[:D], ws[D:2 * D], ws[2 * D:], z["L0_ffn_mu_r"], z["L0_ffn_mu_k"], z["L1_xattn_bk_s"],
            z["L1_xattn_bq_s"], z["L1_xattn_bq_c"], z["L1_xattn_bk_c"], z["L1_xattn_bv_s"], z["L1_xattn_bv_c"],
            z["L3_xattn_bq"],
            np.concatenate([bin_, bin_])]
    cols = np.concatenate([np.stack(vecs, 1), doubled(z["L3_ffn_W1"]), doubled(z["L3_ffn_b1"]),
                           doubled(z["L3_ffn_W2"])], 1)
    rows = np.concatenate([z["L0_xattn_b_qv"], z["L3_xattn_bo"], z["L3_ffn_bout"], z["L1_xattn_bv_s"],
                           z["L1_xattn_bv_c"], z["L1_xattn_bg"], z["g_xattn"], z["g_ffn"], z["L0_xattn_b_sim"]])
    const, pair = shape_constants()
    arrays = {
        "x": z["x"], "ctx": z["ctx_1024"], "ctxT": T(z["ctx_1024"], (2, 0, 1)).reshape(D, B * K),
        "mask": z["mask_Bx1xSxS2_ik1"].reshape(B, S, K), "rows": rows, "cols": cols,
        "mats": np.stack([by_name[n] for n in MATS], 1), "const": const, "pair": pair,
        "b2m": z["L3_ffn_b2"].reshape(M_IN, 1),
        "rwT": np.concatenate([T(z["L1_ffn_router_w"]), T(z["L2_ffn_gate_w"])], 1),
        "b2": z["L1_ffn_b2"],
        "w1": np.concatenate([T(z["L1_ffn_w1"], (2, 0, 1)),
                                                    T(z["L1_ffn_b1"].reshape(E, C1, P), (2, 0, 1))], 2), "w2": T(z["L1_ffn_w2"].reshape(E, D, C1, P), (3, 0, 2, 1)),
        "v13": T(z["L2_ffn_w13_weight"], (2, 0, 1)),
        "v2": T(z["L2_ffn_w2_weight"].reshape(E, D, C2, P), (3, 0, 2, 1)),
    }
    arrays = {f"in_{k}": np.ascontiguousarray(v) for k, v in arrays.items()}
    nc = bacc.Bacc("TRN2", target_bir_lowering=False, num_devices=1)
    aps = {k[3:]: nc.dram_tensor(k, v.shape, mybir.dt.from_np(v.dtype), kind="ExternalInput").ap()
           for k, v in arrays.items()}
    out = nc.dram_tensor("out", (B, S, D), F32, kind="ExternalOutput").ap()
    flamingo_program(nc, aps, out)
    res = run_bass_kernel_spmd(nc, [arrays], core_ids=[0])
    return res.results[0]["out"]
```

```python
from contextlib import ExitStack

import numpy as np

import concourse.bass as bass
from concourse import mybir

F32 = mybir.dt.float32
F32R = mybir.dt.float32r
BF16 = mybir.dt.bfloat16
I32 = mybir.dt.int32
ALU = mybir.AluOpType
ACT = mybir.ActivationFunctionType
AX = mybir.AxisListType.X

B, S, D, K = 2, 512, 128, 77
P = 128
NT = S // P
EPS = 1e-5
E = 8
F1 = 512
C1 = F1 // P
F2 = 256
C2 = F2 // P
H = 16
DH = D // H
GROUPS = 4
SPAN = H * K
CH = -(-SPAN // P)
HB = [(0, 6), (6, 12), (12, 16)]
HW = 3
FIRST = [min(c * P // K, H - HW) for c in range(CH)]
VW = DH + 1
MASKED = -1e30
M_IN = 64
NH = 8
UA, UD = 7, 6

COL = {n: i for i, n in enumerate(
    ["w1", "w2", "w3", "mu_r", "mu_k", "bk_s", "bq_s", "bq_c", "bk_c", "bv_s", "bv_c", "bq3", "bin"])}
NC0 = len(COL)
C_W1, C_B1, C_W2, C_B2 = NC0, NC0 + NH, NC0 + 2 * NH, NC0 + 3 * NH
NCOL = NC0 + 3 * NH
ROW = {n: i for i, n in enumerate(["b_qv", "bo3", "bout", "bv_s", "bv_c", "bg"])}
R_G = len(ROW) * D
R_BSIM = R_G + 8
NROW = R_BSIM + 1
MAT0 = ["Wqv1", "Wqv2", "Wqv3", "Wqv4"]
MAT1 = ["WrT", "WkT", "WvT"]
MAT2 = ["WksT", "WqsT", "WvsT", "WvcT", "Wvc", "Wqc", "Wkc", "Wg1T", "Wg2T"]
MAT3 = ["wq2", "wk2", "wv2", "wo2", "WqT3", "WkT3", "WvT3", "WoT3", "WinD", "WoutD"]
MATS = MAT0 + MAT1 + MAT2 + MAT3
K_ID = 0
K_HEAD = K_ID + P
K_LT8 = K_HEAD + H
K_LT4 = K_LT8 + 64
K_REP = K_LT4 + 16
K_PAIR = K_REP + CH * P
K_INT = K_PAIR + CH * HW
K_SEL = K_INT + S
NK = K_SEL + 4


def flamingo_program(nc, a, out):
    ctx = ExitStack()
    with ctx:
        def sb(name, shape, dt=F32):
            return ctx.enter_context(nc.sbuf_tensor(name, shape, dt))

        def sem(name):
            return ctx.enter_context(nc.semaphore(name))

        const = sb("const", [P, NK])
        mats = sb("mats", [P, len(MATS), P])
        cols = sb("cols", [P, NCOL])
        b2col = sb("b2col", [P, 1])
        rows = sb("rows", [P, NROW])
        ctxT = sb("ctxT", [P, B * K])
        ctxN = sb("ctxN", [K, B, D])
        mask = sb("mask", [P, B, NT, K], I32)
        rwT = sb("rwT", [P, 2 * E])
        b2E = sb("b2E", [2 * E, D])
        up_raw = [sb(f"up_raw{i}", [P, F1 + C1]) for i in range(2)]
        b1s = [sb(f"b1s{i}", [P, C1]) for i in range(2)]
        down_raw = [sb(f"down_raw{i}", [P, C1, D]) for i in range(2)]

        def mat(n):
            return mats[:, MATS.index(n), :]

        def col(n, p=P):
            return cols[0:p, COL[n]:COL[n] + 1]

        def row(n, p=P):
            return rows[0:p, ROW[n] * D:(ROW[n] + 1) * D]

        ident = const[:, K_ID:K_ID + P]
        head = const[:, K_HEAD:K_HEAD + H]

        def rep(c):
            return const[0:K, K_REP + c * P:K_REP + (c + 1) * P]

        pair = const[:, K_PAIR:K_PAIR + CH * HW].rearrange("p (c h) -> p c h", h=HW)
        interpT = const[0:K, K_INT:K_INT + S]

        x = [sb(f"x{b}", [P, NT, D]) for b in range(B)]
        h = [sb(f"h{b}", [P, NT, D]) for b in range(B)]
        hTz = [sb(f"hTz{b}", [P, S + 1]) for b in range(B)]
        hT = [t[:, 1:S + 1] for t in hTz]
        hhi = [sb(f"hhi{b}", [P, S], F32R) for b in range(B)]
        hlo = [sb(f"hlo{b}", [P, S], F32R) for b in range(B)]
        stats = [sb(f"stats{b}", [P, NT, 6]) for b in range(B)]
        mv = [sb(f"mv{b}", [P, NT, 2]) for b in range(B)]
        var = [sb(f"var{b}", [P, NT]) for b in range(B)]
        neghalf = sb("neghalf", [P, NT])
        rstd = [sb(f"rstd{b}", [P, NT]) for b in range(B)]
        ones = sb("ones", [P, P])
        ident_b = sb("ident_b", [P, P], BF16)
        tg = sb("tg", [P, 8])
        htg = sb("htg", [P, 8])
        tgb = sb("tgb", [P, 3, D])

        W1_ = [sb(f"wa{b}", [P, S]) for b in range(B)]
        W2_ = [sb(f"wb{b}", [P, S]) for b in range(B)]
        W3_ = [sb(f"wc{b}", [P, S]) for b in range(B)]
        W4_ = [sb(f"wd{b}", [P, S]) for b in range(B)]
        small = [sb(f"small{b}", [P, 64]) for b in range(B)]

        simR = sb("simR", [P, B * K])
        simrow = sb("simrow", [1, B * K])
        ctxW2 = sb("ctxW2", [K, B, D])
        w14 = [sb(f"w14_{b}", [P, D]) for b in range(B)]
        KsT = sb("KsT", [P, B * K])
        QsT = sb("QsT", [P, B * K])
        VsT = sb("VsT", [P, B * K])
        Mq = sb("Mq", [P, B * K])
        Mk = sb("Mk", [P, B * K])
        qrow = sb("qrow", [1, B * K])
        kshift = sb("kshift", [K, B])
        Vs = sb("Vs", [K, B, D])
        VsG = sb("VsG", [K, B, D])
        intV = [sb(f"intV{b}", [K, 2, D]) for b in range(B)]
        AhT = [sb(f"AhT{b}", [P, K]) for b in range(B)]
        WvG = sb("WvG", [P, 2, D])
        bvB = sb("bvB", [P, K])
        vcrow = sb("vcrow", [K, 2, D])

        BT = B * NT
        lg = sb("lg", [P, BT, E])
        ex = sb("ex", [P, BT, E])
        gt = sb("gt", [P, BT, E, E])
        eq = sb("eq", [P, BT, E, E])
        rank = sb("rank", [P, BT, E])
        best = sb("best", [P, BT, GROUPS])
        grank = sb("grank", [P, BT, GROUPS])
        rsum = sb("rsum", [P, BT])
        rinv = sb("rinv", [P, BT])
        c2 = sb("c2", [P, BT, 2 * E], F32R)
        cT = sb("cT", [2 * E, B * S], F32R)
        cflat = sb("cflat", [4 * B, E // 2, S], F32R)
        sel = sb("sel", [4 * B, 4, P], F32R)
        shared = sb("shared", [P, 2 * CH * P])
        PT = [shared[:, i * CH * P:(i + 1) * CH * P] for i in range(2)]
        ring = [shared[:, i * S:(i + 1) * S] for i in range(4)]
        ysb, acc = W1_, W2_
        rhi = [sb(f"rhi{i}", [P, S], F32R) for i in range(4)]
        rlo = [sb(f"rlo{i}", [P, S], F32R) for i in range(4)]
        wuh = [sb(f"wuh{i}", [P, F1], F32R) for i in range(2)]
        wul = [sb(f"wul{i}", [P, F1], F32R) for i in range(2)]
        wdh = [sb(f"wdh{i}", [P, C1, D], F32R) for i in range(2)]
        wdl = [sb(f"wdl{i}", [P, C1, D], F32R) for i in range(2)]

        nb = sb("nb", [P, B, NT, K], BF16)
        kT = sb("kT", [P, B * K])
        kTh = sb("kTh", [P, B * K], F32R)
        kTl = sb("kTl", [P, B * K])
        kbh = [sb(f"kbh{b}", [P, H, K], F32R) for b in range(B)]
        kbl = [sb(f"kbl{b}", [P, H, K], F32R) for b in range(B)]
        vN = sb("vN", [K, B, D])
        vals = [sb(f"vals{b}", [P, (CH * HW + H - HW) * VW]) for b in range(B)]
        vbd = [v[:, 0:CH * HW * VW].rearrange("p (c h e) -> p c h e", h=HW, e=VW) for v in vals]
        Sx = [sb(f"Sx{i}", [P, CH * P]) for i in range(2)]
        qh, ql = hhi, hlo

        woutS = sb("woutS", [P, NH - UD, D])

        bank = [ctx.enter_context(nc.psum_tensor(f"bank{i}", [P, 512], F32)) for i in range(8)]

        ld = {n: sem(f"ld_{n}") for n in
              ["x0", "x1", "first", "ctx", "l0", "l1", "l2", "l3", "mask", "ident", "const", "moe1", "b2m"]}
        raw_in = [sem(f"raw_in{i}") for i in range(2)]
        out_done = sem("out_done")
        dve_step, pool_step = sem("dve_step"), sem("pool_step")
        ready_const = sem("ready_const")
        ln_var, ln_rstd, ln_h, ln_T, hT_ready = [sem(n) for n in ("ln_var", "ln_rstd", "ln_h", "ln_T", "hT_ready")]
        x_biased, resid = sem("x_biased"), sem("resid")
        gates = sem("gates")
        tgb_ready = sem("tgb_ready")
        p0_dve, p0_pe, p0_act = sem("p0_dve"), sem("p0_pe"), sem("p0_act")
        p2_pe, p2_act = sem("p2_pe"), sem("p2_act")
        l0 = {n: sem(f"l0_{n}") for n in
              ["S", "sub", "exp", "P", "PT", "PTs", "hq", "u", "m1", "nM", "e", "hc", "W", "out"]}
        l1 = {n: sem(f"l1_{n}") for n in ["x", "k", "r", "kr", "rt", "ka", "v"]}
        l2 = {n: sem(f"l2_{n}") for n in
              ["S", "s2", "sub", "exp", "shift2", "exp2", "P", "PT", "PTs", "P2T", "P2Ts", "ah", "ahs", "s2c",
               "s2cs", "c2s", "s2ci", "z", "t", "sc"]}
        m = {n: sem(f"m_{n}") for n in
             ["split", "lg", "sub", "exp", "c", "cT", "cTs", "flat", "b2", "acc0", "zero", "sum", "outN"]}
        q = {n: sem(f"q_{n}") for n in
             ["h", "gelu", "hiA", "hiD", "loD", "loP", "free", "uh", "ul", "dh", "dl", "ys", "row", "mult", "add"]}
        r = {n: sem(f"r_{n}") for n in
             ["g", "silu", "mul", "hi", "loD", "loP", "free", "uh", "ul", "dh", "dl", "ys", "row", "mult", "add"]}
        kv = {n: sem(f"kv_{n}") for n in ["pe", "act", "pool", "rep", "reps", "bd", "hi"]}
        at = {n: sem(f"at_{n}") for n in
              ["q", "qhi", "qlo", "S", "sub", "exp", "T", "PT", "O", "norm", "OT", "OTs", "out"]}
        l3 = {n: sem(f"l3_{n}") for n in ["wout", "s", "ss", "u", "up", "ut", "acc", "out"]}
        nb_ready = sem("nb_ready")

        block = ctx.enter_context(nc.Block())

        def tile(ap, t):
            return ap[:, t * P:(t + 1) * P]

        def over_tiles(ap):
            return ap.unsqueeze(1).broadcast_to([P, NT, D])

        def wait_positive(eng, semaphore, value):
            if not isinstance(value, int) or value > 0:
                eng.wait_ge(semaphore, value)

        def i_is(i, value):
            return isinstance(i, int) and i == value

        def before(members, n):
            return sum(j in members for j in range(n))

        CH1 = [(p, b, c) for p in range(2) for b in range(B) for c in range(C1)]
        CH2 = [(p, b, c) for p in range(2) for b in range(B) for c in range(C2)]
        N1, N2 = len(CH1), len(CH2)
        LAG1, LAG2 = 3, 2
        PASSES = E // 2
        G1, G2 = N1 // C1, N2 // C2
        LO_POOL1 = {n for n in range(N1) if n % 4 in (0, 2)}
        HI_ACT1 = {n for n in range(N1) if n % 4 == 1}
        LO_POOL2 = {1, 5}
        ALL1, ALL2 = set(range(N1)), set(range(N2))
        HI_DVE1, LO_DVE1, LO_DVE2 = ALL1 - HI_ACT1, ALL1 - LO_POOL1, ALL2 - LO_POOL2
        BANKS1 = [1, 2, 3, 7]
        BANKG, BANKU = [1, 2], [3, 7]
        BANKC = [5, 6]
        BANKV = {(0, 0): 5, (0, 1): 2, (1, 0): 7, (1, 1): 3}

        @block.sync
        def _(sp):
            M0, M1 = len(MAT0), len(MAT0 + MAT1)
            M2 = M1 + len(MAT2)
            for b in range(B):
                sp.dma_start(x[b][:, :, :], a["x"][b].rearrange("(t p) d -> p t d", p=P)).then_inc(ld[f"x{b}"], 16)
            sp.dma_start(const[:, 0:K_REP], a["const"][:, 0:K_REP]).then_inc(ld["ident"], 16)
            sp.dma_start(rows[:, :], a["rows"].partition_broadcast(P)).then_inc(ld["first"], 16)
            sp.dma_start(mats[:, 0:M0, :], a["mats"][:, 0:M0, :]).then_inc(ld["l0"], 16)
            sp.dma_start(mats[:, M1:M2, :], a["mats"][:, M1:M2, :]).then_inc(ld["l2"], 16)
            sp.dma_start(mats[:, M0:M1, :], a["mats"][:, M0:M1, :]).then_inc(ld["l1"], 16)
            sp.dma_start(mats[:, M2:, :], a["mats"][:, M2:, :]).then_inc(ld["l3"], 16)
            sp.dma_start(const[:, K_REP:], a["const"][:, K_REP:]).then_inc(ld["const"], 16)
            sp.dma_start(rwT[:, :], a["rwT"]).then_inc(ld["moe1"], 16)
            for p in range(2):
                for j in range(2):
                    r0 = (2 * p + j) * (E // 2)
                    sp.dma_start(b2E[r0:r0 + E // 2, :],
                                 a["b2"].rearrange("(i p) d -> p i d", p=2)[p]).then_inc(ld["moe1"], 16)

            def load_expert(up, down, nd, e, p):
                sp.dma_start(up_raw[p][:, 0:a[up].shape[2]], a[up][:, e, :]).then_inc(raw_in[p], 16)
                sp.dma_start(down_raw[p][:, 0:nd, :], a[down][:, e, :, :]).then_inc(raw_in[p], 16)

            for p in range(2):
                load_expert("w1", "w2", C1, p, p)
            sp.wait_ge(ready_const, 1)
            sp.dma_start(b2col[0:M_IN, :], a["b2m"]).then_inc(ld["b2m"], 16)

            with sp.Fori(0, PASSES - 1) as i:
                for p in range(2):
                    sp.wait_ge(q["dl"], 2 * i + p + 1)
                    load_expert("w1", "w2", C1, 2 * i + 2 + p, p)
            for p in range(2):
                sp.wait_ge(q["dl"], E - 1 + p)
                load_expert("v13", "v2", C2, p, p)
            with sp.Fori(0, PASSES - 1) as i:
                for p in range(2):
                    sp.wait_ge(r["dl"], 2 * i + p + 1)
                    load_expert("v13", "v2", C2, 2 * i + 2 + p, p)
            for b in range(B):
                sp.wait_ge(resid, 2 * 7 + b + 1)
                sp.dma_start(out[b].rearrange("(t p) d -> p t d", p=P), x[b][:, :, :]).then_inc(out_done, 16)
            sp.wait_ge(out_done, 16 * B)

        @block.gpsimd
        def _(pool):
            pool.dma_start(mask[:, :, :, :], a["mask"].rearrange("b (t p) k -> p b t k", p=P)).then_inc(ld["mask"], 16)
            nc.gpsimd.memset(neghalf[:, :], -0.5)
            nc.gpsimd.memset(ones[:, :], 1.0)
            for b in range(B):
                nc.gpsimd.memset(hTz[b][:, 0:1], 0.0)
            for i in range(2):
                nc.gpsimd.memset(Sx[i][:, SPAN:], 0.0)
            for b in range(B):
                nc.gpsimd.memset(vals[b][:, CH * HW * VW:], 0.0)
            nc.gpsimd.memset(b2col[:, :], 0.0).then_inc(ready_const, 1)
            pool.wait_ge(ready_const, 1)
            steps = [0]

            def link(ins):
                steps[0] += 1
                ins.then_inc(pool_step, 1)
                pool.wait_ge(pool_step, steps[0])

            def norm(k):
                b = k % B
                pool.wait_ge(ln_var, k + 1)
                nc.gpsimd.tensor_tensor(rstd[b][:, :], var[b][:, :], neghalf[:, :], ALU.pow).then_inc(ln_rstd, 1)

            def add_bias(n, b):
                pool.wait_ge(ln_h, NT * (2 * [0, 6, 7][n] + b + 1))
                pool.wait_ge(tgb_ready, 1)
                nc.gpsimd.tensor_tensor(x[b][:, :, :], x[b][:, :, :], over_tiles(tgb[:, n, :]),
                                        ALU.add).then_inc(x_biased, 1)

            def key(b, part):
                dst, src = ((kbh, kTh[:, b * K:(b + 1) * K].bitcast(F32)), (kbl, kTl[:, b * K:(b + 1) * K]))[part]
                nc.gpsimd.tensor_tensor(dst[b][:, :, :], src.unsqueeze(1).broadcast_to([P, H, K]),
                                        head.unsqueeze(2).broadcast_to([P, H, K]), ALU.mult).then_inc(kv["pool"], 1)

            def mask_values(n, b):
                pool.wait_ge(kv["reps"], 2 * n + b + 1)
                v = vbd[b][:, :, :, 0:DH]
                nc.gpsimd.tensor_tensor(v, v, pair.unsqueeze(3).broadcast_to([P, CH, HW, DH]),
                                        ALU.mult).then_inc(kv["bd"], 1)

            def split_up(i, p, sems):
                pool.wait_ge(sems["uh"], 2 * i + p + 1)
                nc.gpsimd.tensor_tensor(wul[p][:, :], up_raw[p][:, 0:F1], wuh[p][:, :].bitcast(F32),
                                        ALU.subtract).then_inc(sems["ul"], 1)

            def split_down(i, p, nd, sems):
                pool.wait_ge(sems["dh"], 2 * i + p + 1)
                pool.wait_ge(sems["ul"], 2 * i + p + 1)
                nc.gpsimd.tensor_tensor(wdl[p][:, 0:nd, :], down_raw[p][:, 0:nd, :],
                                        wdh[p][:, 0:nd, :].bitcast(F32), ALU.subtract).then_inc(sems["dl"], 1)

            for k in range(2):
                norm(k)
            for b in range(B):
                add_bias(0, b)
            for b in range(B):
                pool.wait_ge(l0["m1"], b + 1)
                link(nc.gpsimd.partition_all_reduce(small[b][:, 5:6], small[b][:, 4:5], P, bass.bass_isa.ReduceOp.max))
                nc.gpsimd.tensor_scalar(small[b][:, 6:7], small[b][:, 5:6], -1.0, 0.0, ALU.mult,
                                        ALU.add).then_inc(l0["nM"], 1)
            for k in range(2, 6):
                norm(k)
            pool.wait_ge(ld["ident"], 16)
            pool.wait_ge(ld["const"], 16)
            pool.wait_ge(kv["hi"], 1)
            for b in range(B):
                nc.gpsimd.tensor_scalar(vbd[b][:, :, :, DH], pair, 1.0, 0.0, ALU.mult, ALU.add)
                for part in range(2):
                    key(b, part)
            mask_values(0, 0)
            pool.wait_ge(ld["l3"], 16)
            pool.wait_ge(ld["ctx"], 48)
            for j in range(NH - UD):
                w = cols[:, C_W2 + UD + j:C_W2 + UD + j + 1]
                last = nc.gpsimd.tensor_scalar(woutS[:, j, :], mat("WoutD"), w, 0.0, ALU.mult, ALU.add)
            last.then_inc(l3["wout"], 1)
            split_up(0, 0, q)
            split_down(0, 0, C1, q)
            for k in range(6, 8):
                norm(k)

            def low(n, hi, count, lo):
                pool.wait_ge(hi, count)
                nc.gpsimd.tensor_tensor(rlo[n % 4][:, :], ring[n % 4][:, :], rhi[n % 4][:, :].bitcast(F32),
                                        ALU.subtract).then_inc(lo, 1)

            def add(i, j, groups, mult, done):
                G, b = groups * i + j, j % B
                if isinstance(G, int) and G < 0:
                    return
                pool.wait_ge(mult, G + 1)
                wait_positive(pool, done, G - 1)
                nc.gpsimd.tensor_tensor(acc[b][:, :], acc[b][:, :], ysb[b][:, :], ALU.add).then_inc(done, 1)

            def body1(i, last):
                for n in range(N1):
                    if n == 0:
                        split_up(i, 1, q)
                    if n == 3:
                        split_down(i, 1, C1, q)
                    if n == N1 // 2 and not last:
                        split_up(i + 1, 0, q)
                    if n == N1 // 2 + 3 and not last:
                        split_down(i + 1, 0, C1, q)
                    if n in LO_POOL1:
                        low(n, q["hiD"], len(HI_DVE1) * i + before(HI_DVE1, n + 1), q["loP"])
                    if i_is(i, 0) and n == 11:
                        pool.wait_ge(m["acc0"], B)
                    if n % 4 == 3:
                        add(i, (n - 3) // 4 - 2, G1, q["mult"], q["add"])

            mask_values(0, 1)
            body1(0, False)
            with pool.Fori(1, PASSES - 1) as i:
                body1(i, False)
            body1(PASSES - 1, True)

            for k in range(8, 10):
                norm(k)
            split_up(0, 0, r)
            split_down(0, 0, C2, r)
            for k in range(10, 12):
                norm(k)
            for b in range(B):
                nc.gpsimd.memset(acc[b][:, :], 0.0).then_inc(m["zero"], 1)
            pool.wait_ge(kv["hi"], 2)
            pool.wait_ge(at["S"], 3 * NT * B)
            for b, part in ((0, 0), (0, 1), (1, 0)):
                key(b, part)
            mask_values(1, 0)
            pool.wait_ge(m["zero"], B)

            def body2(i, last):
                for n in range(N2):
                    if n == 0:
                        split_up(i, 1, r)
                    if n == 2:
                        split_down(i, 1, C2, r)
                    if n == N2 // 2 and not last:
                        split_up(i + 1, 0, r)
                    if n == N2 // 2 + 2 and not last:
                        split_down(i + 1, 0, C2, r)
                    if n in LO_POOL2:
                        low(n, r["hi"], N2 * i + n + 1, r["loP"])
                    if n % 2 == 1:
                        add(i, (n - 1) // 2 - 2, G2, r["mult"], r["add"])
                    if i_is(i, 0) and n == 4:
                        key(1, 1)

            body2(0, False)
            with pool.Fori(1, PASSES - 1) as i:
                body2(i, False)
            body2(PASSES - 1, True)
            for k in range(12, 14):
                norm(k)
            mask_values(1, 1)
            for b in range(B):
                add_bias(1, b)
            for k in range(14, 16):
                norm(k)
            for b in range(B):
                pool.wait_ge(l3["ss"], b + 1)
                for j in range(NH - UA):
                    i, u = UA + j, (W3_, W4_)[j][b]
                    link(nc.gpsimd.tensor_scalar(u[:, :], W1_[b][:, :], cols[:, C_W1 + i:C_W1 + i + 1],
                                                 cols[:, C_B1 + i:C_B1 + i + 1], ALU.mult, ALU.add))
                    nc.gpsimd.tensor_scalar(u[:, :], u[:, :], 0.0, 0.0, ALU.max, ALU.add).then_inc(l3["up"], 1)
                add_bias(2, b)

        @block.scalar
        def _(act):
            act.dma_start(cols[:, :], a["cols"]).then_inc(ld["ctx"], 16)
            act.dma_start(ctxT[:, :], a["ctxT"]).then_inc(ld["ctx"], 16)
            act.dma_start(ctxN[:, :, :], a["ctx"].rearrange("b k d -> k b d")).then_inc(ld["ctx"], 16)

            def transposed(k):
                b = k % B
                act.wait_ge(ln_T, k + 1)
                nc.scalar.activation(hT[b], bank[4 * b][:, :], ACT.Copy).then_inc(hT_ready, 1)

            def values(n):
                act.wait_ge(kv["pe"], n + 1)
                bk, bv = ((0, 4), (5, 6))[n]
                if n == 1:
                    act.wait_ge(kv["hi"], 1)
                    act.wait_ge(kv["rep"], 2)
                nc.scalar.activation(kT[:, :], bank[bk][:, 0:B * K], ACT.Copy, scale=float(DH) ** -0.5)
                nc.scalar.activation(vN[:, :, :], bank[bv][0:K, 0:B * D], ACT.Copy).then_inc(kv["act"], 1)

            def replicated(n, b):
                act.wait_ge(kv["rep"], 2 * n + b + 1)
                nc.scalar.activation(vbd[b][:, :, :, 0:DH],
                                     bank[BANKV[n, b]][:, 0:CH * HW * DH].rearrange("p (c h e) -> p c h e", h=HW, e=DH),
                                     ACT.Copy).then_inc(kv["reps"], 1)

            def up_hi(i, p, mixture, chunks, sems, in_psum):
                act.wait_ge(raw_in[p], 32 * (PASSES * mixture + i + 1))
                wait_positive(act, in_psum, chunks * i + chunks // 2 * (p - 1))
                if mixture == 0:
                    wait_positive(act, sems["gelu"], chunks * i + chunks // 2 * (p - 1))
                    nc.scalar.activation(b1s[p][:, :], up_raw[p][:, F1:F1 + C1], ACT.Copy)
                nc.scalar.activation(wuh[p][:, :], up_raw[p][:, 0:F1], ACT.Copy).then_inc(sems["uh"], 1)

            def down_hi(i, p, chunks, nd, sems):
                wait_positive(act, sems["free"], chunks * i + chunks // 2 * (p - 1))
                nc.scalar.activation(wdh[p][:, 0:nd, :], down_raw[p][:, 0:nd, :], ACT.Copy).then_inc(sems["dh"], 1)

            act.wait_ge(ld["first"], 16)
            nc.scalar.activation(tg[:, :], rows[:, R_G:R_G + 8], ACT.Tanh).then_inc(gates, 1)
            act.wait_ge(p0_pe, 1)
            nc.scalar.activation(simrow[:, :], bank[1][0:1, 0:B * K], ACT.Identity,
                                 bias=rows[0:1, R_BSIM:R_BSIM + 1])
            nc.scalar.activation(ctxW2[:, :, :], bank[2][0:K, 0:B * D], ACT.Copy).then_inc(p0_act, 1)
            for b in range(B):
                transposed(b)
            for b in range(B):
                act.wait_ge(l0["sub"], b + 1)
                nc.scalar.activation(W1_[b][:, 0:NT * K], W1_[b][:, 0:NT * K], ACT.Exp).then_inc(l0["exp"], 1)
                act.wait_ge(l0["nM"], b + 1)
                nc.scalar.activation(small[b][:, 8:12], small[b][:, 0:4], ACT.Exp, bias=small[b][:, 6:7],
                                     accum_out=small[b][:, 12:13]).then_inc(l0["e"], 1)
                act.wait_ge(l0["PT"], b + 1)
                nc.scalar.activation(W2_[b][0:K, :], bank[4 * b + 2][0:K, :], ACT.Copy).then_inc(l0["PTs"], 1)
            transposed(2)
            act.wait_ge(p2_pe, 1)
            nc.scalar.activation(KsT[:, :], bank[3][:, 0:B * K], ACT.Identity, bias=col("bk_s"))
            nc.scalar.activation(QsT[:, :], bank[3][:, B * K:2 * B * K], ACT.Identity, bias=col("bq_s"))
            nc.scalar.activation(VsT[:, :], bank[6][:, 0:B * K], ACT.Identity, bias=col("bv_s"))
            nc.scalar.activation(Vs[:, :, :], bank[2][0:K, 0:B * D], ACT.Copy).then_inc(p2_act, 1)
            transposed(3)
            act.wait_ge(p2_pe, 2)
            sc = float(D) ** -0.5
            nc.scalar.activation(Mq[:, :], bank[7][:, 0:B * K], ACT.Copy, scale=sc)
            nc.scalar.activation(Mk[:, :], bank[7][:, B * K:2 * B * K], ACT.Copy, scale=sc)
            nc.scalar.activation(WvG[:, 1, :], bank[7][:, 384:512], ACT.Copy)
            nc.scalar.activation(vcrow[:, 1, :], bank[3][0:K, 0:D], ACT.Copy)
            nc.scalar.activation(qrow[:, :], bank[3][0:1, D:D + B * K], ACT.Copy, scale=sc)
            nc.scalar.activation(kshift[:, :], bank[3][0:K, 300:300 + B], ACT.Copy, scale=sc)
            nc.scalar.activation(VsG[:, :, :], bank[6][0:K, 0:B * D], ACT.Copy).then_inc(p2_act, 1)
            for b in range(B):
                act.wait_ge(l1["k"], b + 1)
                nc.scalar.activation(W3_[b][:, :], bank[4 * b + 1][:, :], ACT.Relu).then_inc(l1["kr"], 1)
                act.wait_ge(l1["r"], b + 1)
                nc.scalar.activation(W4_[b][:, :], bank[4 * b + 2][:, :], ACT.Tanh, scale=0.5).then_inc(l1["rt"], 1)
            values(0)
            replicated(0, 0)

            for b in range(B):
                transposed(4 + b)
            for b in range(B):
                act.wait_ge(l2["shift2"], b + 1)
                nc.scalar.activation(W2_[b][0:K, :], bank[4 * b + 2][0:K, :], ACT.Exp, bias=small[b][0:K, 22:23],
                                     accum_out=small[b][0:K, 23:24]).then_inc(l2["exp2"], 1)
            for b in range(B):
                act.wait_ge(l2["sub"], b + 1)
                nc.scalar.activation(W1_[b][:, 0:NT * K], W1_[b][:, 0:NT * K], ACT.Exp).then_inc(l2["exp"], 1)
            for b in range(B):
                act.wait_ge(l2["P2T"], b + 1)
                nc.scalar.activation(W4_[b][:, 0:NT * K], bank[4 * b][:, 0:NT * K], ACT.Copy).then_inc(l2["P2Ts"], 1)
            for b in range(B):
                act.wait_ge(l2["PT"], b + 1)
                nc.scalar.activation(W3_[b][0:K, :], bank[4 * b + 3][0:K, :], ACT.Copy).then_inc(l2["PTs"], 1)
            for b in range(B):
                act.wait_ge(l2["ah"], b + 1)
                nc.scalar.activation(AhT[b][:, :], bank[4 * b + 2][:, 0:K], ACT.Copy).then_inc(l2["ahs"], 1)
            up_hi(0, 0, 0, N1, q, q["h"])
            down_hi(0, 0, N1, C1, q)
            for b in range(B):
                act.wait_ge(l2["s2ci"], b + 1)
                nc.scalar.activation(W2_[b][:, :], bank[4 * b + 3][:, :], ACT.Copy).then_inc(l2["sc"], 1)
                act.wait_ge(l2["z"], b + 1)
                nc.scalar.activation(W1_[b][:, :], bank[4 * b][:, :], ACT.Tanh, scale=0.5).then_inc(l2["t"], 1)
            replicated(0, 1)

            def exponentials(n):
                act.wait_ge(m["sub"], n + 1)
                nc.scalar.activation(ex[:, :, :], lg[:, :, :], ACT.Exp).then_inc(m["exp"], 1)

            def weights_T(n, b):
                act.wait_ge(m["cT"], 2 * n + b + 1)
                nc.scalar.activation(cT[:, b * S:(b + 1) * S], bank[BANKC[b]][0:2 * E, :],
                                     ACT.Copy).then_inc(m["cTs"], 1)
                act.wait_ge(m["cTs"], 2 * n + b + 1)
                act.dma_start(cflat[4 * b:4 * b + 4, :, :].bitcast(F32),
                              cT[:, b * S:(b + 1) * S].bitcast(F32)).then_inc(m["flat"], 16)

            for b in range(B):
                transposed(6 + b)
            exponentials(0)

            def output(i, j, groups, chunks, free, added, done):
                G, b = groups * i + j, j % B
                if isinstance(G, int) and G < 0:
                    return
                act.wait_ge(free, chunks * (G + 1))
                wait_positive(act, added, G - 1)
                nc.scalar.activation(ysb[b][:, :], bank[4 * b][:, :], ACT.Copy).then_inc(done, 1)

            def body1(i, last):
                for n, (p, b, c) in enumerate(CH1):
                    g = N1 * i + n
                    if n == 0:
                        up_hi(i, 1, 0, N1, q, q["h"])
                    if n == 3:
                        down_hi(i, 1, N1, C1, q)
                    if n == N1 // 2 and not last:
                        up_hi(i + 1, 0, 0, N1, q, q["h"])
                    if n == N1 // 2 + 3 and not last:
                        down_hi(i + 1, 0, N1, C1, q)
                    act.wait_ge(q["h"], g + 1)
                    nc.scalar.activation(ring[n % 4][:, :], bank[BANKS1[n % 4]][:, :], ACT.Gelu,
                                         bias=b1s[p][:, c:c + 1]).then_inc(q["gelu"], 1)
                    if n in HI_ACT1:
                        act.wait_ge(q["gelu"], g + 1)
                        nc.scalar.activation(rhi[n % 4][:, :], ring[n % 4][:, :], ACT.Copy).then_inc(q["hiA"], 1)
                    if i_is(i, 0) and n in (5, 6):
                        weights_T(0, n - 5)
                    if i_is(i, 0) and n == 8:
                        for b0 in range(B):
                            act.wait_ge(m["b2"], b0 + 1)
                            nc.scalar.activation(acc[b0][:, :], bank[BANKC[b0]][:, :],
                                                 ACT.Copy).then_inc(m["acc0"], 1)
                    if n % 4 == 2:
                        output(i, (n - 2) // 4 - 1, G1, C1, q["free"], q["add"], q["ys"])

            act.wait_ge(ld["moe1"], 80)
            body1(0, False)
            with act.Fori(1, PASSES - 1) as i:
                body1(i, False)
            body1(PASSES - 1, True)
            output(PASSES - 1, G1 - 1, G1, C1, q["free"], q["add"], q["ys"])

            def attend(n):
                base = [8, 12][n]
                for b in range(B):
                    transposed(base + b)
                    act.wait_ge(at["q"], 2 * n + b + 1)
                    if n == 0:
                        nc.scalar.activation(qh[b][:, :], bank[4 * b][:, :], ACT.Copy).then_inc(at["qhi"], 1)
                    else:
                        nc.scalar.activation(qh[b][:, :], bank[4 * b][:, :], ACT.Identity,
                                             bias=col("bq3")).then_inc(at["qhi"], 1)
                for u in range(NT * B):
                    T = NT * B * n + u
                    if T == 2:
                        up_hi(0, 0, 1, N2, r, r["g"])
                        down_hi(0, 0, N2, C2, r)
                    act.wait_ge(at["sub"], 3 * (T + 1))
                    nc.scalar.activation(Sx[T % 2][:, 0:SPAN], Sx[T % 2][:, 0:SPAN], ACT.Exp).then_inc(at["exp"], 1)
                    if T >= 2:
                        act.wait_ge(at["O"], T - 1)
                    for j, w in enumerate((512, 512, 256)):
                        act.wait_ge(at["T"], 3 * T + j + 1)
                        nc.scalar.activation(PT[T % 2][:, 512 * j:512 * j + w], bank[5 + j][:, 0:w],
                                             ACT.Copy).then_inc(at["PT"], 1)
                for b in range(B):
                    act.wait_ge(at["OT"], 2 * n + b + 1)
                    nc.scalar.activation(W2_[b][:, :], bank[(1, 3)[b]][:, :], ACT.Copy).then_inc(at["OTs"], 1)
                    if n == 0 and b == 0:
                        values(1)

            attend(0)
            for b in range(B):
                replicated(1, b)
            for b in range(B):
                transposed(10 + b)
            exponentials(1)

            def body2(i, last):
                for n, (p, b, c) in enumerate(CH2):
                    g = N2 * i + n
                    if i_is(i, 0) and n in (2, 3):
                        weights_T(1, n - 2)
                    if n == 0:
                        up_hi(i, 1, 1, N2, r, r["g"])
                    if n == 2:
                        down_hi(i, 1, N2, C2, r)
                    if n == N2 // 2 and not last:
                        up_hi(i + 1, 0, 1, N2, r, r["g"])
                    if n == N2 // 2 + 2 and not last:
                        down_hi(i + 1, 0, N2, C2, r)
                    act.wait_ge(r["g"], g + 1)
                    nc.scalar.activation(ring[n % 4][:, :], bank[BANKG[n % 2]][:, :], ACT.Silu).then_inc(r["silu"], 1)
                    if n % 2 == 1:
                        output(i, (n - 1) // 2 - 1, G2, C2, r["free"], r["add"], r["ys"])

            body2(0, False)
            with act.Fori(1, PASSES - 1) as i:
                body2(i, False)
            body2(PASSES - 1, True)
            output(PASSES - 1, G2 - 1, G2, C2, r["free"], r["add"], r["ys"])
            attend(1)

            def hidden_in(b):
                transposed(14 + b)
                act.wait_ge(l3["s"], b + 1)
                nc.scalar.activation(W1_[b][:, :], bank[4 * b + 3][:, :], ACT.Identity,
                                     bias=col("bin")).then_inc(l3["ss"], 1)

            def pair_of_units(b, i):
                if i < UD:
                    n = UD * b + i
                    if n >= 4:
                        act.wait_ge(l3["acc"], n - 3)
                    u, done = ring[n % 4][:, :], l3["u"]
                else:
                    u, done = Sx[b][:, 0:S], l3["ut"]
                nc.scalar.activation(u, W1_[b][:, :], ACT.Relu, scale=cols[:, C_W1 + i:C_W1 + i + 1],
                                     bias=cols[:, C_B1 + i:C_B1 + i + 1]).then_inc(done, 1)

            hidden_in(0)
            act.wait_ge(l3["ss"], 1)
            for i in range(3):
                pair_of_units(0, i)
            hidden_in(1)
            for i in range(3, UA):
                pair_of_units(0, i)
            act.wait_ge(l3["ss"], 2)
            for i in range(UA):
                pair_of_units(1, i)

        @block.vector
        def _(dve):
            steps = [0]
            V = nc.vector

            def link(ins):
                steps[0] += 1
                ins.then_inc(dve_step, 1)
                dve.wait_ge(dve_step, steps[0])

            def statistics(k):
                b = k % B
                for t in range(NT):
                    last = V.bn_stats(stats[b][:, t, :], x[b][:, t, :])
                link(last)
                for t in range(NT):
                    last = V.bn_aggr(mv[b][:, t, :], stats[b][:, t, :])
                link(last)
                V.tensor_scalar(var[b][:, :], mv[b][:, :, 1], EPS, None, ALU.add).then_inc(ln_var, 1)

            def normalised(k):
                b = k % B
                dve.wait_ge(ln_rstd, k + 1)
                for t in range(NT):
                    V.tensor_scalar(h[b][:, t, :], x[b][:, t, :], mv[b][:, t, 0:1], rstd[b][:, t:t + 1],
                                    ALU.subtract, ALU.mult).then_inc(ln_h, 1)

            def updates(k, result, gate):
                for b in range(B):
                    V.scalar_tensor_tensor(x[b][:, :, :], by_tile(result(b)), gate, x[b][:, :, :],
                                           ALU.mult, ALU.add).then_inc(resid, 1)
                    if k + 2 < 16:
                        if b == 1:
                            normalised(k + 2)
                        dve.wait_ge(resid, k + b + 1)
                        statistics(k + 2 + b)
                if k + 2 < 16:
                    normalised(k + 3)

            def tiles3(ap, w=K):
                return ap.rearrange("p (t k) -> p t k", k=w)

            def by_tile(ap):
                return ap.rearrange("p (t d) -> p t d", d=D)

            for b in range(B):
                dve.wait_ge(ld[f"x{b}"], 16)
                statistics(b)
            dve.wait_ge(ld["ctx"], 48)
            V.tensor_scalar(simR[:, :], ctxT[:, :], col("w3"), col("w1"), ALU.mult, ALU.add).then_inc(p0_dve, 1)
            for b in range(B):
                normalised(b)
            dve.wait_ge(ready_const, 1)
            V.tensor_scalar(bvB[:, :], ones[:, 0:K], col("bv_c"), None, ALU.mult).then_inc(p0_dve, 1)
            dve.wait_ge(gates, 1)
            V.tensor_scalar(htg[:, :], tg[:, :], 0.5, None, ALU.mult)
            for n, (name, g) in enumerate((("b_qv", 0), ("bo3", 3), ("bout", 7))):
                last = V.tensor_scalar(tgb[:, n, :], row(name), tg[:, g:g + 1], None, ALU.mult)
            last.then_inc(tgb_ready, 1)
            V.tensor_copy(vcrow[:, 0, :], row("bv_c", K))

            def softmax_in(b, S_sem, sub_sem, maxcol):
                dve.wait_ge(S_sem, b + 1)
                sc = tiles3(bank[4 * b + 1][:, 0:NT * K])
                link(V.reduce_max(small[b][:, maxcol:maxcol + NT], sc, AX))
                V.tensor_tensor(tiles3(W1_[b][:, 0:NT * K]), sc,
                                small[b][:, maxcol:maxcol + NT].unsqueeze(2).broadcast_to([P, NT, K]),
                                ALU.subtract).then_inc(sub_sem, 1)

            def softmax_out(b, exp_sem, P_sem, sumcol):
                dve.wait_ge(exp_sem, b + 1)
                pr = tiles3(W1_[b][:, 0:NT * K])
                link(V.reduce_sum(small[b][:, sumcol:sumcol + NT], pr, AX))
                link(V.reciprocal(small[b][:, sumcol + NT:sumcol + 2 * NT], small[b][:, sumcol:sumcol + NT]))
                V.tensor_tensor(pr, pr, small[b][:, sumcol + NT:sumcol + 2 * NT].unsqueeze(2).broadcast_to([P, NT, K]),
                                ALU.mult).then_inc(P_sem, 1)


            def probabilities(b):
                softmax_in(b, l0["S"], l0["sub"], 0)
                V.reduce_max(small[b][:, 4:5], small[b][:, 0:NT], AX).then_inc(l0["m1"], 1)

            def token_sum(b):
                dve.wait_ge(l0["hc"], b + 1)
                link(V.reciprocal(small[b][:, 14:15], bank[4 * b][:, 1:2]))
                link(V.tensor_tensor(small[b][:, 15:16], bank[4 * b][:, 0:1], small[b][:, 14:15], ALU.mult))
                V.scalar_tensor_tensor(w14[b][:, :], mat("Wqv4"), small[b][:, 15:16], mat("Wqv1"),
                                       ALU.mult, ALU.add).then_inc(l0["W"], 1)

            def product(b):
                dve.wait_ge(l0["hq"], b + 1)
                dve.wait_ge(hT_ready, b + 1)
                V.tensor_tensor(W3_[b][:, :], hT[b], bank[4 * b + 3][:, :], ALU.mult).then_inc(l0["u"], 1)

            probabilities(0)
            softmax_out(0, l0["exp"], l0["P"], 24)
            probabilities(1)
            token_sum(0)
            softmax_out(1, l0["exp"], l0["P"], 24)
            product(0)
            token_sum(1)
            product(1)
            dve.wait_ge(ld["l2"], 16)
            V.tensor_copy(WvG[:, 0, :], mat("WvcT"))
            dve.wait_ge(ld["const"], 16)
            dve.wait_ge(ld["ident"], 16)
            V.tensor_copy(ident_b[:, :], ident)
            V.tensor_copy(sel[:, :, :], const[0:4 * B, K_SEL:K_SEL + 4].unsqueeze(2).broadcast_to([4 * B, 4, P]))
            dve.wait_ge(ld["mask"], 16)
            V.tensor_scalar(nb[:, :, :, :], mask[:, :, :, :], 0.0, MASKED, ALU.is_equal, ALU.mult).then_inc(nb_ready, 1)

            def result(b):
                dve.wait_ge(l0["out"], b + 1)
                dve.wait_ge(x_biased, b + 1)
                return bank[4 * b + 1][:, :]

            updates(0, result, tg[:, 0:1])

            def keys(n):
                dve.wait_ge(kv["act"], n + 1)
                if n == 1:
                    dve.wait_ge(kv["pool"], 4)
                link(V.tensor_copy(kTh[:, :], kT[:, :]))
                V.tensor_tensor(kTl[:, :], kT[:, :], kTh[:, :].bitcast(F32), ALU.subtract).then_inc(kv["hi"], 1)

            for b in range(B):
                dve.wait_ge(hT_ready, 2 + b + 1)
                link(V.tensor_tensor(W1_[b][:, :], hTz[b][:, 1:S + 1], hTz[b][:, 0:S], ALU.subtract))
                V.scalar_tensor_tensor(W2_[b][:, :], W1_[b][:, :], col("mu_k"), hTz[b][:, 0:S], ALU.mult,
                                       ALU.add).then_inc(l1["x"], 1)
                V.scalar_tensor_tensor(W4_[b][:, :], W1_[b][:, :], col("mu_r"), hTz[b][:, 0:S], ALU.mult,
                                       ALU.add).then_inc(l1["x"], 1)
            for b in range(B):
                dve.wait_ge(l1["kr"], b + 1)
                V.scalar_tensor_tensor(W3_[b][:, :], bank[4 * b + 1][:, :], 0.0, W3_[b][:, :], ALU.max,
                                       ALU.mult).then_inc(l1["ka"], 1)

            def result(b):
                dve.wait_ge(l1["v"], b + 1)
                dve.wait_ge(l1["rt"], b + 1)
                link(V.scalar_tensor_tensor(W1_[b][:, :], W4_[b][:, :], 1.0, bank[4 * b + 3][:, :], ALU.add, ALU.mult))
                return W1_[b][:, :]

            updates(2, result, htg[:, 4:5])
            keys(0)

            for b in range(B):
                dve.wait_ge(l2["s2"], b + 1)
                link(V.reduce_max(small[b][0:K, 20:21], bank[4 * b + 2][0:K, :], AX))
                link(V.tensor_tensor(small[b][0:K, 21:22], small[b][0:K, 20:21], kshift[:, b:b + 1], ALU.add))
                V.tensor_tensor(small[b][0:K, 22:23], kshift[:, b:b + 1], small[b][0:K, 21:22],
                                ALU.subtract).then_inc(l2["shift2"], 1)
            for b in range(B):
                softmax_in(b, l2["S"], l2["sub"], 16)
            for b in range(B):
                softmax_out(b, l2["exp"], l2["P"], 32)
            for b in range(B):
                dve.wait_ge(l2["exp2"], b + 1)
                link(V.reciprocal(small[b][0:K, 40:41], small[b][0:K, 23:24]))
                dve.wait_ge(l2["s2c"], b + 1)
                V.scalar_tensor_tensor(intV[b][:, :, :], bank[4 * b + 2][0:K, 128:384].rearrange("k (j d) -> k j d", d=D),
                                       small[b][0:K, 40:41], vcrow[:, :, :], ALU.mult, ALU.add).then_inc(l2["s2cs"], 1)

            def result(b):
                dve.wait_ge(l2["sc"], b + 1)
                dve.wait_ge(l2["c2s"], b + 1)
                link(V.tensor_tensor(W4_[b][:, :], bank[4 * b + 1][:, :], W2_[b][:, :], ALU.subtract))
                dve.wait_ge(l2["t"], b + 1)
                link(V.scalar_tensor_tensor(W4_[b][:, :], W1_[b][:, :], 1.0, W4_[b][:, :], ALU.add, ALU.mult))
                link(V.scalar_tensor_tensor(W4_[b][:, :], W4_[b][:, :], 0.5, W2_[b][:, :], ALU.mult, ALU.add))
                return W4_[b][:, :]

            updates(4, result, tg[:, 1:2])

            def ranks(src, n, lt, out):
                big, same = gt[:, :, 0:n, 0:n], eq[:, :, 0:n, 0:n]
                this = src.unsqueeze(3).broadcast_to([P, BT, n, n])
                other = src.unsqueeze(2).broadcast_to([P, BT, n, n])
                V.tensor_tensor(big, other, this, ALU.is_gt)
                link(V.tensor_tensor(same, other, this, ALU.is_equal))
                link(V.tensor_tensor(same, same, lt.unsqueeze(1).broadcast_to([P, BT, n, n]), ALU.mult))
                link(V.tensor_tensor(big, big, same, ALU.add))
                link(V.tensor_reduce(out, big, AX, ALU.add))
                link(V.tensor_scalar(out, out, 1.5, None, ALU.is_lt))

            def parts(k, b):
                dve.wait_ge(hT_ready, k + 1)
                link(V.tensor_copy(hhi[b][:, :], hT[b]))
                V.tensor_tensor(hlo[b][:, :], hT[b], hhi[b][:, :].bitcast(F32), ALU.subtract).then_inc(m["split"], 1)

            lt8 = const[:, K_LT8:K_LT8 + 64].rearrange("p (e j) -> p e j", j=8)
            lt4 = const[:, K_LT4:K_LT4 + 16].rearrange("p (e j) -> p e j", j=4)

            def bcast_e(ap):
                return ap.unsqueeze(2).broadcast_to([P, BT, E])

            def logits(n):
                dve.wait_ge(m["lg"], n + 1)
                lp = bank[BANKC[0]][:, 0:BT * E].rearrange("p (t e) -> p t e", e=E)
                link(V.reduce_max(rsum[:, :], lp, AX))
                V.tensor_tensor(lg[:, :, :], lp, bcast_e(rsum[:, :]), ALU.subtract).then_inc(m["sub"], 1)

            def weights(top):
                link(V.tensor_tensor(top, top, ex[:, :, :], ALU.mult))
                link(V.reduce_sum(rsum[:, :], top, AX))
                link(V.reciprocal(rinv[:, :], rsum[:, :]))
                link(V.tensor_tensor(top, top, bcast_e(rinv[:, :]), ALU.mult))
                by_parity = top.rearrange("p t (i q) -> p t q i", q=2)
                cp = c2[:, :, :].rearrange("p t (q j i) -> p t q j i", q=2, j=2)
                link(V.tensor_copy(cp[:, :, :, 0, :], by_parity))
                V.tensor_tensor(cp[:, :, :, 1, :], by_parity, cp[:, :, :, 0, :].bitcast(F32),
                                ALU.subtract).then_inc(m["c"], 1)

            def route1():
                dve.wait_ge(m["sub"], 1)
                ranks(lg[:, :, :], E, lt8, rank[:, :, :])
                dve.wait_ge(m["exp"], 1)
                weights(rank[:, :, :])

            def route2():
                dve.wait_ge(m["exp"], 2)
                link(V.reduce_sum(rsum[:, :], ex[:, :, :], AX))
                link(V.reciprocal(rinv[:, :], rsum[:, :]))
                link(V.tensor_tensor(ex[:, :, :], ex[:, :, :], bcast_e(rinv[:, :]), ALU.mult))
                paired = ex[:, :, :].rearrange("p t (g e) -> p t g e", e=2)
                link(V.reduce_max(best[:, :, :], paired, AX))
                ranks(best[:, :, :], GROUPS, lt4, grank[:, :, :])
                link(V.tensor_tensor(paired, paired, grank[:, :, :].unsqueeze(3).broadcast_to([P, BT, GROUPS, 2]),
                                     ALU.mult))
                ranks(ex[:, :, :], E, lt8, rank[:, :, :])
                weights(rank[:, :, :])

            def weigh(i, j, groups, ys, row_ready, done):
                G, b = groups * i + j, j % B
                if isinstance(G, int) and G < 0:
                    return
                dve.wait_ge(ys, G + 1)
                dve.wait_ge(row_ready, G + 1)
                V.tensor_tensor(ysb[b][:, :], ysb[b][:, :], bank[BANKC[b]][:, :], ALU.mult).then_inc(done, 1)

            def weigh_and_add(j, groups, sems):
                G, b = groups * (PASSES - 1) + j, j % B
                weigh(PASSES - 1, j, groups, sems["ys"], sems["row"], sems["mult"])
                dve.wait_ge(sems["mult"], G + 1)
                dve.wait_ge(sems["add"], G - 1)
                V.tensor_tensor(acc[b][:, :], acc[b][:, :], ysb[b][:, :], ALU.add).then_inc(m["sum"], 1)

            for b in range(B):
                parts(6 + b, b)
            logits(0)
            route1()

            def body1(i, last):
                for n in range(N1):
                    g = N1 * i + n
                    if n not in HI_ACT1:
                        dve.wait_ge(q["gelu"], g + 1)
                        V.tensor_copy(rhi[n % 4][:, :], ring[n % 4][:, :]).then_inc(q["hiD"], 1)
                    if n not in LO_POOL1:
                        if n in HI_ACT1:
                            dve.wait_ge(q["hiA"], len(HI_ACT1) * i + before(HI_ACT1, n + 1))
                        else:
                            dve.wait_ge(q["hiD"], len(HI_DVE1) * i + before(HI_DVE1, n + 1))
                        V.tensor_tensor(rlo[n % 4][:, :], ring[n % 4][:, :], rhi[n % 4][:, :].bitcast(F32),
                                        ALU.subtract).then_inc(q["loD"], 1)
                    if n % 4 == 2:
                        weigh(i, (n - 2) // 4 - 2, G1, q["ys"], q["row"], q["mult"])

            body1(0, False)
            with dve.Fori(1, PASSES - 1) as i:
                body1(i, False)
            body1(PASSES - 1, True)
            for j in range(G1 - B, G1):
                weigh_and_add(j, G1, q)


            def result(b):
                dve.wait_ge(m["outN"], b + 1)
                return bank[1 + b][:, :]

            updates(6, result, tg[:, 5:6])

            def attend(n):
                base, gate = [8, 12][n], [2, 3][n]

                def query_lo(b):
                    dve.wait_ge(at["qhi"], 2 * n + b + 1)
                    if n == 0:
                        V.tensor_tensor(ql[b][:, :], bank[4 * b][:, :], qh[b][:, :].bitcast(F32),
                                        ALU.subtract).then_inc(at["qlo"], 1)
                    else:
                        V.scalar_tensor_tensor(ql[b][:, :], bank[4 * b][:, :], col("bq3"), qh[b][:, :].bitcast(F32),
                                               ALU.add, ALU.subtract).then_inc(at["qlo"], 1)

                def normalise(u):
                    b, t = u // NT, u % NT
                    dve.wait_ge(at["O"], NT * B * n + u + 1)
                    o = bank[4 * (u % 2)][:, 0:H * VW].rearrange("p (h e) -> p h e", e=VW)
                    inv = small[b][:, 16 * (t % 2):16 * (t % 2) + 16]
                    link(V.reciprocal(inv, o[:, :, DH]))
                    V.tensor_tensor(W1_[b][:, t * D:(t + 1) * D].rearrange("p (h e) -> p h e", e=DH),
                                    o[:, :, 0:DH],
                                    inv.unsqueeze(2).broadcast_to([P, H, DH]), ALU.mult).then_inc(at["norm"], 1)

                query_lo(0)
                for u in range(NT * B):
                    b, T = u // NT, NT * B * n + u
                    if u == 1:
                        query_lo(1)
                    if T >= 2:
                        dve.wait_ge(at["T"], 3 * (T - 1))
                    for j, (h0, h1) in enumerate(HB):
                        dve.wait_ge(at["S"], 3 * T + j + 1)
                        sc = bank[1 + j][:, 0:(h1 - h0) * K].rearrange("p (h k) -> p h k", k=K)
                        mx = small[b][:, 32 + h0:32 + h1]
                        link(V.reduce_max(mx, sc, AX))
                        V.tensor_tensor(Sx[T % 2][:, h0 * K:h1 * K].rearrange("p (h k) -> p h k", k=K), sc,
                                        mx.unsqueeze(2).broadcast_to([P, h1 - h0, K]),
                                        ALU.subtract).then_inc(at["sub"], 1)
                    if u >= 3:
                        normalise(u - 3)
                for u in range(NT * B - 3, NT * B):
                    normalise(u)

                def result(b):
                    dve.wait_ge(at["out"], 2 * n + b + 1)
                    if n == 1:
                        dve.wait_ge(x_biased, B + b + 1)
                    return bank[(2, 1)[b]][:, :]

                updates(base, result, tg[:, gate:gate + 1])

            attend(0)
            keys(1)

            for b in range(B):
                parts(10 + b, b)
            logits(1)
            route2()

            def body2(i, last):
                for n in range(N2):
                    g = N2 * i + n
                    dve.wait_ge(r["silu"], g + 1)
                    V.tensor_tensor(ring[n % 4][:, :], ring[n % 4][:, :], bank[BANKU[n % 2]][:, :],
                                    ALU.mult).then_inc(r["mul"], 1)
                    dve.wait_ge(r["mul"], g + 1)
                    V.tensor_copy(rhi[n % 4][:, :], ring[n % 4][:, :]).then_inc(r["hi"], 1)
                    if n not in LO_POOL2:
                        dve.wait_ge(r["hi"], g + 1)
                        V.tensor_tensor(rlo[n % 4][:, :], ring[n % 4][:, :], rhi[n % 4][:, :].bitcast(F32),
                                        ALU.subtract).then_inc(r["loD"], 1)
                    if n % 2 == 1:
                        weigh(i, (n - 1) // 2 - 2, G2, r["ys"], r["row"], r["mult"])

            body2(0, False)
            with dve.Fori(1, PASSES - 1) as i:
                body2(i, False)
            body2(PASSES - 1, True)
            for j in range(G2 - B, G2):
                weigh_and_add(j, G2, r)

            def result(b):
                dve.wait_ge(m["outN"], B + b + 1)
                return bank[1 + b][:, :]

            updates(10, result, tg[:, 6:7])
            attend(1)

            dve.wait_ge(ld["b2m"], 16)
            for b in range(B):
                for i in range(UD):
                    n = UD * b + i
                    dve.wait_ge(l3["u"], n + 1)
                    w = cols[:, C_W2 + i:C_W2 + i + 1]
                    if i == 0:
                        V.tensor_scalar(W2_[b][:, :], ring[n % 4][:, :], w, b2col[:, 0:1], ALU.mult,
                                        ALU.add).then_inc(l3["acc"], 1)
                    else:
                        V.scalar_tensor_tensor(W2_[b][:, :], ring[n % 4][:, :], w, W2_[b][:, :], ALU.mult,
                                               ALU.add).then_inc(l3["acc"], 1)
                    if i + 1 < UD:
                        dve.wait_ge(l3["acc"], n + 1)

            def result(b):
                dve.wait_ge(l3["out"], b + 1)
                dve.wait_ge(x_biased, 2 * B + b + 1)
                return bank[4 * b + 2][:, :]

            updates(14, result, tg[:, 7:8])

        @block.tensor
        def _(pe):
            mm = nc.tensor.matmul

            def mm3(o, lh, ll, rh, rl, start, stop):
                mm(o, lh, rh, start=start, stop=False)
                mm(o, lh, rl, start=False, stop=False)
                return mm(o, ll, rh, start=False, stop=stop)

            def transposes(k):
                b = k % B
                for t in range(NT):
                    pe.wait_ge(ln_h, NT * k + t + 1)
                    last = nc.tensor.transpose(tile(bank[4 * b], t), h[b][:, t, :], ident)
                last.then_inc(ln_T, 1)

            pe.wait_ge(ld["ctx"], 48)
            pe.wait_ge(ld["l0"], 16)
            mm(bank[1][0:1, 0:B * K], col("w2"), ctxT[:, :], start=True, stop=True)
            for b in range(B):
                last = mm(bank[2][0:K, b * D:(b + 1) * D], ctxT[:, b * K:(b + 1) * K], mat("Wqv2"), start=True, stop=True)
            last.then_inc(p0_pe, 1)
            def scores(b, right, shift, done):
                mm(bank[4 * b + 1][:, 0:NT * K].rearrange("p (t k) -> p t k", k=K), ones[0:1, :],
                   shift[:, b * K:(b + 1) * K].unsqueeze(1).broadcast_to([1, NT, K]), start=True, stop=False)
                for t in range(NT):
                    last = mm(bank[4 * b + 1][:, t * K:(t + 1) * K], tile(hT[b], t), right[:, b * K:(b + 1) * K],
                              start=False, stop=(t == NT - 1))
                last.then_inc(done, 1)

            def context(n):
                wk, wv = (("wk2", "wv2"), ("WkT3", "WvT3"))[n]
                bk, bv = ((0, 4), (5, 6))[n]
                mm(bank[bk][:, 0:B * K], mat(wk), ctxT[:, :], start=True, stop=True)
                for b in range(B):
                    last = mm(bank[bv][0:K, b * D:(b + 1) * D], ctxT[:, b * K:(b + 1) * K], mat(wv), start=True, stop=True)
                last.then_inc(kv["pe"], 1)

            def replicate(n, b):
                pe.wait_ge(kv["act"], n + 1)
                for c, h0 in enumerate(FIRST):
                    r0 = (CH - 1 - c) * HW * DH
                    last = mm(bank[BANKV[n, b]][:, r0:r0 + HW * DH], rep(c),
                              vN[:, b, h0 * DH:(h0 + HW) * DH], start=True, stop=True)
                last.then_inc(kv["rep"], 1)

            pe.wait_ge(ld["ident"], 16)
            pe.wait_ge(ready_const, 1)
            for b in range(B):
                transposes(b)
                pe.wait_ge(p0_dve, 1)
                pe.wait_ge(p0_act, 1)
                pe.wait_ge(hT_ready, b + 1)
                scores(b, simR, simrow, l0["S"])

            def probabilities_T(b):
                pe.wait_ge(l0["P"], b + 1)
                for t in range(NT):
                    last = nc.tensor.transpose(bank[4 * b + 2][0:K, t * P:(t + 1) * P], W1_[b][:, t * K:(t + 1) * K], ident)
                last.then_inc(l0["PT"], 1)
                pe.wait_ge(l0["e"], b + 1)
                for t in range(NT):
                    mm(bank[4 * b][:, 0:1], h[b][:, t, :], small[b][:, 8 + t:9 + t], start=(t == 0), stop=(t == NT - 1))
                mm(bank[4 * b][:, 1:2], ones[:, :], small[b][:, 12:13], start=True, stop=True).then_inc(l0["hc"], 1)

            def attended(b):
                pe.wait_ge(l0["PTs"], b + 1)
                mm(bank[4 * b + 3][:, :], ctxN[:, b, :], W2_[b][0:K, :], start=True, stop=True).then_inc(l0["hq"], 1)

            def output(b):
                pe.wait_ge(l0["W"], b + 1)
                pe.wait_ge(l0["u"], b + 1)
                for t in range(NT):
                    o = tile(bank[4 * b + 1], t)
                    mm(o, tile(hT[b], t), w14[b][:, :], start=True, stop=False)
                    mm(o, W2_[b][0:K, t * P:(t + 1) * P], ctxW2[:, b, :], start=False, stop=False)
                    last = mm(o, tile(W3_[b], t), mat("Wqv3"), start=False, stop=True)
                last.then_inc(l0["out"], 1)

            probabilities_T(0)
            attended(0)
            probabilities_T(1)
            output(0)
            attended(1)
            output(1)

            transposes(2)
            pe.wait_ge(ld["l2"], 16)
            mm(bank[3][:, 0:B * K], mat("WksT"), ctxT[:, :], start=True, stop=True)
            mm(bank[3][:, B * K:2 * B * K], mat("WqsT"), ctxT[:, :], start=True, stop=True)
            mm(bank[6][:, 0:B * K], mat("WvsT"), ctxT[:, :], start=True, stop=True)

            def with_row(o, left, right, name):
                mm(o[0:K, 0:B * D].rearrange("k (b d) -> k b d", b=B), ones[0:1, 0:K],
                   row(name, 1).unsqueeze(1).broadcast_to([1, B, D]), start=True, stop=False)
                for b in range(B):
                    last = mm(o[0:K, b * D:(b + 1) * D], left[:, b * K:(b + 1) * K], right, start=False, stop=(b == B - 1))
                return last

            with_row(bank[2], ctxT, mat("WvsT"), "bv_s").then_inc(p2_pe, 1)
            transposes(3)
            pe.wait_ge(p2_act, 1)
            pe.wait_ge(p0_dve, 2)
            mm(bank[7][:, 0:B * K], mat("Wqc"), KsT[:, :], start=True, stop=True)
            mm(bank[7][:, B * K:2 * B * K], mat("Wkc"), QsT[:, :], start=True, stop=True)
            mm(bank[7][:, 384:512], mat("Wvc"), mat("Wg2T"), start=True, stop=True)
            mm(bank[3][0:K, 0:D], bvB[:, :], mat("Wg2T"), start=True, stop=True)
            mm(bank[3][0:1, D:D + B * K], col("bq_c"), KsT[:, :], start=True, stop=True)
            for b in range(B):
                mm(bank[3][0:K, 300 + b:301 + b], QsT[:, b * K:(b + 1) * K], col("bk_c"), start=True, stop=True)
            with_row(bank[6], VsT, mat("Wg1T"), "bg").then_inc(p2_pe, 1)

            pe.wait_ge(ld["l1"], 16)
            for b in range(B):
                pe.wait_ge(l1["x"], 2 * b + 1)
                mm(bank[4 * b + 1][:, :], mat("WkT"), W2_[b][:, :], start=True, stop=True).then_inc(l1["k"], 1)
                pe.wait_ge(l1["x"], 2 * b + 2)
                pe.wait_ge(p2_act, 2)
                for t in range(NT):
                    last = mm(tile(bank[4 * b + 2], t), tile(W4_[b], t), mat("WrT"), start=True, stop=True)
                last.then_inc(l1["r"], 1)
            for b in range(B):
                pe.wait_ge(l1["ka"], b + 1)
                for t in range(NT):
                    last = mm(tile(bank[4 * b + 3], t), tile(W3_[b], t), mat("WvT"), start=True, stop=True)
                last.then_inc(l1["v"], 1)
            pe.wait_ge(ld["l3"], 16)
            pe.wait_ge(ld["const"], 16)
            context(0)
            pe.wait_ge(l1["rt"], B)
            replicate(0, 0)

            for b in range(B):
                transposes(4 + b)
                pe.wait_ge(kv["reps"], 1)
                pe.wait_ge(hT_ready, 4 + b + 1)
                mm(bank[4 * b + 2][0:K, :], Mk[:, b * K:(b + 1) * K], hT[b], start=True, stop=True).then_inc(l2["s2"], 1)
                scores(b, Mq, qrow, l2["S"])
            for b in range(B):
                pe.wait_ge(l2["exp2"], b + 1)
                for t in range(NT):
                    last = nc.tensor.transpose(bank[4 * b][:, t * K:(t + 1) * K], W2_[b][0:K, t * P:(t + 1) * P],
                                               ident[0:K, 0:K])
                last.then_inc(l2["P2T"], 1)
            for b in range(B):
                pe.wait_ge(l2["P2Ts"], b + 1)
                for t in range(NT):
                    last = mm(bank[4 * b + 2][:, 0:K], h[b][:, t, :], W4_[b][:, t * K:(t + 1) * K],
                              start=(t == 0), stop=(t == NT - 1))
                last.then_inc(l2["ah"], 1)
                pe.wait_ge(l2["P"], b + 1)
                for t in range(NT):
                    last = nc.tensor.transpose(bank[4 * b + 3][0:K, t * P:(t + 1) * P], W1_[b][:, t * K:(t + 1) * K], ident)
                last.then_inc(l2["PT"], 1)
            for b in range(B):
                pe.wait_ge(l2["PTs"], b + 1)
                for t in range(NT):
                    last = mm(tile(bank[4 * b + 1], t), W3_[b][0:K, t * P:(t + 1) * P], Vs[:, b, :], start=True, stop=True)
                last.then_inc(l2["c2s"], 1)
                for t in range(NT):
                    mm(tile(bank[4 * b], t), W3_[b][0:K, t * P:(t + 1) * P], VsG[:, b, :], start=(t == 0), stop=False)
                pe.wait_ge(l2["ahs"], b + 1)
                mm(bank[4 * b + 2][0:K, 128:384], AhT[b][:, :], WvG[:, :, :], start=True, stop=True).then_inc(l2["s2c"], 1)
            for b in range(B):
                pe.wait_ge(l2["s2cs"], b + 1)
                for t in range(NT):
                    last = mm(tile(bank[4 * b + 3], t), interpT[:, t * P:(t + 1) * P], intV[b][:, 0, :], start=True, stop=True)
                last.then_inc(l2["s2ci"], 1)
                for t in range(NT):
                    last = mm(tile(bank[4 * b], t), interpT[:, t * P:(t + 1) * P], intV[b][:, 1, :], start=False, stop=(t == NT - 1))
                last.then_inc(l2["z"], 1)
            pe.wait_ge(l2["sc"], 1)
            replicate(0, 1)

            def router(n, b, k):
                pe.wait_ge(hT_ready, k + 1)
                for t in range(NT):
                    c0 = E * (NT * b + t)
                    last = mm(bank[BANKC[0]][:, c0:c0 + E], tile(hT[b], t), rwT[:, n * E:(n + 1) * E],
                              start=True, stop=True)
                if b == B - 1:
                    last.then_inc(m["lg"], 1)

            def weights_T(n, b):
                pe.wait_ge(m["c"], n + 1)
                for t in range(NT):
                    last = nc.tensor.transpose(bank[BANKC[b]][0:2 * E, t * P:(t + 1) * P],
                                               c2[:, NT * b + t, :].bitcast(F32), ident)
                last.then_inc(m["cT"], 1)

            def weights_row(i, j, groups, done):
                if isinstance(i, int) and groups * i + j < 0:
                    return
                p, b = j // B % 2, j % B
                mm(bank[BANKC[b]][:, :], sel[:, 2 * b + p, :], cflat[:, i + j // (2 * B), :],
                   start=True, stop=True).then_inc(done, 1)

            def down(i, n, last, chunks, groups, sems, lo, lo_count):
                j, c = n // chunks, n % chunks
                G, b = groups * i + j, j % B
                if c == 0 and b == 0:
                    pe.wait_ge(sems["dl"], 2 * i + j // B + 1)
                if c == 0:
                    wait_positive(pe, sems["ys"], G - 1)
                end = c == chunks - 1
                with_row = c == (0 if last and j == groups - 1 else chunks - 1)
                if with_row:
                    wait_positive(pe, sems["mult"], G - 2)
                    if i_is(i, 0) and j == 1:
                        pe.wait_ge(m["flat"], 16 * B * ((sems is r) + 1))
                        if sems is q:
                            pe.wait_ge(m["acc0"], B)
                pe.wait_ge(lo, lo_count)
                o = bank[4 * b][:, :]
                mm(o, wdh[j // B][:, c, :], rhi[n % 4][:, :], start=(c == 0), stop=False)
                if with_row:
                    weights_row(i, j - 1, groups, sems["row"])
                mm(o, wdh[j // B][:, c, :], rlo[n % 4][:, :], start=False, stop=False)
                mm(o, wdl[j // B][:, c, :], rhi[n % 4][:, :], start=False, stop=end).then_inc(sems["free"], 1)

            pe.wait_ge(kv["reps"], 2)
            pe.wait_ge(ld["moe1"], 80)
            pe.wait_ge(resid, 6)
            for b in range(B):
                transposes(6 + b)
                router(0, b, 6 + b)

            def hidden1(i, n):
                p, b, c = CH1[n]
                g = N1 * i + n
                if c == 0 and b == 0:
                    pe.wait_ge(q["ul"], 2 * i + p + 1)
                wait_positive(pe, q["gelu"], g - 3)
                w = slice(c * P, (c + 1) * P)
                mm3(bank[BANKS1[n % 4]][:, :], wuh[p][:, w], wul[p][:, w], hhi[b][:, :], hlo[b][:, :],
                    True, True).then_inc(q["h"], 1)

            def body1(i, last):
                for n in range(N1):
                    if n + LAG1 < N1:
                        hidden1(i, n + LAG1)
                    elif not last:
                        hidden1(i + 1, n + LAG1 - N1)
                    if i_is(i, 0) and n in (2, 3):
                        weights_T(0, n - 2)
                    if i_is(i, 0) and n == 5:
                        for b in range(B):
                            pe.wait_ge(m["cTs"], b + 1)
                            mm(bank[BANKC[b]][:, :], b2E[:, :], cT[:, b * S:(b + 1) * S].bitcast(F32),
                               start=True, stop=True).then_inc(m["b2"], 1)
                    if n in LO_POOL1:
                        down(i, n, last, C1, G1, q, q["loP"], len(LO_POOL1) * i + before(LO_POOL1, n + 1))
                    else:
                        down(i, n, last, C1, G1, q, q["loD"], len(LO_DVE1) * i + before(LO_DVE1, n + 1))

            def finish(n, sems, groups):
                pe.wait_ge(sems["mult"], PASSES * groups - 2)
                weights_row(PASSES - 1, groups - 1, groups, sems["row"])
                for b in range(B):
                    pe.wait_ge(m["sum"], B * n + b + 1)
                    for t in range(NT):
                        last = nc.tensor.transpose(tile(bank[1 + b], t), tile(acc[b], t), ident)
                    last.then_inc(m["outN"], 1)

            pe.wait_ge(m["split"], B)
            for n in range(LAG1):
                hidden1(0, n)
            body1(0, False)
            with pe.Fori(1, PASSES - 1) as i:
                body1(i, False)
            body1(PASSES - 1, True)
            pe.wait_ge(q["gelu"], N1 * PASSES)
            finish(0, q, G1)

            def attend(n):
                base = [8, 12][n]
                wq, wo = (("wq2", "wo2"), ("WqT3", "WoT3"))[n]
                pe.wait_ge(nb_ready, 1)

                def queries(b):
                    pe.wait_ge(hT_ready, base + b + 1)
                    mm(bank[4 * b][:, :], mat(wq), hT[b], start=True, stop=True).then_inc(at["q"], 1)


                def scores_of(u):
                    b, t = u // NT, u % NT
                    T = NT * B * n + u
                    pe.wait_ge(at["qlo"], 2 * n + b + 1)
                    for j, (h0, h1) in enumerate(HB):
                        if u >= 1:
                            pe.wait_ge(at["sub"], 3 * (T - 1) + j + 1)
                        o = bank[1 + j][:, 0:(h1 - h0) * K]
                        if n == 0:
                            mm(o, ident_b[:, :], nb[:, b, t, :].unsqueeze(1).broadcast_to([P, h1 - h0, K]),
                               start=True, stop=False)
                        mm3(o, tile(qh[b], t), tile(ql[b], t), kbh[b][:, h0:h1, :], kbl[b][:, h0:h1, :],
                            n == 1, True).then_inc(at["S"], 1)

                def transpose_of(u):
                    T = NT * B * n + u
                    pe.wait_ge(at["exp"], T + 1)
                    if T >= 1:
                        pe.wait_ge(at["PT"], 3 * T)
                    for c in range(CH):
                        last = nc.tensor.transpose(tile(bank[5 + c // 4], c % 4), tile(Sx[T % 2], c), ident)
                        if c % 4 == 3 or c == CH - 1:
                            last.then_inc(at["T"], 1)

                def values_of(u):
                    b = u // NT
                    T = NT * B * n + u
                    pe.wait_ge(at["PT"], 3 * (T + 1))
                    if u < B:
                        pe.wait_ge(at["qlo"], 2 * n + u + 1)
                    else:
                        pe.wait_ge(at["norm"], T - 1)
                    if u % NT == 0:
                        pe.wait_ge(kv["bd"], 2 * n + b + 1)
                    for c, h0 in enumerate(FIRST):
                        heads = HW if c > 0 else H
                        r0 = (CH - 1 - c) * HW * VW
                        last = mm(bank[4 * (u % 2)][:, h0 * VW:(h0 + heads) * VW], tile(PT[T % 2], c),
                                  vals[b][:, r0:r0 + heads * VW], start=(c == 0), stop=(c == CH - 1))
                    last.then_inc(at["O"], 1)

                def output_T(b):
                    pe.wait_ge(at["norm"], NT * (B * n + b + 1))
                    for t in range(NT):
                        last = nc.tensor.transpose(tile(bank[(1, 3)[b]], t), tile(W1_[b], t), ident)
                    last.then_inc(at["OT"], 1)

                def output_of(b):
                    pe.wait_ge(at["OTs"], 2 * n + b + 1)
                    for t in range(NT):
                        last = mm(tile(bank[(2, 1)[b]], t), tile(W2_[b], t), mat(wo), start=True, stop=True)
                    last.then_inc(at["out"], 1)

                transposes(base)
                queries(0)
                transposes(base + 1)
                pe.wait_ge(kv["pool"], 4 * (n + 1))
                scores_of(0)
                queries(1)
                for u in range(NT * B):
                    if u + 1 < NT * B:
                        scores_of(u + 1)
                    transpose_of(u)
                    if u >= 1:
                        values_of(u - 1)
                pe.wait_ge(at["sub"], 3 * NT * B * (n + 1))
                output_T(0)
                values_of(NT * B - 1)
                if n == 0:
                    context(1)
                output_of(0)
                output_T(1)
                output_of(1)

            attend(0)
            for b in range(B):
                replicate(1, b)
            for b in range(B):
                transposes(10 + b)
            pe.wait_ge(kv["reps"], 4)
            for b in range(B):
                router(1, b, 10 + b)

            def hidden2(i, n):
                p, b, c = CH2[n]
                g = N2 * i + n
                if c == 0 and b == 0:
                    pe.wait_ge(r["ul"], 2 * i + p + 1)
                wait_positive(pe, r["mul"], g - 1)
                for bk, off in ((BANKG[n % 2], 0), (BANKU[n % 2], F2)):
                    w = slice(off + c * P, off + (c + 1) * P)
                    last = mm3(bank[bk][:, :], wuh[p][:, w], wul[p][:, w], hhi[b][:, :], hlo[b][:, :], True, True)
                last.then_inc(r["g"], 1)

            def body2(i, last):
                for n in range(N2):
                    if n + LAG2 < N2:
                        hidden2(i, n + LAG2)
                    elif not last:
                        hidden2(i + 1, n + LAG2 - N2)
                    if i_is(i, 0) and n in (0, 1):
                        weights_T(1, n)
                    if n in LO_POOL2:
                        down(i, n, last, C2, G2, r, r["loP"], len(LO_POOL2) * i + before(LO_POOL2, n + 1))
                    else:
                        down(i, n, last, C2, G2, r, r["loD"], len(LO_DVE2) * i + before(LO_DVE2, n + 1))

            pe.wait_ge(resid, 10)
            pe.wait_ge(m["split"], 2 * B)
            for n in range(LAG2):
                hidden2(0, n)
            body2(0, False)
            with pe.Fori(1, PASSES - 1) as i:
                body2(i, False)
            body2(PASSES - 1, True)
            finish(1, r, G2)
            attend(1)

            for b in range(B):
                transposes(14 + b)
                pe.wait_ge(hT_ready, 14 + b + 1)
                mm(bank[4 * b + 3][:, :], mat("WinD"), hT[b], start=True, stop=True).then_inc(l3["s"], 1)
            pe.wait_ge(l3["wout"], 1)
            for b in range(B):
                o = bank[4 * b + 2]
                for j in range(NH - UA):
                    pe.wait_ge(l3["up"], (NH - UA) * b + j + 1)
                    for t in range(NT):
                        mm(tile(o, t), tile((W3_, W4_)[j][b], t), woutS[:, UA - UD + j, :],
                           start=(j == 0 and t == 0), stop=False)
                pe.wait_ge(l3["ut"], (UA - UD) * (b + 1))
                for t in range(NT):
                    mm(tile(o, t), tile(Sx[b], t), woutS[:, 0, :], start=False, stop=False)
                pe.wait_ge(l3["acc"], UD * (b + 1))
                for t in range(NT):
                    last = mm(tile(o, t), tile(W2_[b], t), mat("WoutD"), start=False, stop=(t == NT - 1))
                last.then_inc(l3["out"], 1)


def shape_constants():
    c = np.zeros((P, NK), np.float32)
    c[:, K_ID:K_ID + P] = np.eye(P)
    c[np.arange(D), K_HEAD + np.arange(D) // DH] = 1
    c[:, K_LT8:K_LT8 + 64] = np.tril(np.ones((8, 8)), -1).ravel()
    c[:, K_LT4:K_LT4 + 16] = np.tril(np.ones((4, 4)), -1).ravel()
    pairs = np.arange(SPAN)
    c[pairs % K, K_REP + pairs] = 1
    pair = np.zeros((P, CH, HW), np.float32)
    pair[pairs % P, CH - 1 - pairs // P, pairs // K - np.array(FIRST)[pairs // P]] = 1
    c[:, K_PAIR:K_PAIR + CH * HW] = pair.reshape(P, -1)
    pos = np.clip((np.arange(S, dtype=np.float32) + np.float32(0.5)) * np.float32(K / S) - np.float32(0.5), 0, K - 1)
    lo = np.floor(pos).astype(np.int64)
    hi = np.minimum(lo + 1, K - 1)
    w = (pos - lo).astype(np.float32)
    for i in range(S):
        c[lo[i], K_INT + i] += 1 - w[i]
        c[hi[i], K_INT + i] += w[i]
    c[np.arange(8), K_SEL + np.arange(8) // 2] = 1
    return c


def kernel(**inputs):
    import concourse.bacc as bacc
    from concourse.bass_utils import run_bass_kernel_spmd

    z = {k: np.asarray(v) for k, v in inputs.items()}
    T = np.transpose
    qv = z["L0_xattn_W_qv"].reshape(4, D, D)
    wg = z["L1_xattn_Wg"]
    kv3 = z["L3_xattn_Wkv"]
    by_name = {
        "Wqv1": qv[0], "Wqv2": qv[1], "Wqv3": qv[2], "Wqv4": qv[3],
        "WrT": T(z["L0_ffn_W_r"]), "WkT": T(z["L0_ffn_W_k"]), "WvT": T(z["L0_ffn_W_v"]),
        "WksT": T(z["L1_xattn_Wk_s"]), "WqsT": T(z["L1_xattn_Wq_s"]), "WvsT": T(z["L1_xattn_Wv_s"]),
        "WvcT": T(z["L1_xattn_Wv_c"]), "Wvc": z["L1_xattn_Wv_c"], "Wqc": z["L1_xattn_Wq_c"], "Wkc": z["L1_xattn_Wk_c"],
        "Wg1T": T(wg[:, :D]), "Wg2T": T(wg[:, D:]),
        "wq2": z["L2_xattn_w_q"], "wk2": z["L2_xattn_w_k"], "wv2": z["L2_xattn_w_v"], "wo2": z["L2_xattn_w_o"],
        "WqT3": T(z["L3_xattn_Wq"]), "WkT3": T(kv3[:D]), "WvT3": T(kv3[D:]), "WoT3": T(z["L3_xattn_Wo"]),
        "WinD": np.concatenate([z["L3_ffn_Win"]] * 2, 1), "WoutD": np.concatenate([z["L3_ffn_Wout"]] * 2, 0),
    }
    ws = z["L0_xattn_w_sim"]

    def doubled(w):
        return np.concatenate([w[:, :NH], w[:, NH:]], 0)

    bin_ = z["L3_ffn_bin_"]
    vecs = [ws[:D], ws[D:2 * D], ws[2 * D:], z["L0_ffn_mu_r"], z["L0_ffn_mu_k"], z["L1_xattn_bk_s"],
            z["L1_xattn_bq_s"], z["L1_xattn_bq_c"], z["L1_xattn_bk_c"], z["L1_xattn_bv_s"], z["L1_xattn_bv_c"],
            z["L3_xattn_bq"],
            np.concatenate([bin_, bin_])]
    cols = np.concatenate([np.stack(vecs, 1), doubled(z["L3_ffn_W1"]), doubled(z["L3_ffn_b1"]),
                           doubled(z["L3_ffn_W2"])], 1)
    rows = np.concatenate([z["L0_xattn_b_qv"], z["L3_xattn_bo"], z["L3_ffn_bout"], z["L1_xattn_bv_s"],
                           z["L1_xattn_bv_c"], z["L1_xattn_bg"], z["g_xattn"], z["g_ffn"], z["L0_xattn_b_sim"]])
    const = shape_constants()
    arrays = {
        "x": z["x"], "ctx": z["ctx_1024"], "ctxT": T(z["ctx_1024"], (2, 0, 1)).reshape(D, B * K),
        "mask": z["mask_Bx1xSxS2_ik1"].reshape(B, S, K), "rows": rows, "cols": cols,
        "mats": np.stack([by_name[n] for n in MATS], 1), "const": const,
        "b2m": z["L3_ffn_b2"].reshape(M_IN, 1),
        "rwT": np.concatenate([T(z["L1_ffn_router_w"]), T(z["L2_ffn_gate_w"])], 1),
        "b2": z["L1_ffn_b2"],
        "w1": np.concatenate([T(z["L1_ffn_w1"], (2, 0, 1)), T(z["L1_ffn_b1"].reshape(E, C1, P), (2, 0, 1))], 2),
        "w2": T(z["L1_ffn_w2"].reshape(E, D, C1, P), (3, 0, 2, 1)),
        "v13": T(z["L2_ffn_w13_weight"], (2, 0, 1)),
        "v2": T(z["L2_ffn_w2_weight"].reshape(E, D, C2, P), (3, 0, 2, 1)),
    }
    arrays = {f"in_{k}": np.ascontiguousarray(v) for k, v in arrays.items()}
    nc = bacc.Bacc("TRN2", target_bir_lowering=False, num_devices=1)
    aps = {k[3:]: nc.dram_tensor(k, v.shape, mybir.dt.from_np(v.dtype), kind="ExternalInput").ap()
           for k, v in arrays.items()}
    out = nc.dram_tensor("out", (B, S, D), F32, kind="ExternalOutput").ap()
    flamingo_program(nc, aps, out)
    res = run_bass_kernel_spmd(nc, [arrays], core_ids=[0])
    return res.results[0]["out"]
```
